# Optimizing a Trainium2 kernel written in Bass

```python
import numpy as np
import jax
import jax.numpy as jnp

def _softmax(x, axis=-1):
    return jax.nn.softmax(x, axis=axis)

def _gelu(x):
    return jax.nn.gelu(x, approximate=True)

def _silu(x):
    return jax.nn.silu(x)

def _sigmoid(x):
    return jax.nn.sigmoid(x)

def _layernorm(x, axis=-1, eps=1e-05):
    m = jnp.mean(x, axis=axis, keepdims=True)
    v = jnp.var(x, axis=axis, keepdims=True)
    return (x - m) / jnp.sqrt(v + eps)

def _scatter_add(tgt, idx, src, axis=0):
    return tgt.at[idx].add(src)

def _segment_sum(src, seg, n):
    return jax.ops.segment_sum(src, seg, n)
kernel_name = 'mk_adaln_d1_jaxref_r8_badde6'

def setup_inputs(seed: int=0):
    np.random.seed(seed)
    _w = jnp.asarray

    def _L0_attn_setup():
        import math
        import jax, jax.numpy as jnp
        import numpy as np
        B, S, H = (1, 256, 256)
        NH = 16
        DN = 128
        DR = 64
        DV = 128
        QL = 192
        KL = 64
        EPS = 1e-06
        ROPE_BASE = 10000.0

        def _rmsnorm(x, gamma, eps=EPS):
            return x * gamma * jax.lax.rsqrt(jnp.mean(x * x, axis=-1, keepdims=True) + eps)

        def _rope_tables(seq_len, dim, dtype):
            inv_freq = 1.0 / ROPE_BASE ** (jnp.arange(0, dim, 2, dtype=jnp.float32) / dim)
            ang = jnp.arange(seq_len, dtype=jnp.float32)[:, None] * inv_freq
            cos = jnp.concatenate([jnp.cos(ang)] * 2, axis=-1).astype(dtype)
            sin = jnp.concatenate([jnp.sin(ang)] * 2, axis=-1).astype(dtype)
            return (cos[None, :, None, :], sin[None, :, None, :])

        def _rotate_half(x):
            h = x.shape[-1] // 2
            return jnp.concatenate([-x[..., h:], x[..., :h]], axis=-1)
        key = jax.random.key(seed)
        ks = jax.random.split(key, 6)
        w = 0.02
        return {'hidden': jax.random.normal(ks[0], (B, S, H), jnp.float32), 'w_kv_a': jax.random.normal(ks[1], (H, QL + KL + DR), jnp.float32) * w, 'q_a_gamma': jnp.ones((QL,), jnp.float32), 'w_qb': jax.random.normal(ks[2], (QL, NH * (DN + DR)), jnp.float32) * w, 'kv_a_gamma': jnp.ones((KL,), jnp.float32), 'w_kvb': jax.random.normal(ks[3], (KL, NH * (DN + DV)), jnp.float32) * w, 'w_o': jax.random.normal(ks[4], (NH * DV, H), jnp.float32) * w}
    _L0_attn_in = _L0_attn_setup()

    def _L0_ffn_setup():
        import jax, jax.numpy as jnp
        import numpy as np
        B, S, H = (1, 256, 256)
        E, K, I = (16, 4, 176)
        IS = 352
        CAP = 128
        key = jax.random.key(seed)
        ks = jax.random.split(key, 8)
        sc = 0.02
        return {'hidden_states': jax.random.normal(ks[0], (B, S, H), jnp.float32), 'gate_w': jax.random.normal(ks[1], (E, H), jnp.float32) * sc, 'w_gate': jax.random.normal(ks[2], (E, H, I), jnp.float32) * sc, 'w_up': jax.random.normal(ks[3], (E, H, I), jnp.float32) * sc, 'w_down': jax.random.normal(ks[4], (E, I, H), jnp.float32) * sc, 'sw_gate': jax.random.normal(ks[5], (H, IS), jnp.float32) * sc, 'sw_up': jax.random.normal(ks[6], (H, IS), jnp.float32) * sc, 'sw_down': jax.random.normal(ks[7], (IS, H), jnp.float32) * sc}
    _L0_ffn_in = _L0_ffn_setup()
    _L0_c = _w((lambda *s: np.random.randn(*s).astype(np.float32) * 0.05)(8, 256))
    _L0_wmod = _w((lambda *s: np.random.randn(*s).astype(np.float32) * 0.05)(256, 6 * 256) * 256 ** (-0.5))
    _d = {'L0_attn_hidden': _L0_attn_in['hidden'], 'L0_attn_w_kv_a': _L0_attn_in['w_kv_a'], 'L0_attn_q_a_gamma': _L0_attn_in['q_a_gamma'], 'L0_attn_w_qb': _L0_attn_in['w_qb'], 'L0_attn_kv_a_gamma': _L0_attn_in['kv_a_gamma'], 'L0_attn_w_kvb': _L0_attn_in['w_kvb'], 'L0_attn_w_o': _L0_attn_in['w_o'], 'L0_ffn_gate_w': _L0_ffn_in['gate_w'], 'L0_ffn_w_gate': _L0_ffn_in['w_gate'], 'L0_ffn_w_up': _L0_ffn_in['w_up'], 'L0_ffn_w_down': _L0_ffn_in['w_down'], 'L0_ffn_sw_gate': _L0_ffn_in['sw_gate'], 'L0_ffn_sw_up': _L0_ffn_in['sw_up'], 'L0_ffn_sw_down': _L0_ffn_in['sw_down'], 'L0_c': _L0_c, 'L0_wmod': _L0_wmod}
    _x0 = _d['L0_attn_hidden']
    _d['L0_attn_hidden'] = jax.random.normal(jax.random.fold_in(jax.random.key(seed), 1), (8, 512, 256), dtype=_x0.dtype)
    del _x0
    return _d

def reference(L0_attn_hidden, L0_attn_w_kv_a, L0_attn_q_a_gamma, L0_attn_w_qb, L0_attn_kv_a_gamma, L0_attn_w_kvb, L0_attn_w_o, L0_ffn_gate_w, L0_ffn_w_gate, L0_ffn_w_up, L0_ffn_w_down, L0_ffn_sw_gate, L0_ffn_sw_up, L0_ffn_sw_down, L0_c, L0_wmod):

    def _L0_attn_ref(hidden, w_kv_a, q_a_gamma, w_qb, kv_a_gamma, w_kvb, w_o):
        import math
        import jax, jax.numpy as jnp
        import numpy as np
        B, S, H = (1, 256, 256)
        NH = 16
        DN = 128
        DR = 64
        DV = 128
        QL = 192
        KL = 64
        EPS = 1e-06
        ROPE_BASE = 10000.0

        def _rmsnorm(x, gamma, eps=EPS):
            return x * gamma * jax.lax.rsqrt(jnp.mean(x * x, axis=-1, keepdims=True) + eps)

        def _rope_tables(seq_len, dim, dtype):
            inv_freq = 1.0 / ROPE_BASE ** (jnp.arange(0, dim, 2, dtype=jnp.float32) / dim)
            ang = jnp.arange(seq_len, dtype=jnp.float32)[:, None] * inv_freq
            cos = jnp.concatenate([jnp.cos(ang)] * 2, axis=-1).astype(dtype)
            sin = jnp.concatenate([jnp.sin(ang)] * 2, axis=-1).astype(dtype)
            return (cos[None, :, None, :], sin[None, :, None, :])

        def _rotate_half(x):
            h = x.shape[-1] // 2
            return jnp.concatenate([-x[..., h:], x[..., :h]], axis=-1)
        b, s, _ = hidden.shape
        fused = hidden @ w_kv_a
        q_c = fused[..., :QL]
        kv_c = fused[..., QL:QL + KL]
        k_pe = fused[..., QL + KL:]
        q = _rmsnorm(q_c, q_a_gamma) @ w_qb
        q = q.reshape(b, s, NH, DN + DR)
        q_nope, q_pe = (q[..., :DN], q[..., DN:])
        kv = _rmsnorm(kv_c, kv_a_gamma) @ w_kvb
        kv = kv.reshape(b, s, NH, DN + DV)
        k_nope, v = (kv[..., :DN], kv[..., DN:])
        cos, sin = _rope_tables(s, DR, hidden.dtype)
        q_pe = q_pe * cos + _rotate_half(q_pe) * sin
        k_pe = k_pe[:, :, None, :]
        k_pe = k_pe * cos + _rotate_half(k_pe) * sin
        q_full = jnp.concatenate([q_nope, q_pe], axis=-1)
        k_full = jnp.concatenate([k_nope, jnp.broadcast_to(k_pe, (b, s, NH, DR))], axis=-1)
        scale = 1.0 / math.sqrt(DN + DR)
        scores = jnp.einsum('bqhd,bkhd->bhqk', q_full, k_full) * scale
        pos = jnp.arange(s)
        causal = pos[:, None] >= pos[None, :]
        scores = jnp.where(causal[None, None], scores, jnp.asarray(-1e+30, scores.dtype))
        probs = jax.nn.softmax(scores, axis=-1)
        attn = jnp.einsum('bhqk,bkhd->bqhd', probs, v)
        return attn.reshape(b, s, NH * DV) @ w_o

    def _L0_ffn_ref(hidden_states, gate_w, w_gate, w_up, w_down, sw_gate, sw_up, sw_down):
        import jax, jax.numpy as jnp
        import numpy as np
        B, S, H = (1, 256, 256)
        E, K, I = (16, 4, 176)
        IS = 352
        CAP = 128
        b, s, h = hidden_states.shape
        x = hidden_states.reshape(-1, h)
        T = x.shape[0]
        scores = jax.nn.softmax(x @ gate_w.T, axis=-1)
        topk_w, topk_i = jax.lax.top_k(scores, K)
        topk_w = topk_w / (topk_w.sum(-1, keepdims=True) + 1e-20)
        flat_i = topk_i.reshape(-1)
        flat_w = topk_w.reshape(-1)
        order = jnp.argsort(flat_i)
        se = flat_i[order]
        counts = jax.ops.segment_sum(jnp.ones_like(flat_i), flat_i, num_segments=E)
        starts = jnp.cumsum(counts) - counts
        rank = jnp.arange(T * K) - starts[se]
        tok = order // K
        slot = jnp.where(rank < CAP, rank, CAP)
        buf = jnp.full((E, CAP + 1), T, dtype=jnp.int32).at[se, slot].set(tok)[:, :CAP]
        wbuf = jnp.zeros((E, CAP + 1), x.dtype).at[se, slot].set(flat_w[order])[:, :CAP]
        xpad = jnp.concatenate([x, jnp.zeros((1, h), x.dtype)], axis=0)
        xg = xpad[buf]
        gact = jax.nn.silu(jnp.einsum('ech,ehi->eci', xg, w_gate))
        mid = gact * jnp.einsum('ech,ehi->eci', xg, w_up)
        eout = jnp.einsum('eci,eih->ech', mid, w_down) * wbuf[..., None]
        y = jnp.zeros((T + 1, h), x.dtype).at[buf.reshape(-1)].add(eout.reshape(-1, h))[:T]
        shared = jax.nn.silu(x @ sw_gate) * (x @ sw_up) @ sw_down
        return (y + shared).reshape(b, s, h)
    x = L0_attn_hidden
    mod = (_silu(L0_c) @ L0_wmod).reshape(L0_c.shape[0], 6, 1, -1)
    sa, ca, ga, sb, cb, gb = (mod[:, 0], mod[:, 1], mod[:, 2], mod[:, 3], mod[:, 4], mod[:, 5])
    ga = (2 * (ga >= 0) - 1) * jnp.maximum(jnp.abs(ga), 0.25)
    gb = (2 * (gb >= 0) - 1) * jnp.maximum(jnp.abs(gb), 0.25)
    h = _layernorm(x, axis=-1) * (1 + ca) + sa
    x = x + ga * _L0_attn_ref(h, L0_attn_w_kv_a, L0_attn_q_a_gamma, L0_attn_w_qb, L0_attn_kv_a_gamma, L0_attn_w_kvb, L0_attn_w_o)
    h = _layernorm(x, axis=-1) * (1 + cb) + sb
    x = x + gb * _L0_ffn_ref(h, L0_ffn_gate_w, L0_ffn_w_gate, L0_ffn_w_up, L0_ffn_w_down, L0_ffn_sw_gate, L0_ffn_sw_up, L0_ffn_sw_down)
    return x

_drawn_inputs = setup_inputs


def setup_inputs(seed=0):
    import zlib

    import numpy as np

    out = dict(_drawn_inputs(seed))
    spreads = {'L0_attn_q_a_gamma': (1.0, 0.6), 'L0_attn_kv_a_gamma': (1.0, 0.6)}
    factors = {'L0_attn_w_kv_a': 8.0,
     'L0_attn_w_qb': 8.0,
     'L0_attn_w_kvb': 8.0,
     'L0_attn_w_o': 8.0,
     'L0_ffn_gate_w': 8.0,
     'L0_ffn_w_gate': 8.0,
     'L0_ffn_w_up': 8.0,
     'L0_ffn_w_down': 8.0,
     'L0_ffn_sw_gate': 8.0,
     'L0_ffn_sw_up': 8.0,
     'L0_ffn_sw_down': 8.0,
     'L0_c': 8.0,
     'L0_wmod': 8.0}
    for name, (base, spread) in spreads.items():
        noise = np.random.default_rng([zlib.crc32(name.encode()), seed]).standard_normal(out[name].shape)
        drawn = base * np.exp(spread * noise) if base else spread * noise
        out[name] = jnp.asarray(drawn.astype(out[name].dtype))
    for name, factor in factors.items():
        out[name] = (out[name] * factor).astype(out[name].dtype)
    return out
```

```python
from contextlib import ExitStack

import numpy as np

import concourse.bass as bass
from concourse import mybir

F32 = mybir.dt.float32
BF16 = mybir.dt.bfloat16
I32 = mybir.dt.int32
U32 = mybir.dt.uint32
ALU = mybir.AluOpType
ACT = mybir.ActivationFunctionType
AX = mybir.AxisListType

P = 128
B, S, H = 8, 512, 256
T = B * S
NT = S // P
LAST = B - 1
NH, DN, DR, DV = 16, 128, 64, 128
QL, KL = 192, 64
QR = QL - P
FW = QL + KL + DR
NPAIR = NH // 2
NE, TOPK, IM, IS, CAP = 16, 4, 176, 352, 128
IR = IM - P
MT = [(0, 128), (128, 128), (256, 96)]
LN_EPS, RMS_EPS = 1e-5, 1e-6
SCALE = 1.0 / float(np.sqrt(DN + DR))
NEG = -1e30
FAR = 1e5
UNITS = [(h, i) for h in range(2) for i in (3, 2, 1, 0)]
NU = len(UNITS)
SBANKS, TBANKS, OBANK, QBANKS = [0, 1, 2], [3, 4], 5, [6, 7]
SA, CA, GA, SB, CB, GB = range(6)

CHAIN_PROLOGUE, CHAIN_PAIR, CHAIN_BATCH = 39, 11, 153


class Chain:

    def __init__(self, eng, sem):
        self.eng, self.sem, self.base, self.n = eng, sem, 0, 0

    def link(self, ins):
        self.n += 1
        ins.then_inc(self.sem, 1)

    def wait(self):
        self.eng.wait_ge(self.sem, self.base + self.n)

    def step(self, ins):
        self.link(ins)
        self.wait()


def adaln_block(nc, x, wkva, wqnT, wqpe, wkT, wvT, wo, qgam, kgam, sgate, sup, sdown,
                egate, eup, edown, cT, wmod, cos, sin, out):
    xr = x.rearrange("b s h -> (b s) h")
    outr = out.rearrange("b s h -> (b s) h")
    mod_dram = nc.dram_tensor("mod_dram", (B, 6 * H), F32, kind="Internal").ap()
    gb_dram = nc.dram_tensor("gb_dram", (B, H), F32, kind="Internal").ap()
    h2_dram = nc.dram_tensor("h2_dram", (T + P, H), F32, kind="Internal").ap()
    acc_dram = nc.dram_tensor("acc_dram", (T + P, H), F32, kind="Internal").ap()
    tab_dram = nc.dram_tensor("tab_dram", (NE * CAP, 2), F32, kind="Internal").ap()

    def wait_alone(eng, semaphore, value):
        if not isinstance(value, int):
            value = eng.snap(eng.to_reg(value))
            eng.wait_ge(const_ready, 3)
        eng.wait_ge(semaphore, value)

    def rows(ap, b):
        return ap[bass.ts(b, S), :].rearrange("(t p) h -> p t h", p=P)

    with ExitStack() as ctx:
        def sb(name, shape, dt=F32):
            return ctx.enter_context(nc.sbuf_tensor(name, shape, dt))

        def sem(name):
            return ctx.enter_context(nc.semaphore(name))

        wq0 = sb("wq0", [P, NH * P])
        wq1 = sb("wq1", [QR, NH * P])
        wvo = sb("wvo", [P, NPAIR, H])
        wkva_sb = sb("wkva_sb", [P, 2, FW])
        sg_sb = sb("sg_sb", [P, 2, IS + NE])
        su_sb = sb("su_sb", [P, 2, IS])
        sd_sb = sb("sd_sb", [P, 3, H])
        cos_sb = sb("cos_sb", [P, NT, DR])
        sin_sb = sb("sin_sb", [P, NT, DR])
        qg_sb = sb("qg_sb", [P, 2])
        kg_sb = sb("kg_sb", [P, KL])
        ident = sb("ident", [P, P])
        identb = sb("identb", [P, P], BF16)
        caus = sb("caus", [P, P])
        causb = sb("causb", [P, P], BF16)
        tri = sb("tri", [P, P])
        trib = sb("trib", [P, P], BF16)
        onesb = sb("onesb", [P, P], BF16)
        iota_i = sb("iota_i", [P, 3, NE], I32)
        eid = sb("eid", [P, NE])
        ebase = sb("ebase", [P, NE])
        tid = sb("tid", [P, NT])
        tab_init = sb("tab_init", [P, NE, 2])
        zrow = sb("zrow", [P, H])
        mhalf = sb("mhalf", [P, 2 * NT])

        x_in = sb("x_in", [P, NT, H])
        x_res = sb("x_res", [P, NT, H])
        x1 = sb("x1", [P, NT, H])
        h1 = sb("h1", [P, NT, H])
        h2 = sb("h2", [P, NT, H])
        tmp = sb("tmp", [P, NT, H])
        hT = sb("hT", [P, 2, S])
        h2T = sb("h2T", [P, 2, S])
        moda = sb("moda", [P, 2, H])
        modb = sb("modb", [P, 4, H])
        st = sb("st", [P, NT, 6])
        mv = sb("mv", [P, NT, 2])
        rstd = sb("rstd", [P, NT])
        st2 = sb("st2", [P, NT, 6])
        mv2 = sb("mv2", [P, NT, 2])
        rstd2 = sb("rstd2", [P, NT])
        sq = sb("sq", [P, QL])
        ssq = sb("ssq", [P, 2, NT])
        qn = sb("qn", [P, NT, QL])
        kmat = sb("kmat", [P, NT, KL + DR])
        kr1 = sb("kr1", [P, NT, DR])
        kr2 = sb("kr2", [P, NT, DR])
        kT = sb("kT", [P, S])
        ql0 = sb("ql0", [P, S])
        ql1 = sb("ql1", [QR, S])
        base = sb("base", [P, NT, H])

        qtok = sb("qtok", [P, 2 * NT, P])
        qr1 = sb("qr1", [P, 2 * NT, DR])
        qr2 = sb("qr2", [P, 2 * NT, DR])
        qT = sb("qT", [P, 2, S])
        probs = sb("probs", [P, NU, S])
        pT = sb("pT", [P, 2, NT, S])
        nmax = sb("nmax", [P, NU])
        psums = sb("psums", [P, NU])
        prec = sb("prec", [P, NU])
        oT = sb("oT", [P, NPAIR, S])

        th = sb("th", [P, S])
        mid = sb("mid", [P, S])
        midT = sb("midT", [P, 3, S])
        lgT = sb("lgT", [NE, S])
        lmax = sb("lmax", [P, NT])
        ls = sb("ls", [P, NT, NE])
        ex = sb("ex", [P, NT, NE])
        esum = sb("esum", [P, NT])
        score = sb("score", [P, NT, NE])
        top = sb("top", [P, NT, 8])
        topi = sb("topi", [P, NT, 8], U32)
        topf = sb("topf", [P, NT, TOPK])
        tsum = sb("tsum", [P, NT])
        oh = sb("oh", [P, NT, TOPK, NE])
        ohs = sb("ohs", [P, NT, TOPK, NE])
        mask = sb("mask", [P, NT, NE])
        maskb = sb("maskb", [P, NT, NE], BF16)
        before = sb("before", [P, NT + 1, NE])
        beforeb = sb("beforeb", [P, NT, NE], BF16)
        slot_e = sb("slot_e", [P, NT, NE])
        over = sb("over", [P, NT, NE])
        slotf = sb("slotf", [P, NT * TOPK])
        slot = sb("slot", [P, NT * TOPK], U32)
        entry = sb("entry", [P, NT * TOPK, 2])

        RE = 4
        ewts = sb("ewts", [P, RE, 2 * 2 * IM + 2 * H])
        tab = sb("tab", [P, NE, 2])
        toku = sb("toku", [P, NE], U32)
        bidf = sb("bidf", [P, NE])
        bidi = sb("bidi", [P, NE], I32)
        bid = sb("bid", [P, NE], I32)
        xg = sb("xg", [P, 2, H])
        gbg = sb("gbg", [P, 2, H])
        xgT = sb("xgT", [P, 2, 2, P])
        eth = sb("eth", [P, IM])
        emid = sb("emid", [P, 2, IM])
        emT = sb("emT", [P, 2, 2, P])
        ey = sb("ey", [P, 2, H])

        cT_sb = sb("cT_sb", [P, 2, B])
        cth = sb("cth", [P, 2, B])
        csl = sb("csl", [P, 2, B])
        mod_sb = midT[0:B].rearrange("b a s -> b (a s)").rearrange("b (a h) -> b a h", h=H)
        sgn = mid[0:B].rearrange("b (a h) -> b a h", h=H)
        wo_st = pT[:].rearrange("p a b s -> p (a b s)").rearrange("p (h n) -> p h n", h=NH)
        wqn_st = oT[:].rearrange("p a s -> p (a s)")[:, 0:NH * QL].rearrange("p (h n) -> p h n", h=NH)
        wk_st = oT[:].rearrange("p a s -> p (a s)")[:, NH * QL:NH * (QL + KL)].rearrange("p (h n) -> p h n", h=NH)
        wv_st = probs[:].rearrange("p a s -> p (a s)")[:, 0:NH * KL].rearrange("p (h n) -> p h n", h=NH)
        wm_st = ewts[:].rearrange("p a s -> p (a s)")[:, 0:2 * 6 * H].rearrange("p (c n) -> p c n", c=2)
        pe0_st = probs[:].rearrange("p a s -> p (a s)")[:, 1024:2048].rearrange("p (h n) -> p h n", h=NH)
        pe1_st = probs[:].rearrange("p a s -> p (a s)")[0:QR, 2048:3072].rearrange("p (h n) -> p h n", h=NH)

        PS = ctx.enter_context(nc.psum_tensor("PS", [P, 8, 512], F32))
        qps = PS[:, 6:8, :].rearrange("p a (c d) -> p (a c) d", d=P)

        w_in = sem("w_in")
        mod_in = sem("mod_in")
        const_ready = sem("const_ready")
        c_tanh = sem("c_tanh")
        c_ready = sem("c_ready")
        mod_ps = sem("mod_ps")
        mod_ready = sem("mod_ready")
        mod_out = sem("mod_out")
        init_out = sem("init_out")
        wabs_ps = sem("wabs_ps")
        wabs_ready = sem("wabs_ready")
        x_landed = sem("x_landed")
        moda_landed = sem("moda_landed")
        modb_landed = sem("modb_landed")
        res_ready = sem("res_ready")
        h1_ready = sem("h1_ready")
        hT_ps = sem("hT_ps")
        hT_ready = sem("hT_ready")
        kv_ps = sem("kv_ps")
        ssq_ready = sem("ssq_ready")
        qn_ready = sem("qn_ready")
        k_ready = sem("k_ready")
        kq_ps = sem("kq_ps")
        kq_ready = sem("kq_ready")
        q_ps = sem("q_ps")
        nope_ready = sem("nope_ready")
        rope_ready = sem("rope_ready")
        qT_ps = sem("qT_ps")
        qT_ready = sem("qT_ready")
        s_ps = sem("s_ps")
        max_ready = sem("max_ready")
        exp_ready = sem("exp_ready")
        p_ready = sem("p_ready")
        pT_ps = sem("pT_ps")
        pT_act = sem("pT_act")
        pT_dve = sem("pT_dve")
        o_ps = sem("o_ps")
        oT_ready = sem("oT_ready")
        attn_ps = sem("attn_ps")
        x1_ready = sem("x1_ready")
        h2_ready = sem("h2_ready")
        h2_out = sem("h2_out")
        h2T_ps = sem("h2T_ps")
        h2T_ready = sem("h2T_ready")
        gu_ps = sem("gu_ps")
        th_ready = sem("th_ready")
        mid_ready = sem("mid_ready")
        lg_ready = sem("lg_ready")
        lgT_ps = sem("lgT_ps")
        ls_ready = sem("ls_ready")
        ex_ready = sem("ex_ready")
        mask_ready = sem("mask_ready")
        rank_ps = sem("rank_ps")
        slot_ready = sem("slot_ready")
        scattered = sem("scattered")
        entries_free = sem("entries_free")
        down_ps = sem("down_ps")
        base_ready = sem("base_ready")
        base_out = sem("base_out")
        dve_chain = sem("dve_chain")
        pool_chain = sem("pool_chain")
        var1_ready = sem("var1_ready")
        rs1_ready = sem("rs1_ready")
        var2_ready = sem("var2_ready")
        rs2_ready = sem("rs2_ready")
        rsq_ready = sem("rsq_ready")
        eps1 = sem("eps1")
        eps2 = sem("eps2")
        eps3 = sem("eps3")
        tab_landed = sem("tab_landed")
        tok_ready = sem("tok_ready")
        ew_landed = [sem(f"ew_landed{i}") for i in range(RE)]
        xg_landed = [sem(f"xg_landed{i}") for i in range(2)]
        xgT_ps = sem("xgT_ps")
        xgT_ready = sem("xgT_ready")
        egu_ps = sem("egu_ps")
        eth_ready = sem("eth_ready")
        emid_ready = sem("emid_ready")
        emT_ps = sem("emT_ps")
        emT_ready = sem("emT_ready")
        ey_ps = sem("ey_ps")
        ey_ready = sem("ey_ready")
        added = sem("added")
        done = sem("done")

        block = ctx.enter_context(nc.Block())

        W_LOADS = 13
        ew_g = lambda r, k: ewts[:, r, k * 2 * IM:(k + 1) * 2 * IM]
        ew_d = lambda r, k, n: ewts[0:n, r, 4 * IM + k * H:4 * IM + (k + 1) * H]

        @block.sync
        def _(sp):
            sp.dma_start(cT_sb[:], cT.rearrange("(c p) b -> p c b", p=P)).then_inc(mod_in, 16)
            sp.dma_start(wm_st, wmod.rearrange("(c p) n -> p c n", p=P)).then_inc(mod_in, 16)
            sp.dma_start(x_in[:], rows(xr, 0)).then_inc(x_landed, 16)
            sp.dma_start(wkva_sb[:], wkva.rearrange("(c p) n -> p c n", p=P)).then_inc(w_in, 16)
            sp.dma_start(wqn_st, wqnT.rearrange("h p n -> p h n")).then_inc(w_in, 16)
            sp.dma_start(wk_st, wkT).then_inc(w_in, 16)
            sp.dma_start(pe0_st, wqpe[0:P]).then_inc(w_in, 16)
            sp.dma_start(pe1_st, wqpe[P:QL]).then_inc(w_in, 16)
            sp.dma_start(qg_sb[:, 0:1], qgam[0:P].rearrange("(p a) -> p a", a=1)).then_inc(w_in, 16)
            sp.dma_start(qg_sb[0:QR, 1:2], qgam[P:QL].rearrange("(p a) -> p a", a=1)).then_inc(w_in, 16)
            sp.dma_start(kg_sb[:], kgam.partition_broadcast(P)).then_inc(w_in, 16)
            sp.dma_start(cos_sb[:], cos.rearrange("(t p) d -> p t d", p=P)).then_inc(w_in, 16)
            sp.dma_start(sin_sb[:], sin.rearrange("(t p) d -> p t d", p=P)).then_inc(w_in, 16)
            sp.dma_start(wv_st, wvT).then_inc(w_in, 16)
            sp.dma_start(wo_st, wo.rearrange("(h p) n -> p h n", p=P)).then_inc(w_in, 16)
            sp.dma_start(sg_sb[:], sgate.rearrange("(c p) n -> p c n", p=P)).then_inc(w_in, 16)
            sp.dma_start(su_sb[:], sup.rearrange("(c p) n -> p c n", p=P)).then_inc(init_out, 16)
            sp.dma_start(sd_sb[:, 0:2, :], sdown[0:2 * P].rearrange("(c p) n -> p c n", p=P)).then_inc(init_out, 16)
            sp.dma_start(sd_sb[0:MT[2][1], 2, :], sdown[2 * P:IS]).then_inc(init_out, 16)
            sp.wait_ge(mod_ready, 1)
            sp.dma_start(mod_dram, midT[0:B].rearrange("b a s -> b (a s)")).then_inc(mod_out, 16)
            sp.dma_start(gb_dram, mod_sb[:, GB, :]).then_inc(mod_out, 16)
            sp.wait_ge(const_ready, 3)
            sp.dma_start(h2_dram[T:T + P, :], zrow[:]).then_inc(init_out, 16)
            sp.dma_start(acc_dram[T:T + P, :], zrow[:]).then_inc(init_out, 16)
            sp.dma_start(tab_dram.rearrange("(e p) c -> p e c", p=P), tab_init[:]).then_inc(init_out, 16)
            sp.wait_ge(mod_out, 32)

            def load_moda(n):
                sp.dma_start(moda[:].rearrange("p a h -> p (a h)"),
                             mod_dram[bass.ds(n, 1), 0:2 * H].rearrange("a n -> (a n)").partition_broadcast(P)
                             ).then_inc(moda_landed, 16)

            def load_modb(b):
                sp.dma_start(modb[:].rearrange("p a h -> p (a h)"),
                             mod_dram[bass.ds(b, 1), 2 * H:6 * H].rearrange("a n -> (a n)").partition_broadcast(P)
                             ).then_inc(modb_landed, 16)

            def store_batch(b):
                sp.wait_ge(h2_ready, b + 1)
                sp.dma_start(rows(h2_dram, b), h2[:]).then_inc(h2_out, 16)
                sp.wait_ge(base_ready, b + 1)
                sp.dma_start(rows(acc_dram, b), base[:]).then_inc(base_out, 16)

            load_moda(0)
            load_modb(0)
            with sp.Fori(0, B - 1) as b:
                n = b + 1
                sp.wait_ge(h1_ready, n)
                sp.wait_ge(res_ready, n)
                sp.dma_start(x_in[:], rows(xr, n)).then_inc(x_landed, 16)
                load_moda(n)
                store_batch(b)
                load_modb(n)
            store_batch(B - 1)
            sp.wait_ge(scattered, B * NT * TOPK * 16)
            sp.dma_start(tab[:], tab_dram.rearrange("(e p) c -> p e c", p=P)).then_inc(tab_landed, 16)
            sp.wait_ge(added, NE * 16)
            sp.wait_ge(base_out, B * 16 + 16)
            for q in range(4):
                sp.dma_start(outr[q * T // 4:(q + 1) * T // 4, :],
                             acc_dram[q * T // 4:(q + 1) * T // 4, :]).then_inc(done, 16)
            sp.wait_ge(done, 4 * 16)
            sp.wait_ge(h2_out, B * 16 + 16)
            sp.wait_ge(init_out, 6 * 16)

        @block.gpsimd
        def _(pool):
            ch = Chain(pool, pool_chain)
            ch.link(pool.memset(ident[:], 0.0))
            ch.link(pool.memset(caus[:], 0.0))
            ch.link(pool.memset(tri[:], 0.0))
            ch.link(pool.memset(zrow[:], 0.0))
            ch.link(pool.memset(mhalf[:], -0.5))
            ch.link(pool.memset(tab_init[:], 0.0))
            ch.wait()
            ch.link(pool.affine_select(out=ident[:], in_=ident[:], compare_op=ALU.not_equal, fill=1.0, base=0,
                                       pattern=[[-1, P]], channel_multiplier=1))
            ch.link(pool.affine_select(out=caus[:], in_=caus[:], compare_op=ALU.is_ge, fill=NEG, base=0,
                                       pattern=[[-1, P]], channel_multiplier=1))
            ch.link(pool.affine_select(out=tri[:], in_=tri[:], compare_op=ALU.is_ge, fill=1.0, base=0,
                                       pattern=[[-1, P]], channel_multiplier=1))
            ch.link(pool.iota(iota_i[:, 0, :], pattern=[[1, NE]], base=0, channel_multiplier=0))
            ch.link(pool.iota(iota_i[:, 1, :], pattern=[[0, NE]], base=T, channel_multiplier=1))
            ch.link(pool.iota(iota_i[:, 2, 0:NT], pattern=[[P, NT]], base=0, channel_multiplier=1))
            ch.wait()
            ch.link(pool.tensor_copy(identb[:], ident[:]))
            ch.link(pool.tensor_copy(causb[:], caus[:]))
            ch.link(pool.tensor_copy(trib[:], tri[:]))
            ch.link(pool.memset(onesb[:], 1.0))
            ch.link(pool.tensor_copy(eid[:], iota_i[:, 0, :]))
            ch.link(pool.tensor_copy(tid[:], iota_i[:, 2, 0:NT]))
            ch.link(pool.tensor_copy(tab_init[:, :, 0], iota_i[:, 1, :]))
            ch.link(pool.memset(before[:, 0, :], 0.0))
            ch.wait()
            pool.tensor_scalar(ebase[:], eid[:], float(CAP), None, ALU.mult).then_inc(const_ready, 3)

            def inverse_roots(b, n, post, pre):
                def root(dst, src, eps, added_eps, ready, k):
                    pool.tensor_scalar(dst, src, eps, None, ALU.add).then_inc(added_eps, 1)
                    pool.wait_ge(added_eps, k + 1)
                    pool.tensor_tensor(dst, dst, mhalf[:, 0:dst.shape[1]], ALU.pow).then_inc(ready, 1)

                if pre:
                    wait_alone(pool, var1_ready, NT * (n + 1))
                    root(rstd[:], mv[:, :, 1], LN_EPS, eps1, rs1_ready, n)
                if post:
                    wait_alone(pool, var2_ready, NT * (b + 1))
                    root(rstd2[:], mv2[:, :, 1], LN_EPS, eps2, rs2_ready, b)
                if pre:
                    wait_alone(pool, ssq_ready, 8 * (n + 1))
                    ssqf = ssq[:].rearrange("p a t -> p (a t)")
                    root(ssqf, ssqf, RMS_EPS, eps3, rsq_ready, n)

            inverse_roots(0, 0, False, True)
            pool.wait_ge(x_landed, 16)
            pool.tensor_copy(x_res[:], x_in[:]).then_inc(res_ready, 1)
            pool.wait_ge(init_out, 6 * 16)

            def scatter(b):
                wait_alone(pool, slot_ready, b + 1)
                for j in range(NT * TOPK):
                    pool.indirect_dma_start(
                        tab_dram[:, :], bass.IndirectOffsetOnAxis(ap=slot[:, j:j + 1], axis=0),
                        entry[:, j, :], None, bounds_check=NE * CAP - 1, oob_is_err=False,
                    ).then_inc(scattered, 16)
                pool.wait_ge(scattered, (b + 1) * NT * TOPK * 16)
                pool.sem_inc(entries_free, 1)

            with pool.Fori(0, B - 1) as b:
                inverse_roots(b, b + 1, True, True)
                wait_alone(pool, x1_ready, b + 1)
                wait_alone(pool, x_landed, (b + 2) * 16)
                pool.tensor_copy(x_res[:], x_in[:]).then_inc(res_ready, 1)
                scatter(b)
            inverse_roots(LAST, None, True, False)
            scatter(LAST)

            pool.wait_ge(tok_ready, 1)
            pool.wait_ge(h2_out, B * 16 + 16)
            pool.wait_ge(base_out, B * 16 + 16)

            def gather(e):
                if e >= 2:
                    pool.wait_ge(xgT_ps, e - 1)
                    pool.wait_ge(ey_ready, e - 1)
                pool.indirect_dma_start(xg[:, e % 2, :], None, h2_dram[:, :],
                                        bass.IndirectOffsetOnAxis(ap=toku[:, e:e + 1], axis=0),
                                        bounds_check=T + P - 1).then_inc(xg_landed[e % 2], 16)
                pool.indirect_dma_start(gbg[:, e % 2, :], None, gb_dram[:, :],
                                        bass.IndirectOffsetOnAxis(ap=bid[:, e:e + 1].bitcast(U32), axis=0),
                                        bounds_check=B - 1).then_inc(xg_landed[e % 2], 16)

            gather(0)
            gather(1)
            for e in range(NE):
                pool.wait_ge(ey_ready, e + 1)
                if e:
                    pool.wait_ge(added, 16 * e)
                pool.indirect_dma_start(acc_dram[:, :], bass.IndirectOffsetOnAxis(ap=toku[:, e:e + 1], axis=0),
                                        ey[:, e % 2, :], None, bounds_check=T + P - 1,
                                        compute_op=ALU.add).then_inc(added, 16)
                if e + 2 < NE:
                    gather(e + 2)

        @block.tensor
        def _(pe):
            pe.wait_ge(mod_in, 32)
            pe.wait_ge(c_ready, 1)
            for n in range(3):
                for c in range(2):
                    mm = pe.matmul(PS[0:B, n, :], csl[:, c, :], wm_st[:, c, bass.ts(n, 512)],
                                   start=c == 0, stop=c == 1)
            mm.then_inc(mod_ps, 1)
            pe.wait_ge(w_in, W_LOADS * 16)
            pe.wait_ge(const_ready, 3)
            for h in range(NH):
                bank, col = 3 + h // 8, (h % 8) * KL
                pe.matmul(PS[:, bank, col:col + KL], wqn_st[:, h, 0:P], wk_st[:, h, :], start=True, stop=True)
                mm = pe.matmul(PS[0:QR, 2 + bank, col:col + KL], wqn_st[:, h, P:QL], wk_st[:, h, :],
                               start=True, stop=True)
            mm.then_inc(wabs_ps, 1)
            pe.wait_ge(mod_ready, 1)
            pe.wait_ge(wabs_ready, 1)
            for h in range(NH):
                p, half = h // 2, (h % 2) * KL
                mm = pe.matmul(PS[half:half + KL, p // 2, (p % 2) * H:(p % 2 + 1) * H], wv_st[:, h, :],
                               wo_st[:, h, :], start=True, stop=True)
            mm.then_inc(wabs_ps, 1)
            pe.wait_ge(wabs_ready, 2)

            def q_project(p, g):
                cols = bass.ts(p, 2 * P)
                for t in range(NT):
                    dst = PS[:, QBANKS[t // 2], (t % 2) * 2 * P:(t % 2 + 1) * 2 * P]
                    pe.matmul(dst, ql0[:, bass.ts(t, P)], wq0[:, cols], start=True, stop=False)
                    mm = pe.matmul(dst, ql1[:, bass.ts(t, P)], wq1[:, cols], start=False, stop=True)
                mm.then_inc(q_ps, 1)

            def q_turn(g):
                pe.wait_ge(nope_ready, g + 1)
                pe.wait_ge(rope_ready, g + 1)
                for h in range(2):
                    for t in range(NT):
                        mm = pe.transpose(PS[:, QBANKS[h], bass.ts(t, P)], qtok[:, 2 * t + h, :], ident[:])
                mm.then_inc(qT_ps, 1)

            def pair(p, g, more):
                pe.wait_ge(qT_ready, g + 1)
                for u, (h, i) in enumerate(UNITS):
                    bank = SBANKS[u % 3]
                    if u >= 3:
                        pe.wait_ge(exp_ready, g * NU + u - 2)
                    n = (i + 1) * P
                    pe.matmul(PS[:, bank, 0:n], qT[:, h, bass.ts(i, P)], kT[:, 0:n], start=True, stop=False)
                    pe.matmul(PS[:, bank, i * P:n], identb[:], causb[:], start=False, stop=True).then_inc(s_ps, 1)
                if more:
                    q_project(p + 1, g + 1)
                for u, (h, i) in enumerate(UNITS):
                    pe.wait_ge(p_ready, g * NU + u + 1)
                    if u >= 2:
                        pe.wait_ge(pT_dve if u % 2 else pT_act, g * (NU // 2) + u // 2)
                    for j in range(i + 1):
                        mm = pe.transpose(PS[:, TBANKS[u % 2], bass.ts(j, P)], probs[:, u, bass.ts(j, P)], ident[:])
                    mm.then_inc(pT_ps, 1)
                if more:
                    q_turn(g + 1)
                pe.wait_ge(pT_act, (g + 1) * (NU // 2))
                pe.wait_ge(pT_dve, (g + 1) * (NU // 2))
                pe.wait_ge(oT_ready, g + 1)
                for j in range(NT):
                    for h in range(2):
                        mm = pe.matmul(PS[h * KL:(h + 1) * KL, OBANK, j * P:S], kmat[:, j, 0:KL],
                                       pT[:, h, j, j * P:S], start=j == 0, stop=j == NT - 1)
                mm.then_inc(o_ps, 1)

            def turn8(sem_ps, src):
                for c in range(2):
                    for t in range(NT):
                        mm = pe.transpose(PS[:, c, bass.ts(t, P)], src[:, t, bass.ts(c, P)], ident[:])
                    mm.then_inc(sem_ps, 1)

            def ffn(b, m, banks, first):
                off, w = MT[m]
                wide = w + (NE if m == 2 else 0)
                for c in range(2):
                    pe.matmul(PS[0:wide, banks[0], :], sg_sb[:, c, off:off + wide], h2T[:, c, :],
                              start=c == 0, stop=c == 1)
                for c in range(2):
                    mm = pe.matmul(PS[0:w, banks[1], :], su_sb[:, c, off:off + w], h2T[:, c, :],
                                   start=c == 0, stop=c == 1)
                mm.then_inc(gu_ps, 1)

            def middle(b, n, post, pre):
                if post:
                    pe.wait_ge(oT_ready, (b + 1) * NPAIR + 1)
                    for t in range(NT):
                        for p in range(NPAIR):
                            mm = pe.matmul(PS[:, QBANKS[t // 2], (t % 2) * H:(t % 2 + 1) * H],
                                           oT[:, p, bass.ts(t, P)], wvo[:, p, :], start=p == 0, stop=p == NPAIR - 1)
                        if t % 2:
                            mm.then_inc(attn_ps, 1)
                if pre:
                    pe.wait_ge(h1_ready, n + 1)
                    turn8(hT_ps, h1)
                    pe.wait_ge(hT_ready, 2 * (n + 1))
                    for t in range(NT):
                        for c in range(2):
                            mm = pe.matmul(PS[:, 2 + t, 0:FW], hT[:, c, bass.ts(t, P)], wkva_sb[:, c, :],
                                           start=c == 0, stop=c == 1)
                        mm.then_inc(kv_ps, 1)
                if post:
                    pe.wait_ge(h2_ready, b + 1)
                    turn8(h2T_ps, h2)
                if pre:
                    pe.wait_ge(qn_ready, n + 1)
                    pe.wait_ge(k_ready, n + 1)
                    for t in range(NT):
                        mm = pe.transpose(PS[:, 6, bass.ts(t, P)], kmat[:, t, :], ident[:])
                    mm.then_inc(kq_ps, 1)
                    for t in range(NT):
                        mm = pe.transpose(PS[:, 7, bass.ts(t, P)], qn[:, t, 0:P], ident[:])
                    mm.then_inc(kq_ps, 1)
                    for t in range(NT):
                        mm = pe.transpose(PS[0:QR, 2, bass.ts(t, P)], qn[:, t, P:QL], ident[:])
                    mm.then_inc(kq_ps, 1)
                if post:
                    pe.wait_ge(h2T_ready, 2 * (b + 1))
                    ffn(b, 2, (3, 4), True)
                    ffn(b, 0, (0, 1), True)
                if pre:
                    pe.wait_ge(kq_ready, 3 * (n + 1))
                    q_project(0, n * NPAIR)
                if post:
                    wait_alone(pe, lg_ready, b + 1)
                    for t in range(NT):
                        mm = pe.transpose(PS[:, 5, bass.ts(t, NE)], lgT[:, bass.ts(t, P)], ident[0:NE, 0:NE])
                    mm.then_inc(lgT_ps, 1)
                    pe.wait_ge(mid_ready, 3 * b + 1)
                    ffn(b, 1, (3, 4), False)
                if pre:
                    q_turn(n * NPAIR)
                if post:
                    pe.wait_ge(mid_ready, 3 * b + 3)
                    for t in range(NT):
                        for k, (off, w) in enumerate(MT):
                            mm = pe.matmul(PS[:, t // 2, (t % 2) * H:(t % 2 + 1) * H],
                                           midT[0:w, k, bass.ts(t, P)], sd_sb[0:w, k, :], start=k == 0, stop=k == 2)
                        if t % 2:
                            mm.then_inc(down_ps, 1)
                    pe.wait_ge(mask_ready, b + 1)
                    pe.matmul(PS[:, 5, 64:64 + NT * NE], trib[:], maskb[:].rearrange("p t e -> p (t e)"),
                              start=True, stop=False)
                    pe.matmul(PS[:, 5, 64:64 + NT * NE], onesb[:], beforeb[:].rearrange("p t e -> p (t e)"),
                              start=False, stop=True).then_inc(rank_ps, 1)
                    pe.wait_ge(base_ready, b + 1)
                    pe.wait_ge(slot_ready, b + 1)

            middle(0, 0, False, True)
            with pe.Fori(0, B - 1) as b:
                with pe.Fori(0, NPAIR - 1) as p:
                    pair(p, b * NPAIR + p, True)
                pair(NPAIR - 1, b * NPAIR + NPAIR - 1, False)
                middle(b, b + 1, True, True)
            with pe.Fori(0, NPAIR - 1) as p:
                pair(p, LAST * NPAIR + p, True)
            pair(NPAIR - 1, LAST * NPAIR + NPAIR - 1, False)
            middle(LAST, None, True, False)

            for e in range(NE):
                r, q = e % RE, e % 2
                pe.wait_ge(xg_landed[q], 32 * (e // 2 + 1))
                for c in range(2):
                    mm = pe.transpose(PS[:, q, bass.ts(c, P)], xg[:, q, bass.ts(c, P)], ident[:])
                mm.then_inc(xgT_ps, 1)
                pe.wait_ge(xgT_ready, e + 1)
                pe.wait_ge(ew_landed[r], 64 * (e // RE + 1))
                for c in range(2):
                    mm = pe.matmul(PS[:, 2 + q, 0:2 * IM], xgT[:, q, c, :], ew_g(r, c), start=c == 0, stop=c == 1)
                mm.then_inc(egu_ps, 1)
                pe.wait_ge(emid_ready, e + 1)
                pe.transpose(PS[:, 4 + q, 0:P], emid[:, q, 0:P], ident[:])
                pe.transpose(PS[0:IR, 4 + q, P:2 * P], emid[:, q, P:IM], ident[:]).then_inc(emT_ps, 1)
                pe.wait_ge(emT_ready, e + 1)
                pe.matmul(PS[:, 6 + q, 0:H], emT[:, q, 0, :], ew_d(r, 0, P), start=True, stop=False)
                pe.matmul(PS[:, 6 + q, 0:H], emT[0:IR, q, 1, :], ew_d(r, 1, IR), start=False,
                          stop=True).then_inc(ey_ps, 1)

        @block.scalar
        def _(act):
            act.sem_inc(oT_ready, 1)
            act.sem_inc(h2_out, 16)
            act.sem_inc(base_out, 16)
            act.sem_inc(entries_free, 1)
            act.wait_ge(mod_in, 32)
            act.activation(cth[:], cT_sb[:], ACT.Tanh, scale=0.5).then_inc(c_tanh, 1)

            def nope_copy(g):
                act.wait_ge(q_ps, g + 1)
                act.activation(qtok[:, :, 0:KL], qps[:, :, 0:KL], ACT.Copy).then_inc(nope_ready, 1)

            def q_out(g):
                act.wait_ge(qT_ps, g + 1)
                act.activation(qT[:], PS[:, 6:8, :], ACT.Copy).then_inc(qT_ready, 1)

            def pair(p, g, more):
                for u, (h, i) in enumerate(UNITS):
                    n = (i + 1) * P
                    act.wait_ge(max_ready, g * NU + u + 1)
                    act.activation(probs[:, u, 0:n], PS[:, SBANKS[u % 3], 0:n], ACT.Exp, bias=nmax[:, u:u + 1],
                                   accum_out=psums[:, u:u + 1]).then_inc(exp_ready, 1)
                if more:
                    nope_copy(g + 1)
                for u in range(0, NU, 2):
                    h, i = UNITS[u]
                    act.wait_ge(pT_ps, g * NU + u + 1)
                    act.activation(pT[:, h, 0:i + 1, bass.ts(i, P)],
                                   PS[:, TBANKS[0], 0:(i + 1) * P].rearrange("p (j q) -> p j q", q=P),
                                   ACT.Copy).then_inc(pT_act, 1)
                if more:
                    q_out(g + 1)
                act.wait_ge(o_ps, g + 1)
                act.activation(oT[:, p, :], PS[:, OBANK, :], ACT.Copy).then_inc(oT_ready, 1)

            def tanh_gate(b, k, m, bank):
                w = MT[m][1]
                act.wait_ge(gu_ps, 3 * b + k + 1)
                if k:
                    act.wait_ge(mid_ready, 3 * b + k)
                act.activation(th[0:w, :], PS[0:w, bank, :], ACT.Tanh, scale=0.5).then_inc(th_ready, 1)

            def turned(sem_ps, sem_ready, dst, b):
                for c in range(2):
                    act.wait_ge(sem_ps, 2 * b + c + 1)
                    act.activation(dst[:, c, :], PS[:, c, :], ACT.Copy).then_inc(sem_ready, 1)

            def middle(b, n, post, pre):
                if pre:
                    turned(hT_ps, hT_ready, hT, n)
                    for t in range(NT):
                        act.wait_ge(kv_ps, NT * n + t + 1)
                        act.activation(sq[:], PS[:, 2 + t, 0:QL], ACT.Square, scale=QL ** -0.5,
                                       accum_out=ssq[:, 0, t:t + 1]).then_inc(ssq_ready, 1)
                        act.wait_ge(ssq_ready, 2 * (NT * n + t) + 1)
                        act.activation(sq[:, 0:KL], PS[:, 2 + t, QL:QL + KL], ACT.Square, scale=KL ** -0.5,
                                       accum_out=ssq[:, 1, t:t + 1]).then_inc(ssq_ready, 1)
                        act.wait_ge(ssq_ready, 2 * (NT * n + t) + 2)
                if post:
                    turned(h2T_ps, h2T_ready, h2T, b)
                if pre:
                    for k, (dst, w, bank) in enumerate([(kT, P, 6), (ql0, P, 7), (ql1, QR, 2)]):
                        act.wait_ge(kq_ps, 3 * n + k + 1)
                        act.activation(dst[0:w, :], PS[0:w, bank, :], ACT.Copy).then_inc(kq_ready, 1)
                if post:
                    tanh_gate(b, 0, 2, 3)
                    w = MT[2][1]
                    act.activation(lgT[:], PS[w:w + NE, 3, :], ACT.Copy).then_inc(lg_ready, 1)
                    tanh_gate(b, 1, 0, 0)
                if pre:
                    nope_copy(n * NPAIR)
                if post:
                    tanh_gate(b, 2, 1, 3)
                    act.wait_ge(ls_ready, b + 1)
                    act.activation(ex[:], ls[:], ACT.Exp).then_inc(ex_ready, 1)
                if pre:
                    q_out(n * NPAIR)

            middle(0, 0, False, True)
            with act.Fori(0, B - 1) as b:
                with act.Fori(0, NPAIR - 1) as p:
                    pair(p, b * NPAIR + p, True)
                pair(NPAIR - 1, b * NPAIR + NPAIR - 1, False)
                middle(b, b + 1, True, True)
            with act.Fori(0, NPAIR - 1) as p:
                pair(p, LAST * NPAIR + p, True)
            pair(NPAIR - 1, LAST * NPAIR + NPAIR - 1, False)
            middle(LAST, None, True, False)

            def load(e):
                r = e % RE
                if e >= RE:
                    act.wait_ge(ey_ps, e - RE + 1)
                act.dma_start(ewts[:, r, 0:4 * IM].rearrange("p (c n) -> p c n", c=2)[:, :, 0:IM],
                              egate[e].rearrange("(c p) n -> p c n", p=P)).then_inc(ew_landed[r], 16)
                act.dma_start(ewts[:, r, 0:4 * IM].rearrange("p (c n) -> p c n", c=2)[:, :, IM:2 * IM],
                              eup[e].rearrange("(c p) n -> p c n", p=P)).then_inc(ew_landed[r], 16)
                act.dma_start(ew_d(r, 0, P), edown[e, 0:P, :]).then_inc(ew_landed[r], 16)
                act.dma_start(ew_d(r, 1, IR), edown[e, P:IM, :]).then_inc(ew_landed[r], 16)

            for e in range(RE):
                load(e)
            for e in range(NE):
                q = e % 2
                act.wait_ge(xgT_ps, e + 1)
                act.activation(xgT[:, q, :, :].rearrange("p c s -> p (c s)"), PS[:, q, 0:2 * P],
                               ACT.Copy).then_inc(xgT_ready, 1)
                act.wait_ge(egu_ps, e + 1)
                if e:
                    act.wait_ge(emid_ready, e)
                act.activation(eth[:], PS[:, 2 + q, 0:IM], ACT.Tanh, scale=0.5).then_inc(eth_ready, 1)
                act.wait_ge(emT_ps, e + 1)
                act.activation(emT[:, q, 0, :], PS[:, 4 + q, 0:P], ACT.Copy)
                act.activation(emT[0:IR, q, 1, :], PS[0:IR, 4 + q, P:2 * P], ACT.Copy).then_inc(emT_ready, 1)
                if e + RE < NE:
                    load(e + RE)

        @block.vector
        def _(dve):
            ch = Chain(dve, dve_chain)
            dve.wait_ge(c_tanh, 1)
            ch.step(dve.tensor_scalar(cth[:], cth[:], 1.0, 0.5, ALU.add, ALU.mult))
            dve.tensor_tensor(csl[:], cth[:], cT_sb[:], ALU.mult).then_inc(c_ready, 1)
            dve.wait_ge(mod_ps, 1)
            ch.step(dve.tensor_copy(midT[0:B].rearrange("b a s -> b (a s)"),
                                    PS[0:B, 0:3, :].rearrange("b a n -> b (a n)")))
            for k, i in enumerate((GA, GB)):
                ch.step(dve.tensor_scalar(sgn[:, 0, :], mod_sb[:, i, :], 0.0, 2.0, ALU.is_ge, ALU.mult))
                ch.step(dve.tensor_scalar(sgn[:, 0, :], sgn[:, 0, :], -1.0, 0.5 if i == GB else 1.0, ALU.add, ALU.mult))
                ch.step(dve.scalar_tensor_tensor(out=sgn[:, 1, :], in0=mod_sb[:, i, :], scalar=-1.0,
                                                 in1=mod_sb[:, i, :], op0=ALU.mult, op1=ALU.max))
                ch.step(dve.scalar_tensor_tensor(out=mod_sb[:, i, :], in0=sgn[:, 1, :], scalar=0.25,
                                                 in1=sgn[:, 0, :], op0=ALU.max, op1=ALU.mult))
            ch.step(dve.tensor_scalar(mod_sb[:, CA, :], mod_sb[:, CA, :], 1.0, None, ALU.add))
            dve.tensor_scalar(mod_sb[:, CB, :], mod_sb[:, CB, :], 1.0, None, ALU.add).then_inc(mod_ready, 1)
            dve.wait_ge(w_in, W_LOADS * 16)
            ch.step(dve.tensor_scalar(qg_sb[:, 0:1], qg_sb[:, 0:1], SCALE, None, ALU.mult))
            ch.step(dve.tensor_scalar(qg_sb[0:QR, 1:2], qg_sb[0:QR, 1:2], SCALE, None, ALU.mult))
            dve.wait_ge(wabs_ps, 1)
            for k, (w, n, pe_st) in enumerate([(wq0, P, pe0_st), (wq1, QR, pe1_st)]):
                wv = w[0:n, :].rearrange("p (h c) -> p h c", c=P)
                ch.link(dve.tensor_scalar(wv[:, :, 0:KL],
                                          PS[0:n, 3 + 2 * k:5 + 2 * k, :].rearrange("p a (c d) -> p (a c) d", d=KL),
                                          qg_sb[0:n, k:k + 1], None, ALU.mult))
                ch.link(dve.tensor_scalar(wv[:, :, KL:P], pe_st, qg_sb[0:n, k:k + 1], None, ALU.mult))
            ch.wait()
            dve.memset(xg[:], 0.0).then_inc(wabs_ready, 1)
            dve.wait_ge(wabs_ps, 2)
            dve.tensor_copy(wvo[:].rearrange("p a n -> p (a n)"),
                            PS[:, 0:4, :].rearrange("p a n -> p (a n)")).then_inc(wabs_ready, 1)

            def norm(src, dst, stats, mean_var, rs, scale, shift, ready, var_ready, rs_ready, n):
                for t in range(NT):
                    ch.link(dve.bn_stats(stats[:, t, :], src[:, t, :]))
                wait_alone(dve, ch.sem, ch.base + ch.n)
                for t in range(NT):
                    dve.bn_aggr(mean_var[:, t, :], stats[:, t, :]).then_inc(var_ready, 1)
                dve.wait_ge(var_ready, NT * (n + 1))
                dve.wait_ge(rs_ready, n + 1)
                for t in range(NT):
                    ch.link(dve.tensor_scalar(dst[:, t, :], src[:, t, :], mean_var[:, t, 0:1], rs[:, t:t + 1],
                                              ALU.subtract, ALU.mult))
                ch.wait()
                ch.step(dve.tensor_tensor(dst[:], dst[:], scale.unsqueeze(1).to_broadcast([P, NT, H]), ALU.mult))
                dve.tensor_tensor(dst[:], dst[:], shift.unsqueeze(1).to_broadcast([P, NT, H]),
                                  ALU.add).then_inc(ready, 1)

            HALF = DR // 2

            def rope_parts(raw, t1, t2, heads):
                def tab(a, lo, hi):
                    return a[:, :, lo:hi].unsqueeze(2).to_broadcast([P, NT, heads, hi - lo])

                def v(a, lo, hi):
                    return a[:, :, lo:hi].rearrange("p (t h) d -> p t h d", h=heads)
                return [lambda: dve.tensor_tensor(v(t1, 0, DR), v(raw, 0, DR), tab(cos_sb, 0, DR), ALU.mult),
                        lambda: dve.tensor_tensor(v(t2, 0, HALF), v(raw, HALF, DR), tab(sin_sb, 0, HALF), ALU.mult),
                        lambda: dve.tensor_tensor(v(t2, HALF, DR), v(raw, 0, HALF), tab(sin_sb, HALF, DR), ALU.mult)]

            def q_rope(g):
                parts = rope_parts(qps[:, :, KL:P], qr1, qr2, 2)

                def first():
                    dve.wait_ge(nope_ready, g + 1)
                    ch.link(parts[0]())

                def last():
                    ch.wait()
                    dve.tensor_tensor(qtok[:, :, KL:P], qr1[:], qr2[:], ALU.add).then_inc(rope_ready, 1)
                return [first, lambda: ch.link(parts[1]()), lambda: ch.link(parts[2]()), last]

            def pair(g, more):
                def top_of(u):
                    i = UNITS[u][1]
                    dve.wait_ge(s_ps, g * NU + u + 1)
                    dve.tensor_reduce(nmax[:, u:u + 1], PS[:, SBANKS[u % 3], 0:(i + 1) * P], AX.X, ALU.max,
                                      negate=True).then_inc(max_ready, 1)

                def scale_of(u):
                    n = (UNITS[u][1] + 1) * P
                    dve.wait_ge(exp_ready, g * NU + u + 1)
                    ch.step(dve.reciprocal(prec[:, u:u + 1], psums[:, u:u + 1]))
                    dve.tensor_scalar(probs[:, u, 0:n], probs[:, u, 0:n], prec[:, u:u + 1], None,
                                      ALU.mult).then_inc(p_ready, 1)

                for u in range(NU):
                    top_of(u)
                    if u >= 2:
                        scale_of(u - 2)
                scale_of(NU - 2)
                scale_of(NU - 1)
                rope = q_rope(g + 1) if more else [lambda: None] * 4
                for k, u in enumerate(range(1, NU, 2)):
                    rope[k]()
                    h, i = UNITS[u]
                    dve.wait_ge(pT_ps, g * NU + u + 1)
                    dve.tensor_copy(pT[:, h, 0:i + 1, bass.ts(i, P)],
                                    PS[:, TBANKS[1], 0:(i + 1) * P].rearrange("p (j q) -> p j q", q=P)
                                    ).then_inc(pT_dve, 1)

            def silu_mid(b, k, m, banks):
                w = MT[m][1]
                dve.wait_ge(th_ready, 3 * b + k + 1)
                ch.step(dve.scalar_tensor_tensor(out=mid[0:w, :], in0=th[0:w, :], scalar=1.0,
                                                 in1=PS[0:w, banks[0], :], op0=ALU.add, op1=ALU.mult))
                dve.tensor_tensor(midT[0:w, m, :], mid[0:w, :], PS[0:w, banks[1], :], ALU.mult).then_inc(mid_ready, 1)

            def over_e(a):
                return a.unsqueeze(2).to_broadcast([P, NT, NE])

            def route(b):
                dve.wait_ge(lgT_ps, b + 1)
                lg = PS[:, 5, 0:NT * NE].rearrange("p (t e) -> p t e", e=NE)
                ch.step(dve.tensor_reduce(lmax[:], lg, AX.X, ALU.max))
                dve.tensor_tensor(ls[:], lg, over_e(lmax[:]), ALU.subtract).then_inc(ls_ready, 1)
                dve.wait_ge(ex_ready, b + 1)
                ch.step(dve.tensor_reduce(esum[:], ex[:], AX.X, ALU.add))
                ch.step(dve.reciprocal(esum[:], esum[:]))
                ch.link(dve.tensor_tensor(score[:], ex[:], over_e(esum[:]), ALU.mult))
                wait_alone(dve, ch.sem, ch.base + ch.n)
                for t in range(NT):
                    ch.link(dve.max(top[:, t, :], score[:, t, :]))
                wait_alone(dve, ch.sem, ch.base + ch.n)
                for t in range(NT):
                    ch.link(dve.max_index(topi[:, t, :], top[:, t, :], score[:, t, :]))
                ch.step(dve.tensor_reduce(tsum[:], top[:, :, 0:TOPK], AX.X, ALU.add))
                ch.step(dve.tensor_scalar(tsum[:], tsum[:], 1e-20, None, ALU.add))
                ch.step(dve.reciprocal(tsum[:], tsum[:]))
                ch.step(dve.tensor_copy(topf[:], topi[:, :, 0:TOPK]))
                ent = entry[:].rearrange("p (t k) c -> p t k c", k=TOPK)

                def over_k(a):
                    return a.unsqueeze(2).to_broadcast([P, NT, TOPK])
                dve.wait_ge(entries_free, b + 1)
                ch.link(dve.tensor_tensor(ent[:, :, :, 1], top[:, :, 0:TOPK], over_k(tsum[:]), ALU.mult))
                ch.link(dve.tensor_copy(ent[:, :, :, 0], over_k(tid[:])))
                ch.step(dve.tensor_tensor(oh[:].rearrange("p t k e -> p (t k) e"),
                                          eid[:].unsqueeze(1).to_broadcast([P, NT * TOPK, NE]),
                                          topf[:].rearrange("p t k -> p (t k)").unsqueeze(2).to_broadcast(
                                              [P, NT * TOPK, NE]), ALU.is_equal))
                ch.step(dve.tensor_scalar(tid[:], tid[:], float(S), None, ALU.add))
                ch.step(dve.tensor_reduce(mask[:], oh[:].rearrange("p t k e -> p t e k"), AX.X, ALU.add))
                ch.link(dve.tensor_copy(maskb[:], mask[:]))
                for t in range(NT):
                    ch.step(dve.tensor_tensor(before[:, t + 1, :], before[:, t, :], mask[:, t, :], ALU.add))
                ch.step(dve.tensor_copy(beforeb[:], before[:, 0:NT, :]))
                dve.tensor_copy(before[:, 0, :], before[:, NT, :]).then_inc(mask_ready, 1)

            def slots(b):
                dve.wait_ge(rank_ps, b + 1)
                rank = PS[:, 5, 64:64 + NT * NE].rearrange("p (t e) -> p t e", e=NE)
                ch.link(dve.tensor_scalar(over[:], rank, float(CAP), FAR, ALU.is_ge, ALU.mult))
                ch.step(dve.tensor_tensor(slot_e[:], rank, ebase[:].unsqueeze(1).to_broadcast([P, NT, NE]), ALU.add))
                ch.step(dve.tensor_tensor(slot_e[:], slot_e[:], over[:], ALU.add))
                ch.step(dve.tensor_tensor(ohs[:], oh[:], slot_e[:].unsqueeze(2).to_broadcast([P, NT, TOPK, NE]),
                                          ALU.mult))
                ch.step(dve.tensor_reduce(slotf[:], ohs[:].rearrange("p t k e -> p (t k) e"), AX.X, ALU.add))
                dve.tensor_copy(slot[:], slotf[:]).then_inc(slot_ready, 1)

            def gate_of(i):
                return modb[:, i, :].unsqueeze(1).to_broadcast([P, NT, H])

            def middle(b, n, post, pre):
                if pre:
                    dve.wait_ge(x_landed, 16 * (n + 1))
                    dve.wait_ge(moda_landed, 16 * (n + 1))
                    norm(x_in, h1, st, mv, rstd, moda[:, 1, :], moda[:, 0, :], h1_ready,
                         var1_ready, rs1_ready, n)
                if post:
                    dve.wait_ge(modb_landed, 16 * (b + 1))
                    dve.wait_ge(res_ready, b + 1)
                    dve.wait_ge(attn_ps, 2 * (b + 1))
                    ch.step(dve.tensor_tensor(tmp[:], PS[:, 6:8, :].rearrange("p a (c n) -> p (a c) n", n=H),
                                              gate_of(0), ALU.mult))
                    dve.tensor_tensor(x1[:], tmp[:], x_res[:], ALU.add).then_inc(x1_ready, 1)
                    dve.wait_ge(x1_ready, b + 1)
                    dve.wait_ge(h2_out, 16 * b + 16)
                    norm(x1, h2, st2, mv2, rstd2, modb[:, 2, :], modb[:, 1, :], h2_ready,
                         var2_ready, rs2_ready, b)
                if pre:
                    dve.wait_ge(rsq_ready, n + 1)
                    for t in range(NT):
                        ins = dve.tensor_scalar(qn[:, t, :], PS[:, 2 + t, 0:QL], ssq[:, 0, t:t + 1], None, ALU.mult)
                        if t < NT - 1:
                            ch.link(ins)
                    ins.then_inc(qn_ready, 1)
                    for t in range(NT):
                        ch.link(dve.scalar_tensor_tensor(out=kmat[:, t, 0:KL], in0=PS[:, 2 + t, QL:QL + KL],
                                                         scalar=ssq[:, 1, t:t + 1], in1=kg_sb[:],
                                                         op0=ALU.mult, op1=ALU.mult))
                    for part in rope_parts(PS[:, 2:6, QL + KL:FW], kr1, kr2, 1):
                        ch.link(part())
                    ch.wait()
                    dve.tensor_tensor(kmat[:, :, KL:], kr1[:], kr2[:], ALU.add).then_inc(k_ready, 1)
                if post:
                    silu_mid(b, 0, 2, (3, 4))
                    silu_mid(b, 1, 0, (0, 1))
                if pre:
                    for part in q_rope(n * NPAIR):
                        part()
                if post:
                    silu_mid(b, 2, 1, (3, 4))
                    route(b)
                    slots(b)
                    dve.wait_ge(down_ps, 2 * (b + 1))
                    ch.step(dve.tensor_tensor(tmp[:], PS[:, 0:2, :].rearrange("p a (c n) -> p (a c) n", n=H),
                                              gate_of(3), ALU.mult))
                    dve.wait_ge(base_out, 16 * b + 16)
                    dve.tensor_tensor(base[:], tmp[:], x1[:], ALU.add).then_inc(base_ready, 1)

            dve.wait_ge(const_ready, 3)
            middle(0, 0, False, True)
            assert ch.n == CHAIN_PROLOGUE, ch.n

            def batch(b, base, more):
                with dve.Fori(0, NPAIR - 1) as p:
                    ch.base, ch.n = base + p * CHAIN_PAIR, 0
                    pair(b * NPAIR + p, True)
                    assert ch.n == CHAIN_PAIR, ch.n
                ch.base, ch.n = base + (NPAIR - 1) * CHAIN_PAIR, 0
                pair(b * NPAIR + NPAIR - 1, False)
                middle(b, b + 1 if more else None, True, more)

            with dve.Fori(0, LAST) as b:
                batch(b, CHAIN_PROLOGUE + b * CHAIN_BATCH, True)
                assert (NPAIR - 1) * CHAIN_PAIR + ch.n == CHAIN_BATCH, (NPAIR - 1) * CHAIN_PAIR + ch.n
            batch(LAST, CHAIN_PROLOGUE + LAST * CHAIN_BATCH, False)

            dve.wait_ge(tab_landed, 16)
            ch.link(dve.tensor_copy(toku[:], tab[:, :, 0]))
            ch.step(dve.tensor_scalar(bidf[:], tab[:, :, 0], float(T - 1), None, ALU.min))
            ch.step(dve.tensor_copy(bidi[:], bidf[:]))
            dve.tensor_scalar(bid[:], bidi[:], 9, None, ALU.arith_shift_right).then_inc(tok_ready, 1)
            for e in range(NE):
                q = e % 2
                dve.wait_ge(eth_ready, e + 1)
                if e >= 2:
                    dve.wait_ge(emT_ps, e - 1)
                ch.step(dve.scalar_tensor_tensor(out=eth[:], in0=eth[:], scalar=1.0, in1=PS[:, 2 + q, 0:IM],
                                                 op0=ALU.add, op1=ALU.mult))
                dve.tensor_tensor(emid[:, q, :], eth[:], PS[:, 2 + q, IM:2 * IM], ALU.mult).then_inc(emid_ready, 1)
                dve.wait_ge(ey_ps, e + 1)
                dve.wait_ge(xg_landed[q], 32 * (e // 2 + 1))
                if e >= 2:
                    dve.wait_ge(added, 16 * (e - 1))
                dve.scalar_tensor_tensor(out=ey[:, q, :], in0=PS[:, 6 + q, 0:H], scalar=tab[:, e, 1:2],
                                         in1=gbg[:, q, :], op0=ALU.mult, op1=ALU.mult).then_inc(ey_ready, 1)


def _rope_tables():
    inv = (np.float32(1.0) / np.float32(10000.0) ** (np.arange(0, DR, 2, dtype=np.float32) / np.float32(DR))).astype(np.float32)
    ang = np.arange(S, dtype=np.float32)[:, None] * inv
    c, s = np.cos(ang).astype(np.float32), np.sin(ang).astype(np.float32)
    return np.concatenate([c, c], -1), np.concatenate([-s, s], -1)


def kernel(**inputs):
    import concourse.bacc as bacc
    from concourse.bass_utils import run_bass_kernel_spmd

    a = {k: np.asarray(v) for k, v in inputs.items()}
    wqb = a["L0_attn_w_qb"].reshape(QL, NH, DN + DR)
    wkvb = a["L0_attn_w_kvb"].reshape(KL, NH, DN + DV)
    cos, sin = _rope_tables()
    arrays = {
        "x": a["L0_attn_hidden"],
        "wkva": a["L0_attn_w_kv_a"],
        "wqnT": wqb[:, :, :DN].transpose(1, 2, 0),
        "wqpe": wqb[:, :, DN:],
        "wkT": wkvb[:, :, :DN].transpose(2, 1, 0),
        "wvT": wkvb[:, :, DN:].transpose(2, 1, 0),
        "wo": a["L0_attn_w_o"],
        "qgam": a["L0_attn_q_a_gamma"],
        "kgam": a["L0_attn_kv_a_gamma"],
        "sgate": np.concatenate([a["L0_ffn_sw_gate"], a["L0_ffn_gate_w"].T], axis=1),
        "sup": a["L0_ffn_sw_up"],
        "sdown": a["L0_ffn_sw_down"],
        "egate": a["L0_ffn_w_gate"],
        "eup": a["L0_ffn_w_up"],
        "edown": a["L0_ffn_w_down"],
        "cT": a["L0_c"].T,
        "wmod": a["L0_wmod"],
        "cos": cos,
        "sin": sin,
    }
    nc = bacc.Bacc("TRN2", target_bir_lowering=False, num_devices=1)
    feed, args = {}, []
    for name, v in arrays.items():
        v = np.ascontiguousarray(v)
        feed[f"in_{name}"] = v
        args.append(nc.dram_tensor(f"in_{name}", v.shape, mybir.dt.from_np(v.dtype), kind="ExternalInput").ap())
    out = nc.dram_tensor("out_0", (B, S, H), F32, kind="ExternalOutput").ap()
    adaln_block(nc, *args, out)
    r = run_bass_kernel_spmd(nc, [feed], core_ids=[0])
    return r.results[0]["out_0"]
```

```python
from contextlib import ExitStack

import numpy as np

import concourse.bass as bass
from concourse import mybir

F32 = mybir.dt.float32
F32R = mybir.dt.float32r
BF16 = mybir.dt.bfloat16
I32 = mybir.dt.int32
U32 = mybir.dt.uint32
ALU = mybir.AluOpType
ACT = mybir.ActivationFunctionType
AX = mybir.AxisListType

P = 128
B, S, H = 8, 512, 256
T = B * S
NT = S // P
LAST = B - 1
NH, DN, DR, DV = 16, 128, 64, 128
QL, KL = 192, 64
QR = QL - P
FW = QL + KL + DR
NPAIR = NH // 2
NE, TOPK, IM, IS, CAP = 16, 4, 176, 352, 128
IR = IM - P
MT = [(0, 128), (128, 128), (256, 96)]
LN_EPS, RMS_EPS = 1e-5, 1e-6
SCALE = 1.0 / float(np.sqrt(DN + DR))
NEG = -1e30
FAR = 1e5
UNITS = [(h, i) for h in range(2) for i in (3, 2, 1, 0)]
NU = len(UNITS)
UW = [(i + 1) * P for _, i in UNITS]
UO = [sum(UW[:u]) for u in range(NU)]
SBANK = [0, 1, 2, 0, 1, 2, 0, 1]
GROUPS = [((0,), 3), ((1,), 4), ((2, 3), 2), ((4,), 0), ((5,), 1), ((6, 7), 3)]
RBANK = 4
OBANK, QBANKS = 5, [6, 7]
KV_ORDER = [2, 0, 1, 3]
SA, CA, GA, SB, CB, GB = range(6)

CHAIN_PROLOGUE, CHAIN_PAIR, CHAIN_BATCH = 48, 4, 93


class Chain:

    def __init__(self, eng, sem):
        self.eng, self.sem, self.base, self.n = eng, sem, 0, 0

    def link(self, ins):
        self.n += 1
        ins.then_inc(self.sem, 1)

    def wait(self):
        self.eng.wait_ge(self.sem, self.base + self.n)

    def step(self, ins):
        self.link(ins)
        self.wait()


def adaln_block(nc, x, wkva, wqnT, wqpe, wkT, wvT, wo, qgam, kgam, sgate, sup, sdown,
                egate, eup, edown, cT, wmod, cos, sin, out):
    xr = x.rearrange("b s h -> (b s) h")
    outr = out.rearrange("b s h -> (b s) h")
    mod_dram = nc.dram_tensor("mod_dram", (B, 4 * H), F32, kind="Internal").ap()
    gb_dram = nc.dram_tensor("gb_dram", (B, H), F32, kind="Internal").ap()
    h2_dram = nc.dram_tensor("h2_dram", (T + P, H), F32, kind="Internal").ap()
    tab_dram = nc.dram_tensor("tab_dram", (NE * CAP, 2), F32, kind="Internal").ap()

    def wait_alone(eng, semaphore, value):
        if not isinstance(value, int):
            value = eng.snap(eng.to_reg(value))
            eng.wait_ge(const_ready, 3)
        eng.wait_ge(semaphore, value)

    def rows(ap, b):
        return ap[bass.ts(b, S), :].rearrange("(t p) h -> p t h", p=P)

    with ExitStack() as ctx:
        def sb(name, shape, dt=F32):
            return ctx.enter_context(nc.sbuf_tensor(name, shape, dt))

        def sem(name):
            return ctx.enter_context(nc.semaphore(name))

        wq0h = sb("wq0h", [P, NH * P], F32R)
        wq0l = sb("wq0l", [P, NH * P], F32R)
        wq1hh = sb("wq1hh", [P, NH * P], F32R)
        wq1l = sb("wq1l", [QR, NH * P], F32R)
        wvo = sb("wvo", [P, NPAIR, H])
        wkva_sb = sb("wkva_sb", [P, 2, FW])
        sg_sb = sb("sg_sb", [P, 2, IS + NE])
        su_sb = sb("su_sb", [P, 2, IS])
        sd_sb = sb("sd_sb", [P, 3, H])
        cos_sb = sb("cos_sb", [P, NT, DR])
        sin_sb = sb("sin_sb", [P, NT, DR])
        qg_sb = sb("qg_sb", [P, 2])
        kg_sb = sb("kg_sb", [P, KL])
        ident = sb("ident", [P, P])
        identb = sb("identb", [P, P], BF16)
        caus = sb("caus", [P, P])
        causb = sb("causb", [P, P], BF16)
        tri = sb("tri", [P, P])
        trib = sb("trib", [P, P], BF16)
        onesb = sb("onesb", [P, P], BF16)
        iota_i = sb("iota_i", [P, 3, NE], I32)
        eid = sb("eid", [P, NE])
        ebase = sb("ebase", [P, NE])
        tid = sb("tid", [P, NT])
        tab_init = sb("tab_init", [P, NE, 2])
        zrow = sb("zrow", [P, H])
        mhalf = sb("mhalf", [P, 2 * NT])

        x_in = sb("x_in", [P, NT, H])
        x_res = sb("x_res", [P, NT, H])
        x1 = sb("x1", [P, NT, H])
        h1 = sb("h1", [P, NT, H])
        h2 = sb("h2", [P, NT, H])
        tmp = sb("tmp", [P, NT, H])
        hT = sb("hT", [P, 2, S])
        h2T = sb("h2T", [P, 2, S])
        modT = sb("modT", [P, 8, B])
        mod1 = sb("mod1", [P, 4])
        mod2 = sb("mod2", [P, 4])
        modb = sb("modb", [P, 4, H])
        st = sb("st", [P, NT, 6])
        mv = sb("mv", [P, NT, 2])
        rstd = sb("rstd", [P, NT])
        st2 = sb("st2", [P, NT, 6])
        mv2 = sb("mv2", [P, NT, 2])
        rstd2 = sb("rstd2", [P, NT])
        sq = sb("sq", [P, QL])
        ssq = sb("ssq", [P, 2, NT])
        qn = sb("qn", [P, NT, 2 * P])
        kmat = sb("kmat", [P, NT, KL + DR])
        kr1 = sb("kr1", [P, NT, DR])
        kr2 = sb("kr2", [P, NT, DR])
        kTh = sb("kTh", [P, S], F32R)
        kTl = sb("kTl", [P, S], F32R)
        ql0h = sb("ql0h", [P, S], F32R)
        ql0l = sb("ql0l", [P, S], F32R)
        ql1s = sb("ql1s", [P, S], F32R)
        base = sb("base", [P, NT, H])

        qtok = sb("qtok", [P, 2 * NT, P])
        qr1 = sb("qr1", [P, 2 * NT, DR])
        qr2 = sb("qr2", [P, 2 * NT, DR])
        qTh = sb("qTh", [P, 2, S], F32R)
        qTl = sb("qTl", [P, 2, S], F32R)
        ql1t = qTh[:, 1, :]
        probs = sb("probs", [P, sum(UW)])
        pT = sb("pT", [P, 2, NT, S])
        nmax = sb("nmax", [P, NU])
        psums = sb("psums", [P, NU])
        prec = sb("prec", [P, NU])
        oT = sb("oT", [P, NPAIR, S])

        th = sb("th", [P, S])
        mid = sb("mid", [P, S])
        wide = mid
        rb = th
        midT = sb("midT", [P, 3, S])
        lgT = sb("lgT", [NE, S])
        lmax = sb("lmax", [P, NT])
        ls = sb("ls", [P, NT, NE])
        ex = sb("ex", [P, NT, NE])
        esum = sb("esum", [P, NT])
        score = sb("score", [P, NT, NE])
        top = sb("top", [P, NT, 8])
        topi = sb("topi", [P, NT, 8], U32)
        topf = sb("topf", [P, NT, TOPK])
        tsum = sb("tsum", [P, NT])
        oh = sb("oh", [P, NT, TOPK, NE])
        ohs = sb("ohs", [P, NT, TOPK, NE])
        mask = sb("mask", [P, NT, NE])
        maskb = sb("maskb", [P, NT, NE], BF16)
        before = sb("before", [P, NT + 1, NE])
        beforeb = sb("beforeb", [P, NT, NE], BF16)
        slot_e = sb("slot_e", [P, NT, NE])
        over = sb("over", [P, NT, NE])
        slotf = sb("slotf", [P, NT * TOPK])
        slot = sb("slot", [P, NT * TOPK], U32)
        entry = sb("entry", [P, NT * TOPK, 2])

        tab = sb("tab", [P, NE, 2])
        toku = sb("toku", [P, NE], U32)
        bidf = sb("bidf", [P, NE])
        bidi = sb("bidi", [P, NE], I32)
        bid = sb("bid", [P, NE], I32)
        xg, gbg, ey = x_in, h1, x_res
        RX = NT
        xgT = sb("xgT", [P, 2, 2, P])
        eth = sb("eth", [P, IM])
        emid = sb("emid", [P, 2, IM])
        emT = sb("emT", [P, 2, 2, P])

        cT_sb = sb("cT_sb", [P, 2, B])
        cth = sb("cth", [P, 2, B])
        csl = sb("csl", [P, 2, B])
        mod_sb = midT[0:B].rearrange("b a s -> b (a s)").rearrange("b (a h) -> b a h", h=H)
        sgn = mid[0:B].rearrange("b (a h) -> b a h", h=H)
        pT_flat = pT[:].rearrange("p a b s -> p (a b s)")
        oT_flat = oT[:].rearrange("p a s -> p (a s)")
        wo_st = pT_flat.rearrange("p (h n) -> p h n", h=NH)
        wqn_st = oT_flat.rearrange("p (h n) -> p h n", h=NH)
        wk_st = h2[:].rearrange("p t n -> p (t n)").rearrange("p (h n) -> p h n", h=NH)
        wv_st = x1[:].rearrange("p t n -> p (t n)").rearrange("p (h n) -> p h n", h=NH)
        wm_st = [t[:].rearrange("p a n -> p (a n)").rearrange("p (c n) -> p c n", c=2) for t in (tmp, base, h2T)]
        pe0_st = probs[:, 0:NH * DR].rearrange("p (h n) -> p h n", h=NH)
        pe1_st = probs[:, NH * DR:2 * NH * DR].rearrange("p (h n) -> p h n", h=NH)

        EW = 4 * IM + 2 * H
        ering = ([pT_flat[:, k * EW:(k + 1) * EW] for k in range(3)] + [probs[:, k * EW:(k + 1) * EW] for k in range(2)]
                 + [oT_flat[:, k * EW:(k + 1) * EW] for k in range(3)])
        RE = len(ering)

        PS = ctx.enter_context(nc.psum_tensor("PS", [P, 8, 512], F32))
        qps = PS[:, 6:8, :].rearrange("p a (c d) -> p (a c) d", d=P)

        w_in = sem("w_in")
        mod_in = sem("mod_in")
        const_ready = sem("const_ready")
        c_tanh = sem("c_tanh")
        c_ready = sem("c_ready")
        mod_ps = sem("mod_ps")
        mod_ready = sem("mod_ready")
        mod_out = sem("mod_out")
        init_out = sem("init_out")
        wabs_ps = sem("wabs_ps")
        wabs_ready = sem("wabs_ready")
        x_landed = sem("x_landed")
        modb_landed = sem("modb_landed")
        res_ready = sem("res_ready")
        modT_ps = sem("modT_ps")
        modT_ready = sem("modT_ready")
        mod1_ready = sem("mod1_ready")
        mod2_ready = sem("mod2_ready")
        h1_ready = sem("h1_ready")
        hT_ps = sem("hT_ps")
        hT_ready = sem("hT_ready")
        kv_ps = sem("kv_ps")
        ssq_ready = sem("ssq_ready")
        k_ready = sem("k_ready")
        kq_ps = sem("kq_ps")
        kqh_ready = sem("kqh_ready")
        kql_ready = sem("kql_ready")
        q_ps = sem("q_ps")
        nope_ready = sem("nope_ready")
        rope_ready = sem("rope_ready")
        qT_ps = sem("qT_ps")
        qTh_ready = sem("qTh_ready")
        qTl_ready = sem("qTl_ready")
        s_ps = sem("s_ps")
        max_ready = sem("max_ready")
        exp_ready = sem("exp_ready")
        wide_ready = sem("wide_ready")
        r_ps = sem("r_ps")
        rb_ready = sem("rb_ready")
        pT_ps = sem("pT_ps")
        pT_act = sem("pT_act")
        pT_dve = sem("pT_dve")
        o_ps = sem("o_ps")
        oT_ready = sem("oT_ready")
        attn_ps = sem("attn_ps")
        x1_ready = sem("x1_ready")
        n2_ready = sem("n2_ready")
        h2_scaled = sem("h2_scaled")
        h2_ready = sem("h2_ready")
        h2_out = sem("h2_out")
        h2T_ps = sem("h2T_ps")
        h2T_ready = sem("h2T_ready")
        gu_ps = sem("gu_ps")
        th_ready = sem("th_ready")
        mid_ready = sem("mid_ready")
        lg_ready = sem("lg_ready")
        lgT_ps = sem("lgT_ps")
        ls_ready = sem("ls_ready")
        ex_ready = sem("ex_ready")
        mask_ready = sem("mask_ready")
        rank_ps = sem("rank_ps")
        slot_ready = sem("slot_ready")
        scattered = sem("scattered")
        entries_free = sem("entries_free")
        down_ps = sem("down_ps")
        gated_ready = sem("gated_ready")
        base_ready = sem("base_ready")
        base_out = sem("base_out")
        dve_chain = sem("dve_chain")
        pool_chain = sem("pool_chain")
        var1_ready = sem("var1_ready")
        rs1_ready = sem("rs1_ready")
        var2_ready = sem("var2_ready")
        rs2_ready = sem("rs2_ready")
        rsq_ready = sem("rsq_ready")
        eps1 = sem("eps1")
        eps2 = sem("eps2")
        eps3 = sem("eps3")
        tab_landed = sem("tab_landed")
        tok_ready = sem("tok_ready")
        ew_landed = [sem(f"ew_landed{i}") for i in range(RE)]
        xg_landed = [sem(f"xg_landed{i}") for i in range(NT)]
        xgT_ps = sem("xgT_ps")
        xgT_ready = sem("xgT_ready")
        egu_ps = sem("egu_ps")
        eth_ready = sem("eth_ready")
        emid_ready = sem("emid_ready")
        emT_ps = sem("emT_ps")
        emT_ready = sem("emT_ready")
        ey_ps = sem("ey_ps")
        ey_ready = sem("ey_ready")
        added = sem("added")

        block = ctx.enter_context(nc.Block())

        W_LOADS = 16
        ew_g = lambda r, k: ering[r][:, k * 2 * IM:(k + 1) * 2 * IM]
        ew_d = lambda r, k, n: ering[r][0:n, 4 * IM + k * H:4 * IM + (k + 1) * H]

        @block.sync
        def _(sp):
            sp.dma_start(cT_sb[:], cT.rearrange("(c p) b -> p c b", p=P)).then_inc(mod_in, 16)
            for n in range(3):
                sp.dma_start(wm_st[n], wmod[:, n * 512:(n + 1) * 512].rearrange("(c p) n -> p c n", p=P)
                             ).then_inc(mod_in, 16)
            sp.dma_start(x_in[:], rows(xr, 0)).then_inc(x_landed, 16)
            sp.dma_start(wkva_sb[:], wkva.rearrange("(c p) n -> p c n", p=P)).then_inc(w_in, 16)
            sp.dma_start(wqn_st[:, :, 0:QL], wqnT.rearrange("h p n -> p h n")).then_inc(w_in, 16)
            sp.dma_start(wqn_st[:, :, QL:], wqnT[:, :, P:QL].rearrange("h p n -> p h n")).then_inc(w_in, 16)
            sp.dma_start(wk_st, wkT).then_inc(w_in, 16)
            sp.dma_start(pe0_st, wqpe[0:P]).then_inc(w_in, 16)
            sp.dma_start(pe1_st[0:QR], wqpe[P:QL]).then_inc(w_in, 16)
            sp.dma_start(pe1_st[QR:P], wqpe[P:QL]).then_inc(w_in, 16)
            sp.dma_start(qg_sb[:, 0:1], qgam[0:P].rearrange("(p a) -> p a", a=1)).then_inc(w_in, 16)
            for lo in (0, QR):
                sp.dma_start(qg_sb[lo:lo + QR, 1:2], qgam[P:QL].rearrange("(p a) -> p a", a=1)).then_inc(w_in, 16)
            sp.dma_start(kg_sb[:], kgam.partition_broadcast(P)).then_inc(w_in, 16)
            sp.dma_start(cos_sb[:], cos.rearrange("(t p) d -> p t d", p=P)).then_inc(w_in, 16)
            sp.dma_start(sin_sb[:], sin.rearrange("(t p) d -> p t d", p=P)).then_inc(w_in, 16)
            sp.dma_start(wv_st, wvT).then_inc(w_in, 16)
            sp.dma_start(wo_st, wo.rearrange("(h p) n -> p h n", p=P)).then_inc(w_in, 16)
            sp.dma_start(sg_sb[:], sgate.rearrange("(c p) n -> p c n", p=P)).then_inc(w_in, 16)
            sp.dma_start(su_sb[:], sup.rearrange("(c p) n -> p c n", p=P)).then_inc(init_out, 16)
            sp.dma_start(sd_sb[:, 0:2, :], sdown[0:2 * P].rearrange("(c p) n -> p c n", p=P)).then_inc(init_out, 16)
            sp.dma_start(sd_sb[0:MT[2][1], 2, :], sdown[2 * P:IS]).then_inc(init_out, 16)
            sp.wait_ge(mod_ready, 1)
            sp.dma_start(mod_dram, midT[0:B].rearrange("b a s -> b (a s)")[:, 2 * H:]).then_inc(mod_out, 16)
            sp.dma_start(gb_dram, mod_sb[:, GB, :]).then_inc(mod_out, 16)
            sp.wait_ge(const_ready, 3)
            sp.dma_start(h2_dram[T:T + P, :], zrow[:]).then_inc(init_out, 16)
            sp.dma_start(tab_dram.rearrange("(e p) c -> p e c", p=P), tab_init[:]).then_inc(init_out, 16)
            sp.wait_ge(mod_out, 32)

            def load_modb(b):
                sp.dma_start(modb[:].rearrange("p a h -> p (a h)"),
                             mod_dram[bass.ds(b, 1), :].rearrange("a n -> (a n)").partition_broadcast(P)
                             ).then_inc(modb_landed, 16)

            def store_batch(b):
                sp.wait_ge(h2_ready, b + 1)
                sp.dma_start(rows(h2_dram, b), h2[:]).then_inc(h2_out, 16)
                sp.wait_ge(base_ready, b + 2)
                sp.dma_start(rows(outr, b), base[:]).then_inc(base_out, 16)

            load_modb(0)
            with sp.Fori(0, B - 1) as b:
                n = b + 1
                sp.wait_ge(h1_ready, n)
                sp.wait_ge(res_ready, n)
                sp.dma_start(x_in[:], rows(xr, n)).then_inc(x_landed, 16)
                store_batch(b)
                load_modb(n)
            store_batch(B - 1)
            sp.wait_ge(scattered, B * NT * TOPK * 16)
            sp.dma_start(tab[:], tab_dram.rearrange("(e p) c -> p e c", p=P)).then_inc(tab_landed, 16)
            sp.wait_ge(added, NE * 16)
            sp.wait_ge(base_out, B * 16 + 16)
            sp.wait_ge(h2_out, B * 16 + 16)
            sp.wait_ge(init_out, 5 * 16)

        @block.gpsimd
        def _(pool):
            ch = Chain(pool, pool_chain)
            ch.link(pool.memset(ident[:], 0.0))
            ch.link(pool.memset(caus[:], 0.0))
            ch.link(pool.memset(tri[:], 0.0))
            ch.link(pool.memset(zrow[:], 0.0))
            ch.link(pool.memset(mhalf[:], -0.5))
            ch.link(pool.memset(tab_init[:], 0.0))
            ch.wait()
            ch.link(pool.affine_select(out=ident[:], in_=ident[:], compare_op=ALU.not_equal, fill=1.0, base=0,
                                       pattern=[[-1, P]], channel_multiplier=1))
            ch.link(pool.affine_select(out=caus[:], in_=caus[:], compare_op=ALU.is_ge, fill=NEG, base=0,
                                       pattern=[[-1, P]], channel_multiplier=1))
            ch.link(pool.affine_select(out=tri[:], in_=tri[:], compare_op=ALU.is_ge, fill=1.0, base=0,
                                       pattern=[[-1, P]], channel_multiplier=1))
            ch.link(pool.iota(iota_i[:, 0, :], pattern=[[1, NE]], base=0, channel_multiplier=0))
            ch.link(pool.iota(iota_i[:, 1, :], pattern=[[0, NE]], base=T, channel_multiplier=1))
            ch.link(pool.iota(iota_i[:, 2, 0:NT], pattern=[[P, NT]], base=0, channel_multiplier=1))
            ch.wait()
            ch.link(pool.tensor_copy(identb[:], ident[:]))
            ch.link(pool.tensor_copy(causb[:], caus[:]))
            ch.link(pool.tensor_copy(trib[:], tri[:]))
            ch.link(pool.memset(onesb[:], 1.0))
            ch.link(pool.tensor_copy(eid[:], iota_i[:, 0, :]))
            ch.link(pool.tensor_copy(tid[:], iota_i[:, 2, 0:NT]))
            ch.link(pool.tensor_copy(tab_init[:, :, 0], iota_i[:, 1, :]))
            ch.link(pool.memset(before[:, 0, :], 0.0))
            ch.wait()
            pool.tensor_scalar(ebase[:], eid[:], float(CAP), None, ALU.mult).then_inc(const_ready, 3)

            def root(dst, src, eps, added_eps, ready, k):
                pool.tensor_scalar(dst, src, eps, None, ALU.add).then_inc(added_eps, 1)
                pool.wait_ge(added_eps, k + 1)
                pool.tensor_tensor(dst, dst, mhalf[:, 0:dst.shape[1]], ALU.pow).then_inc(ready, 1)

            def roots_pre(n):
                wait_alone(pool, var1_ready, NT * (n + 1))
                root(rstd[:], mv[:, :, 1], LN_EPS, eps1, rs1_ready, n)
                wait_alone(pool, ssq_ready, 8 * (n + 1))
                ssqf = ssq[:].rearrange("p a t -> p (a t)")
                root(ssqf, ssqf, RMS_EPS, eps3, rsq_ready, n)

            def post(b, n):
                wait_alone(pool, var2_ready, NT * b + 3)
                root(rstd2[:, 0:3], mv2[:, 0:3, 1], LN_EPS, eps2, rs2_ready, 2 * b)
                wait_alone(pool, var2_ready, NT * (b + 1))
                root(rstd2[:, 3:], mv2[:, 3:, 1], LN_EPS, eps2, rs2_ready, 2 * b + 1)
                spread = lambda i: modb[:, i, :].unsqueeze(1).to_broadcast([P, NT, H])
                pool.wait_ge(n2_ready, 2 * (b + 1))
                pool.wait_ge(h2T_ps, 2 * (b + 1))
                pool.tensor_tensor(h2[:], h2[:], spread(2), ALU.mult).then_inc(h2_scaled, 1)
                pool.wait_ge(h2_scaled, b + 1)
                pool.tensor_tensor(h2[:], h2[:], spread(1), ALU.add).then_inc(h2_ready, 1)
                if n is not None:
                    wait_alone(pool, x1_ready, 3 * (b + 1))
                    wait_alone(pool, x_landed, (b + 2) * 16)
                    pool.tensor_copy(x_res[:], x_in[:]).then_inc(res_ready, 1)

            def shared(b):
                pool.wait_ge(base_out, 16 * b + 16)
                pool.wait_ge(gated_ready, b + 1)
                pool.tensor_tensor(base[:], tmp[:], x1[:], ALU.add).then_inc(base_ready, 1)

            roots_pre(0)
            pool.wait_ge(x_landed, 16)
            pool.tensor_copy(x_res[:], x_in[:]).then_inc(res_ready, 1)
            pool.wait_ge(init_out, 5 * 16)

            def scatter(b):
                wait_alone(pool, slot_ready, b + 1)
                for j in range(NT * TOPK):
                    pool.indirect_dma_start(
                        tab_dram[:, :], bass.IndirectOffsetOnAxis(ap=slot[:, j:j + 1], axis=0),
                        entry[:, j, :], None, bounds_check=NE * CAP - 1, oob_is_err=False,
                    ).then_inc(scattered, 16)
                pool.wait_ge(scattered, (b + 1) * NT * TOPK * 16)
                pool.sem_inc(entries_free, 1)

            with pool.Fori(0, B - 1) as b:
                roots_pre(b + 1)
                post(b, b + 1)
                shared(b)
                scatter(b)
            post(LAST, None)
            scatter(LAST)
            shared(LAST)

            pool.wait_ge(tok_ready, 1)
            pool.wait_ge(h2_out, B * 16 + 16)

            def gather(e):
                r = e % RX
                if e >= RX:
                    pool.wait_ge(xgT_ps, e - RX + 1)
                pool.indirect_dma_start(xg[:, r, :], None, h2_dram[:, :],
                                        bass.IndirectOffsetOnAxis(ap=toku[:, e:e + 1], axis=0),
                                        bounds_check=T + P - 1).then_inc(xg_landed[r], 16)
                pool.indirect_dma_start(gbg[:, r, :], None, gb_dram[:, :],
                                        bass.IndirectOffsetOnAxis(ap=bid[:, e:e + 1].bitcast(U32), axis=0),
                                        bounds_check=B - 1).then_inc(xg_landed[r], 16)

            for e in range(RX):
                gather(e)
            pool.wait_ge(base_out, B * 16 + 16)
            for e in range(NE):
                pool.wait_ge(ey_ready, e + 1)
                if e:
                    pool.wait_ge(added, 16 * e)
                pool.indirect_dma_start(outr, bass.IndirectOffsetOnAxis(ap=toku[:, e:e + 1], axis=0),
                                        ey[:, e % RX, :], None, bounds_check=T - 1, oob_is_err=False,
                                        compute_op=ALU.add).then_inc(added, 16)
                if e + RX < NE:
                    gather(e + RX)

        @block.tensor
        def _(pe):
            pe.wait_ge(mod_in, 64)
            pe.wait_ge(c_ready, 1)
            for n in range(3):
                for c in range(2):
                    mm = pe.matmul(PS[0:B, n, :], csl[:, c, :], wm_st[n][:, c, :],
                                   start=c == 0, stop=c == 1)
            mm.then_inc(mod_ps, 1)
            pe.wait_ge(w_in, W_LOADS * 16)
            pe.wait_ge(const_ready, 3)
            for h in range(NH):
                bank, col = 3 + h // 8, (h % 8) * KL
                pe.matmul(PS[:, bank, col:col + KL], wqn_st[:, h, 0:P], wk_st[:, h, :], start=True, stop=True)
                mm = pe.matmul(PS[:, 2 + bank, col:col + KL], wqn_st[:, h, P:], wk_st[:, h, :], start=True, stop=True)
            mm.then_inc(wabs_ps, 1)
            pe.wait_ge(mod_ready, 1)
            for k in range(8):
                mm = pe.transpose(PS[:, 7, k * B:(k + 1) * B],
                                  mod_sb[:, (SA, CA, SB, CB)[k // 2], bass.ts(k % 2, P)], ident[0:B, 0:B])
            mm.then_inc(modT_ps, 1)
            pe.wait_ge(wabs_ready, 1)
            for h in range(NH):
                p, half = h // 2, (h % 2) * KL
                mm = pe.matmul(PS[half:half + KL, p // 2, (p % 2) * H:(p % 2 + 1) * H], wv_st[:, h, :],
                               wo_st[:, h, :], start=True, stop=True)
            mm.then_inc(wabs_ps, 1)
            pe.wait_ge(wabs_ready, 2)

            def q_project(p, g, tiles):
                cols = bass.ts(p, 2 * P)
                for t in tiles:
                    dst, tok = PS[:, QBANKS[t // 2], (t % 2) * 2 * P:(t % 2 + 1) * 2 * P], bass.ts(t, P)
                    pe.matmul(dst, ql0h[:, tok], wq0h[:, cols], start=True, stop=False)
                    pe.matmul(dst, ql0h[:, tok], wq0l[:, cols], start=False, stop=False)
                    pe.matmul(dst, ql0l[:, tok], wq0h[:, cols], start=False, stop=False)
                    pe.matmul(dst, ql1s[:, tok], wq1hh[:, cols], start=False, stop=False)
                    mm = pe.matmul(dst, ql1s[0:QR, tok], wq1l[:, cols], start=False, stop=True)
                mm.then_inc(q_ps, 2 if len(tiles) == NT else 1)

            def q_turn(g):
                pe.wait_ge(nope_ready, g + 1)
                pe.wait_ge(rope_ready, g + 1)
                for h in range(2):
                    for t in range(NT):
                        mm = pe.transpose(PS[:, QBANKS[h], bass.ts(t, P)], qtok[:, 2 * t + h, :], ident[:])
                    mm.then_inc(qT_ps, 1)

            def scores(g, first, units):
                for u in units:
                    h, i = UNITS[u]
                    bank, n, rows_q = SBANK[u], UW[u], bass.ts(i, P)
                    if i == NT - 1:
                        pe.wait_ge(qTl_ready, 2 * g + h + 1)
                    if u >= 3:
                        pe.wait_ge(exp_ready, g * NU + u - 2)
                    elif not first:
                        pe.wait_ge(*((pT_dve, 2 * g - 1), (pT_act, 4 * g), (pT_act, 4 * g - 1))[u])
                    pe.matmul(PS[:, bank, 0:n], qTh[:, h, rows_q], kTh[:, 0:n], start=True, stop=False)
                    pe.matmul(PS[:, bank, 0:n], qTh[:, h, rows_q], kTl[:, 0:n], start=False, stop=False)
                    pe.matmul(PS[:, bank, 0:n], qTl[:, h, rows_q], kTh[:, 0:n], start=False, stop=False)
                    pe.matmul(PS[:, bank, i * P:n], identb[:], causb[:], start=False, stop=True).then_inc(s_ps, 1)

            def turn_probs(g, first, groups):
                for k in groups:
                    units, bank = GROUPS[k]
                    pe.wait_ge(exp_ready, g * NU + max(units[-1] + 1, (1, 2, 6, 7, 8, 8)[k]))
                    if k == 0 and not first:
                        pe.wait_ge(pT_dve, 2 * g)
                    if k == 1 and not first:
                        pe.wait_ge(rb_ready, g)
                    if k == 5:
                        pe.wait_ge(pT_act, 4 * g + 1)
                    col = 0
                    for u in units:
                        for j in range(UNITS[u][1] + 1):
                            mm = pe.transpose(PS[:, bank, col:col + P], probs[:, UO[u] + j * P:UO[u] + (j + 1) * P],
                                              ident[:])
                            col += P
                    mm.then_inc(pT_ps, 1)

            def spread_sums(g):
                pe.wait_ge(wide_ready, g + 1)
                pe.wait_ge(pT_act, 4 * g + 2)
                for t in range(NT):
                    mm = pe.transpose(PS[:, RBANK, bass.ts(t, P)], wide[:, bass.ts(NT - 1 - t, P)], ident[:])
                mm.then_inc(r_ps, 1)

            def values(g):
                pe.wait_ge(pT_act, (g + 1) * 4)
                pe.wait_ge(pT_dve, (g + 1) * 2)
                pe.wait_ge(oT_ready, g + 1)
                for j in range(NT):
                    for h in range(2):
                        mm = pe.matmul(PS[h * KL:(h + 1) * KL, OBANK, j * P:S], kmat[:, j, 0:KL],
                                       pT[:, h, j, j * P:S], start=j == 0, stop=j == NT - 1)
                mm.then_inc(o_ps, 1)

            def step(p, b, first, last, more):
                g = b * NPAIR + p
                if not last:
                    q_project(p + 1, g + 1, (0, 1))
                scores(g, first, (3, 4))
                if not last:
                    q_project(p + 1, g + 1, (2, 3))
                scores(g, first, (5, 6, 7))
                if not first:
                    values(g - 1)
                if first and more:
                    ranks(b - 1)
                    pe.wait_ge(gated_ready, b)
                turn_probs(g, first, (0, 1))
                if not last:
                    q_turn(g + 1)
                elif more:
                    turn_h1(b + 1)
                turn_probs(g, first, (2, 3, 4, 5))
                spread_sums(g)
                if not last:
                    scores(g + 1, False, (0, 1, 2))
                if first and more:
                    pe.wait_ge(slot_ready, b)

            def ranks(b):
                pe.wait_ge(mask_ready, b + 1)
                pe.matmul(PS[:, OBANK, 64:64 + NT * NE], trib[:], maskb[:].rearrange("p t e -> p (t e)"),
                          start=True, stop=False)
                pe.matmul(PS[:, OBANK, 64:64 + NT * NE], onesb[:], beforeb[:].rearrange("p t e -> p (t e)"),
                          start=False, stop=True).then_inc(rank_ps, 1)

            def turn_h1(n):
                pe.wait_ge(h1_ready, n + 1)
                for c in range(2):
                    for t in range(NT):
                        mm = pe.transpose(PS[:, QBANKS[c], bass.ts(t, P)], h1[:, t, bass.ts(c, P)], ident[:])
                    mm.then_inc(hT_ps, 1)

            def turn_h2(tiles, last):
                for c in range(2):
                    for t in tiles:
                        mm = pe.transpose(PS[:, 1 + c, bass.ts(t, P)], h2[:, t, bass.ts(c, P)], ident[:])
                    if last:
                        mm.then_inc(h2T_ps, 1)

            def ffn(b, m, banks):
                off, w = MT[m]
                wide = w + (NE if m == 2 else 0)
                for c in range(2):
                    if m == 2:
                        pe.wait_ge(h2T_ready, 2 * b + c + 1)
                    pe.matmul(PS[0:wide, banks[0], :], sg_sb[:, c, off:off + wide], h2T[:, c, :],
                              start=c == 0, stop=c == 1)
                    mm = pe.matmul(PS[0:w, banks[1], :], su_sb[:, c, off:off + w], h2T[:, c, :],
                                   start=c == 0, stop=c == 1)
                mm.then_inc(gu_ps, 1)

            def output(tiles, bank):
                for k, t in enumerate(tiles):
                    for p in range(NPAIR):
                        mm = pe.matmul(PS[:, bank, k * H:(k + 1) * H], oT[:, p, bass.ts(t, P)], wvo[:, p, :],
                                       start=p == 0, stop=p == NPAIR - 1)
                mm.then_inc(attn_ps, 1)

            def middle(b, n, post, pre):
                if pre:
                    pe.wait_ge(hT_ready, 2 * (n + 1))
                    for k, t in enumerate(KV_ORDER):
                        if post:
                            pe.wait_ge(*((pT_act, 4 * n * NPAIR - 1), (pT_dve, 2 * n * NPAIR - 1),
                                         (pT_act, 4 * n * NPAIR), (pT_dve, 2 * n * NPAIR))[k])
                        for c in range(2):
                            mm = pe.matmul(PS[:, t, 0:FW], hT[:, c, bass.ts(t, P)], wkva_sb[:, c, :],
                                           start=c == 0, stop=c == 1)
                        mm.then_inc(kv_ps, 1)
                if post:
                    values(b * NPAIR + NPAIR - 1)
                    pe.wait_ge(oT_ready, (b + 1) * NPAIR + 1)
                    output((0, 1), 4)
                if pre:
                    pe.wait_ge(k_ready, n + 1)
                    for bank, src in ((6, kmat[:]), (7, qn[:, :, 0:P]), (0, qn[:, :, P:2 * P])):
                        for t in range(NT):
                            mm = pe.transpose(PS[:, bank, bass.ts(t, P)], src[:, t, :], ident[:])
                        mm.then_inc(kq_ps, 1)
                if post:
                    output((2,), 5)
                    output((3,), 3)
                if pre:
                    pe.wait_ge(kql_ready, 3 * (n + 1))
                    q_project(0, n * NPAIR, range(NT))
                if post:
                    pe.wait_ge(n2_ready, 2 * b + 1)
                    turn_h2((0, 1, 2), False)
                    pe.wait_ge(n2_ready, 2 * b + 2)
                    turn_h2((3,), True)
                    ffn(b, 2, (3, 4))
                if pre:
                    q_turn(n * NPAIR)
                if post:
                    ffn(b, 0, (5, 0))
                    wait_alone(pe, lg_ready, b + 1)
                    for t in range(NT):
                        mm = pe.transpose(PS[:, 1, bass.ts(t, NE)], lgT[:, bass.ts(t, P)], ident[0:NE, 0:NE])
                    mm.then_inc(lgT_ps, 1)
                    pe.wait_ge(mid_ready, 3 * b + 1)
                    ffn(b, 1, (3, 4))
                    pe.wait_ge(mid_ready, 3 * b + 2)
                    pe.wait_ge(ls_ready, b + 1)
                if not pre:
                    ranks(b)
                if pre:
                    scores(n * NPAIR, True, (0, 1, 2))
                if post:
                    pe.wait_ge(mid_ready, 3 * b + 3)
                    for t in range(NT):
                        for k, (off, w) in enumerate(MT):
                            mm = pe.matmul(PS[:, 3 + t // 2, (t % 2) * H:(t % 2 + 1) * H],
                                           midT[0:w, k, bass.ts(t, P)], sd_sb[0:w, k, :], start=k == 0, stop=k == 2)
                        if t % 2:
                            mm.then_inc(down_ps, 1)

            def pairs(b, more):
                with pe.Fori(1, NPAIR - 1) as p:
                    step(p, b, False, False, more)
                step(NPAIR - 1, b, False, True, more)

            turn_h1(0)
            middle(0, 0, False, True)
            step(0, 0, True, False, False)
            with pe.Fori(0, LAST) as b:
                pairs(b, True)
                middle(b, b + 1, True, True)
                step(0, b + 1, True, False, True)
            pairs(LAST, False)
            middle(LAST, None, True, False)
            pe.wait_ge(gated_ready, B)
            pe.wait_ge(slot_ready, B)

            def turn_rows(e):
                q = e % 2
                pe.wait_ge(xg_landed[e % RX], 32 * (e // RX + 1))
                for c in range(2):
                    mm = pe.transpose(PS[:, q, bass.ts(c, P)], xg[:, e % RX, bass.ts(c, P)], ident[:])
                mm.then_inc(xgT_ps, 1)

            def gate_up(e):
                r, q = e % RE, e % 2
                pe.wait_ge(xgT_ready, e + 1)
                pe.wait_ge(ew_landed[r], 64 * (e // RE + 1))
                for c in range(2):
                    mm = pe.matmul(PS[:, 2 + q, 0:2 * IM], xgT[:, q, c, :], ew_g(r, c), start=c == 0, stop=c == 1)
                mm.then_inc(egu_ps, 1)

            def turn_inner(e):
                q = e % 2
                pe.wait_ge(emid_ready, e + 1)
                pe.transpose(PS[:, 4 + q, 0:P], emid[:, q, 0:P], ident[:])
                pe.transpose(PS[0:IR, 4 + q, P:2 * P], emid[:, q, P:IM], ident[:]).then_inc(emT_ps, 1)

            def down(e):
                r, q = e % RE, e % 2
                pe.wait_ge(emT_ready, e + 1)
                if e >= 2:
                    pe.wait_ge(ey_ready, e - 1)
                pe.matmul(PS[:, 6 + q, 0:H], emT[:, q, 0, :], ew_d(r, 0, P), start=True, stop=False)
                pe.matmul(PS[:, 6 + q, 0:H], emT[0:IR, q, 1, :], ew_d(r, 1, IR), start=False,
                          stop=True).then_inc(ey_ps, 1)

            turn_rows(0)
            for e in range(NE):
                gate_up(e)
                if e:
                    down(e - 1)
                if e + 1 < NE:
                    turn_rows(e + 1)
                turn_inner(e)
            down(NE - 1)

        @block.scalar
        def _(act):
            act.sem_inc(oT_ready, 1)
            act.sem_inc(h2_out, 16)
            act.sem_inc(base_out, 16)
            act.sem_inc(base_ready, 1)
            act.sem_inc(entries_free, 1)
            act.wait_ge(mod_in, 64)
            act.activation(cth[:], cT_sb[:], ACT.Tanh, scale=0.5).then_inc(c_tanh, 1)

            def nope_copy(g):
                act.wait_ge(q_ps, 2 * g + 2)
                act.activation(qtok[:, :, 0:KL], qps[:, :, 0:KL], ACT.Copy).then_inc(nope_ready, 1)

            def q_high(g, h):
                act.wait_ge(qT_ps, 2 * g + h + 1)
                act.activation(qTh[:, h, :], PS[:, QBANKS[h], :], ACT.Copy).then_inc(qTh_ready, 1)

            def exps(g, units):
                for u in units:
                    act.wait_ge(max_ready, g * NU + u + 1)
                    act.activation(probs[:, UO[u]:UO[u] + UW[u]], PS[:, SBANK[u], 0:UW[u]], ACT.Exp,
                                   bias=nmax[:, u:u + 1], accum_out=psums[:, u:u + 1]).then_inc(exp_ready, 1)

            def group_out(g, k):
                units, bank = GROUPS[k]
                act.wait_ge(pT_ps, g * len(GROUPS) + k + 1)
                col = 0
                for u in units:
                    h, i = UNITS[u]
                    cp = act.activation(pT[:, h, 0:i + 1, bass.ts(i, P)],
                                        PS[:, bank, col:col + UW[u]].rearrange("p (j q) -> p j q", q=P), ACT.Copy)
                    col += UW[u]
                cp.then_inc(pT_act, 1)

            def sums_out(g):
                act.wait_ge(r_ps, g + 1)
                act.wait_ge(oT_ready, g + 1)
                act.activation(rb[:], PS[:, RBANK, :], ACT.Copy).then_inc(rb_ready, 1)

            def step(p, b, last, more):
                g = b * NPAIR + p
                exps(g, (3, 4))
                if not last:
                    nope_copy(g + 1)
                exps(g, (5, 6, 7))
                group_out(g, 0)
                group_out(g, 1)
                if not last:
                    q_high(g + 1, 0)
                    q_high(g + 1, 1)
                elif more:
                    turned_h1(b + 1)
                group_out(g, 2)
                group_out(g, 4)
                sums_out(g)
                if not last:
                    exps(g + 1, (0, 1, 2))

            def pairs(b, more):
                with act.Fori(1, NPAIR - 1) as p:
                    step(p, b, False, more)
                step(NPAIR - 1, b, True, more)

            def tanh_gate(b, k, m, bank):
                w = MT[m][1]
                act.wait_ge(gu_ps, 3 * b + k + 1)
                if k:
                    act.wait_ge(mid_ready, 3 * b + k)
                act.activation(th[0:w, :], PS[0:w, bank, :], ACT.Tanh, scale=0.5).then_inc(th_ready, 1)

            def turned_h1(n):
                act.wait_ge(mod1_ready, n + 1)
                for c in range(2):
                    act.wait_ge(hT_ps, 2 * n + c + 1)
                    act.activation(hT[:, c, :], PS[:, QBANKS[c], :], ACT.Identity, scale=mod1[:, 2 + c:3 + c],
                                   bias=mod1[:, c:c + 1]).then_inc(hT_ready, 1)

            def turned_h2(b):
                act.wait_ge(mod2_ready, b + 1)
                for c in range(2):
                    act.wait_ge(h2T_ps, 2 * b + c + 1)
                    act.activation(h2T[:, c, :], PS[:, 1 + c, :], ACT.Identity, scale=mod2[:, 2 + c:3 + c],
                                   bias=mod2[:, c:c + 1]).then_inc(h2T_ready, 1)

            def middle(b, n, post, pre):
                if pre:
                    for k, t in enumerate(KV_ORDER):
                        act.wait_ge(kv_ps, NT * n + k + 1)
                        act.activation(sq[:], PS[:, t, 0:QL], ACT.Square, scale=QL ** -0.5,
                                       accum_out=ssq[:, 0, t:t + 1]).then_inc(ssq_ready, 1)
                        act.wait_ge(ssq_ready, 2 * (NT * n + k) + 1)
                        act.activation(sq[:, 0:KL], PS[:, t, QL:QL + KL], ACT.Square, scale=KL ** -0.5,
                                       accum_out=ssq[:, 1, t:t + 1]).then_inc(ssq_ready, 1)
                        act.wait_ge(ssq_ready, 2 * (NT * n + k) + 2)
                    for k, (dst, bank) in enumerate([(kTh, 6), (ql0h, 7)]):
                        act.wait_ge(kq_ps, 3 * n + k + 1)
                        act.activation(dst[:], PS[:, bank, :], ACT.Copy).then_inc(kqh_ready, 1)
                    act.wait_ge(kq_ps, 3 * n + 3)
                    act.activation(ql1s[0:QR, :], PS[0:QR, 0, :], ACT.Copy).then_inc(kqh_ready, 1)
                    act.activation(ql1t[QR:P, :], PS[QR:P, 0, :], ACT.Copy).then_inc(kqh_ready, 1)
                    nope_copy(n * NPAIR)
                if post:
                    turned_h2(b)
                    tanh_gate(b, 0, 2, 3)
                    w = MT[2][1]
                    act.activation(lgT[:], PS[w:w + NE, 3, :], ACT.Copy).then_inc(lg_ready, 1)
                if pre:
                    q_high(n * NPAIR, 0)
                    q_high(n * NPAIR, 1)
                if post:
                    tanh_gate(b, 1, 0, 5)
                    act.wait_ge(ls_ready, b + 1)
                    act.activation(ex[:], ls[:], ACT.Exp).then_inc(ex_ready, 1)
                    tanh_gate(b, 2, 1, 3)
                if pre:
                    exps(n * NPAIR, (0, 1, 2))

            turned_h1(0)
            middle(0, 0, False, True)
            step(0, 0, False, False)
            with act.Fori(0, LAST) as b:
                pairs(b, True)
                middle(b, b + 1, True, True)
                step(0, b + 1, False, True)
            pairs(LAST, False)
            middle(LAST, None, True, False)

            def load(e):
                r = e % RE
                if e >= RE:
                    act.wait_ge(ey_ps, e - RE + 1)
                elif e == 0:
                    act.wait_ge(o_ps, B * NPAIR)
                elif e == 5:
                    act.wait_ge(attn_ps, 3 * B)
                act.dma_start(ering[r][:, 0:4 * IM].rearrange("p (c n) -> p c n", c=2)[:, :, 0:IM],
                              egate[e].rearrange("(c p) n -> p c n", p=P)).then_inc(ew_landed[r], 16)
                act.dma_start(ering[r][:, 0:4 * IM].rearrange("p (c n) -> p c n", c=2)[:, :, IM:2 * IM],
                              eup[e].rearrange("(c p) n -> p c n", p=P)).then_inc(ew_landed[r], 16)
                act.dma_start(ew_d(r, 0, P), edown[e, 0:P, :]).then_inc(ew_landed[r], 16)
                act.dma_start(ew_d(r, 1, IR), edown[e, P:IM, :]).then_inc(ew_landed[r], 16)

            for e in range(RE):
                load(e)

            def rows_out(e):
                act.wait_ge(xgT_ps, e + 1)
                act.activation(xgT[:, e % 2, :, :].rearrange("p c s -> p (c s)"), PS[:, e % 2, 0:2 * P],
                               ACT.Copy).then_inc(xgT_ready, 1)

            rows_out(0)
            for e in range(NE):
                q = e % 2
                act.wait_ge(egu_ps, e + 1)
                if e:
                    act.wait_ge(emid_ready, e)
                act.activation(eth[:], PS[:, 2 + q, 0:IM], ACT.Tanh, scale=0.5).then_inc(eth_ready, 1)
                if e + 1 < NE:
                    rows_out(e + 1)
                act.wait_ge(emT_ps, e + 1)
                act.activation(emT[:, q, 0, :], PS[:, 4 + q, 0:P], ACT.Copy)
                act.activation(emT[0:IR, q, 1, :], PS[0:IR, 4 + q, P:2 * P], ACT.Copy).then_inc(emT_ready, 1)
                if e >= 1 and e - 1 + RE < NE:
                    load(e - 1 + RE)

        @block.vector
        def _(dve):
            ch = Chain(dve, dve_chain)
            dve.wait_ge(c_tanh, 1)
            ch.step(dve.tensor_scalar(cth[:], cth[:], 1.0, 0.5, ALU.add, ALU.mult))
            dve.tensor_tensor(csl[:], cth[:], cT_sb[:], ALU.mult).then_inc(c_ready, 1)
            dve.wait_ge(mod_ps, 1)
            ch.step(dve.tensor_copy(midT[0:B].rearrange("b a s -> b (a s)"),
                                    PS[0:B, 0:3, :].rearrange("b a n -> b (a n)")))
            for k, i in enumerate((GA, GB)):
                ch.step(dve.tensor_scalar(sgn[:, 0, :], mod_sb[:, i, :], 0.0, 2.0, ALU.is_ge, ALU.mult))
                ch.step(dve.tensor_scalar(sgn[:, 0, :], sgn[:, 0, :], -1.0, 0.5 if i == GB else 1.0, ALU.add, ALU.mult))
                ch.step(dve.scalar_tensor_tensor(out=sgn[:, 1, :], in0=mod_sb[:, i, :], scalar=-1.0,
                                                 in1=mod_sb[:, i, :], op0=ALU.mult, op1=ALU.max))
                ch.step(dve.scalar_tensor_tensor(out=mod_sb[:, i, :], in0=sgn[:, 1, :], scalar=0.25,
                                                 in1=sgn[:, 0, :], op0=ALU.max, op1=ALU.mult))
            ch.step(dve.tensor_scalar(mod_sb[:, CA, :], mod_sb[:, CA, :], 1.0, None, ALU.add))
            dve.tensor_scalar(mod_sb[:, CB, :], mod_sb[:, CB, :], 1.0, None, ALU.add).then_inc(mod_ready, 1)
            dve.wait_ge(modT_ps, 1)
            ch.step(dve.tensor_copy(modT[:].rearrange("p k b -> p (k b)"), PS[:, 7, 0:8 * B]))
            dve.wait_ge(w_in, W_LOADS * 16)
            ch.step(dve.tensor_scalar(qg_sb[:, 0:1], qg_sb[:, 0:1], SCALE, None, ALU.mult))
            ch.step(dve.tensor_scalar(qg_sb[:, 1:2], qg_sb[:, 1:2], SCALE, None, ALU.mult))
            dve.wait_ge(wabs_ps, 1)
            for k, (high, low, n, pe_st) in enumerate([(wq0h, wq0l, P, pe0_st), (wq1hh, wq1l, QR, pe1_st)]):
                heads = lambda w, lo, hi: w[:].rearrange("p (h c) -> p h c", c=P)[:, :, lo:hi]
                lat = PS[:, 3 + 2 * k:5 + 2 * k, :].rearrange("p a (c d) -> p (a c) d", d=KL)
                for src, lo, hi in ((lat, 0, KL), (pe_st, KL, P)):
                    ch.step(dve.tensor_scalar(heads(high, lo, hi), src, qg_sb[:, k:k + 1], None, ALU.mult))
                    ch.link(dve.scalar_tensor_tensor(out=heads(low, lo, hi), in0=src[0:n], scalar=qg_sb[0:n, k:k + 1],
                                                     in1=heads(high, lo, hi)[0:n].bitcast(F32),
                                                     op0=ALU.mult, op1=ALU.subtract))
            ch.wait()
            dve.memset(prec[:], 0.0).then_inc(wabs_ready, 1)
            dve.wait_ge(wabs_ps, 2)
            dve.tensor_copy(wvo[:].rearrange("p a n -> p (a n)"),
                            PS[:, 0:4, :].rearrange("p a n -> p (a n)")).then_inc(wabs_ready, 1)

            def statistics(src, stats, mean_var, var_ready, tiles):
                for t in tiles:
                    ch.link(dve.bn_stats(stats[:, t, :], src[:, t, :]))
                wait_alone(dve, ch.sem, ch.base + ch.n)
                for t in tiles:
                    dve.bn_aggr(mean_var[:, t, :], stats[:, t, :]).then_inc(var_ready, 1)

            def normed(src, dst, mean_var, rs, tiles, ready):
                for t in tiles:
                    last = dve.tensor_scalar(dst[:, t, :], src[:, t, :], mean_var[:, t, 0:1], rs[:, t:t + 1],
                                             ALU.subtract, ALU.mult)
                last.then_inc(ready, 1)

            def h1_statistics(n):
                dve.wait_ge(x_landed, 16 * (n + 1))
                dve.tensor_copy(mod1[:], modT[:, 0:4, bass.ds(n, 1)].rearrange("p k b -> p (k b)")).then_inc(mod1_ready, 1)
                statistics(x_in, st, mv, var1_ready, range(NT))

            def h1_normed(n):
                dve.wait_ge(var1_ready, NT * (n + 1))
                dve.wait_ge(rs1_ready, n + 1)
                normed(x_in, h1, mv, rstd, range(NT), h1_ready)

            HALF = DR // 2

            def rope_parts(raw, t1, t2, heads):
                def tab(a, lo, hi):
                    return a[:, :, lo:hi].unsqueeze(2).to_broadcast([P, NT, heads, hi - lo])

                def v(a, lo, hi):
                    return a[:, :, lo:hi].rearrange("p (t h) d -> p t h d", h=heads)
                return [lambda: dve.tensor_tensor(v(t1, 0, DR), v(raw, 0, DR), tab(cos_sb, 0, DR), ALU.mult),
                        lambda: dve.tensor_tensor(v(t2, 0, HALF), v(raw, HALF, DR), tab(sin_sb, 0, HALF), ALU.mult),
                        lambda: dve.tensor_tensor(v(t2, HALF, DR), v(raw, 0, HALF), tab(sin_sb, HALF, DR), ALU.mult)]

            def q_rope(g):
                parts = rope_parts(qps[:, :, KL:P], qr1, qr2, 2)

                def first():
                    dve.wait_ge(nope_ready, g + 1)
                    ch.link(parts[0]())

                def last():
                    ch.wait()
                    dve.tensor_tensor(qtok[:, :, KL:P], qr1[:], qr2[:], ALU.add).then_inc(rope_ready, 1)
                return [first, lambda: ch.link(parts[1]()), lambda: ch.link(parts[2]()), last]

            def maxima(g, units):
                for u in units:
                    dve.wait_ge(s_ps, g * NU + u + 1)
                    dve.tensor_reduce(nmax[:, u:u + 1], PS[:, SBANK[u], 0:UW[u]], AX.X, ALU.max,
                                      negate=True).then_inc(max_ready, 1)

            def invert_sums(g):
                dve.wait_ge(exp_ready, g * NU + NU)
                ch.step(dve.reciprocal(prec[:], psums[:]))
                dve.tensor_copy(wide[:].rearrange("p (t h d) -> p h t d", t=NT, h=2),
                                prec[:].rearrange("p (h t) -> p h t", h=2).unsqueeze(3).to_broadcast(
                                    [P, 2, NT, KL])).then_inc(wide_ready, 1)

            def group_out(g, k):
                units, bank = GROUPS[k]
                dve.wait_ge(pT_ps, g * len(GROUPS) + k + 1)
                col = 0
                for u in units:
                    h, i = UNITS[u]
                    cp = dve.tensor_copy(pT[:, h, 0:i + 1, bass.ts(i, P)],
                                         PS[:, bank, col:col + UW[u]].rearrange("p (j q) -> p j q", q=P))
                    col += UW[u]
                cp.then_inc(pT_dve, 1)

            def values_out(p, g):
                dve.wait_ge(o_ps, g + 1)
                dve.wait_ge(rb_ready, g + 1)
                dve.tensor_tensor(oT[:, p, :], PS[:, OBANK, :], rb[:], ALU.mult).then_inc(oT_ready, 1)

            def q_low(g, h):
                dve.wait_ge(qTh_ready, 2 * g + h + 1)
                dve.tensor_tensor(qTl[:, h, :], PS[:, QBANKS[h], :], qTh[:, h, :].bitcast(F32),
                                  ALU.subtract).then_inc(qTl_ready, 1)

            def step(p, b, first, last, more):
                g = b * NPAIR + p
                maxima(g, (3, 4))
                if last and more:
                    h1_statistics(b + 1)
                maxima(g, (5, 6, 7))
                if not last:
                    for part in q_rope(g + 1):
                        part()
                elif more:
                    h1_normed(b + 1)
                invert_sums(g)
                if not first:
                    values_out(p - 1, g - 1)
                elif more:
                    slots(b - 1)
                if not last:
                    q_low(g + 1, 0)
                    q_low(g + 1, 1)
                group_out(g, 3)
                group_out(g, 5)
                if not last:
                    maxima(g + 1, (0, 1, 2))

            def silu_mid(b, k, m, banks):
                w = MT[m][1]
                dve.wait_ge(th_ready, 3 * b + k + 1)
                ch.step(dve.scalar_tensor_tensor(out=mid[0:w, :], in0=th[0:w, :], scalar=1.0,
                                                 in1=PS[0:w, banks[0], :], op0=ALU.add, op1=ALU.mult))
                dve.tensor_tensor(midT[0:w, m, :], mid[0:w, :], PS[0:w, banks[1], :], ALU.mult).then_inc(mid_ready, 1)

            def over_e(a):
                return a.unsqueeze(2).to_broadcast([P, NT, NE])

            def router_scores(b):
                dve.wait_ge(lgT_ps, b + 1)
                lg = PS[:, 1, 0:NT * NE].rearrange("p (t e) -> p t e", e=NE)
                ch.step(dve.tensor_reduce(lmax[:], lg, AX.X, ALU.max))
                dve.tensor_tensor(ls[:], lg, over_e(lmax[:]), ALU.subtract).then_inc(ls_ready, 1)

            def route(b):
                dve.wait_ge(ex_ready, b + 1)
                ch.step(dve.tensor_reduce(esum[:], ex[:], AX.X, ALU.add))
                ch.step(dve.reciprocal(esum[:], esum[:]))
                ch.link(dve.tensor_tensor(score[:], ex[:], over_e(esum[:]), ALU.mult))
                wait_alone(dve, ch.sem, ch.base + ch.n)
                for t in range(NT):
                    ch.link(dve.max(top[:, t, :], score[:, t, :]))
                wait_alone(dve, ch.sem, ch.base + ch.n)
                for t in range(NT):
                    ch.link(dve.max_index(topi[:, t, :], top[:, t, :], score[:, t, :]))
                ch.step(dve.tensor_reduce(tsum[:], top[:, :, 0:TOPK], AX.X, ALU.add))
                ch.step(dve.tensor_scalar(tsum[:], tsum[:], 1e-20, None, ALU.add))
                ch.step(dve.reciprocal(tsum[:], tsum[:]))
                ch.step(dve.tensor_copy(topf[:], topi[:, :, 0:TOPK]))
                ent = entry[:].rearrange("p (t k) c -> p t k c", k=TOPK)

                def over_k(a):
                    return a.unsqueeze(2).to_broadcast([P, NT, TOPK])
                dve.wait_ge(entries_free, b + 1)
                ch.link(dve.tensor_tensor(ent[:, :, :, 1], top[:, :, 0:TOPK], over_k(tsum[:]), ALU.mult))
                ch.link(dve.tensor_copy(ent[:, :, :, 0], over_k(tid[:])))
                ch.step(dve.tensor_tensor(oh[:].rearrange("p t k e -> p (t k) e"),
                                          eid[:].unsqueeze(1).to_broadcast([P, NT * TOPK, NE]),
                                          topf[:].rearrange("p t k -> p (t k)").unsqueeze(2).to_broadcast(
                                              [P, NT * TOPK, NE]), ALU.is_equal))
                ch.step(dve.tensor_scalar(tid[:], tid[:], float(S), None, ALU.add))
                ch.step(dve.tensor_reduce(mask[:], oh[:].rearrange("p t k e -> p t e k"), AX.X, ALU.add))
                ch.link(dve.tensor_copy(maskb[:], mask[:]))
                for t in range(NT):
                    ch.step(dve.tensor_tensor(before[:, t + 1, :], before[:, t, :], mask[:, t, :], ALU.add))
                ch.step(dve.tensor_copy(beforeb[:], before[:, 0:NT, :]))
                dve.tensor_copy(before[:, 0, :], before[:, NT, :]).then_inc(mask_ready, 1)

            def slots(b):
                dve.wait_ge(rank_ps, b + 1)
                rank = PS[:, OBANK, 64:64 + NT * NE].rearrange("p (t e) -> p t e", e=NE)
                ch.link(dve.tensor_scalar(over[:], rank, float(CAP), FAR, ALU.is_ge, ALU.mult))
                ch.step(dve.tensor_tensor(slot_e[:], rank, ebase[:].unsqueeze(1).to_broadcast([P, NT, NE]), ALU.add))
                ch.step(dve.tensor_tensor(slot_e[:], slot_e[:], over[:], ALU.add))
                ch.step(dve.tensor_tensor(ohs[:], oh[:], slot_e[:].unsqueeze(2).to_broadcast([P, NT, TOPK, NE]),
                                          ALU.mult))
                ch.step(dve.tensor_reduce(slotf[:], ohs[:].rearrange("p t k e -> p (t k) e"), AX.X, ALU.add))
                dve.tensor_copy(slot[:], slotf[:]).then_inc(slot_ready, 1)

            def gate_of(i, tiles):
                return modb[:, i, :].unsqueeze(1).to_broadcast([P, tiles, H])

            def residual(b, k, lo, hi, bank):
                dve.wait_ge(attn_ps, 3 * b + k + 1)
                ch.step(dve.tensor_tensor(tmp[:, lo:hi, :], PS[:, bank, 0:(hi - lo) * H].rearrange(
                    "p (c n) -> p c n", n=H), gate_of(0, hi - lo), ALU.mult))
                dve.tensor_tensor(x1[:, lo:hi, :], tmp[:, lo:hi, :], x_res[:, lo:hi, :], ALU.add).then_inc(x1_ready, 1)
                dve.wait_ge(x1_ready, 3 * b + k + 1)
                for t in range(lo, hi):
                    ch.link(dve.bn_stats(st2[:, t, :], x1[:, t, :]))

            def variances(tiles):
                wait_alone(dve, ch.sem, ch.base + ch.n)
                for t in tiles:
                    dve.bn_aggr(mv2[:, t, :], st2[:, t, :]).then_inc(var2_ready, 1)

            def middle(b, n, post, pre):
                if post:
                    values_out(NPAIR - 1, b * NPAIR + NPAIR - 1)
                if pre:
                    dve.wait_ge(rsq_ready, n + 1)
                    for t in range(NT):
                        ch.link(dve.tensor_scalar(qn[:, t, 0:QL], PS[:, t, 0:QL], ssq[:, 0, t:t + 1], None, ALU.mult))
                        ch.link(dve.tensor_scalar(qn[:, t, QL:], PS[:, t, P:QL], ssq[:, 0, t:t + 1], None, ALU.mult))
                    for t in range(NT):
                        ch.link(dve.scalar_tensor_tensor(out=kmat[:, t, 0:KL], in0=PS[:, t, QL:QL + KL],
                                                         scalar=ssq[:, 1, t:t + 1], in1=kg_sb[:],
                                                         op0=ALU.mult, op1=ALU.mult))
                    for part in rope_parts(PS[:, 0:4, QL + KL:FW], kr1, kr2, 1):
                        ch.link(part())
                    ch.wait()
                    dve.tensor_tensor(kmat[:, :, KL:], kr1[:], kr2[:], ALU.add).then_inc(k_ready, 1)
                if post:
                    dve.tensor_copy(mod2[:], modT[:, 4:8, bass.ds(b, 1)].rearrange("p k b -> p (k b)")
                                    ).then_inc(mod2_ready, 1)
                    dve.wait_ge(modb_landed, 16 * (b + 1))
                    dve.wait_ge(res_ready, b + 1)
                    dve.wait_ge(base_ready, b + 1)
                    residual(b, 0, 0, 2, 4)
                if pre:
                    for k, (low, high, bank, lo) in enumerate([(kTl, kTh, 6, 0), (ql0l, ql0h, 7, 0),
                                                               (ql1s, ql1t, 0, QR)]):
                        dve.wait_ge(kqh_ready, 4 * n + (k + 1 if k < 2 else 4))
                        dve.tensor_tensor(low[lo:P, :], PS[lo:P, bank, :], high[lo:P, :].bitcast(F32),
                                          ALU.subtract).then_inc(kql_ready, 1)
                if post:
                    residual(b, 1, 2, 3, 5)
                    variances(range(3))
                    residual(b, 2, 3, 4, 3)
                    variances(range(3, 4))
                    dve.wait_ge(h2_out, 16 * b + 16)
                    dve.wait_ge(rs2_ready, 2 * b + 1)
                    normed(x1, h2, mv2, rstd2, range(3), n2_ready)
                    dve.wait_ge(rs2_ready, 2 * b + 2)
                    normed(x1, h2, mv2, rstd2, range(3, 4), n2_ready)
                if pre:
                    for part in q_rope(n * NPAIR):
                        part()
                if post:
                    silu_mid(b, 0, 2, (3, 4))
                if pre:
                    q_low(n * NPAIR, 0)
                    q_low(n * NPAIR, 1)
                if post:
                    router_scores(b)
                    if not pre:
                        route(b)
                    silu_mid(b, 1, 0, (5, 0))
                    if not pre:
                        slots(b)
                    silu_mid(b, 2, 1, (3, 4))
                if pre:
                    maxima(n * NPAIR, (0, 1, 2))
                    if post:
                        route(b)
                if post:
                    dve.wait_ge(down_ps, 2 * (b + 1))
                    dve.tensor_tensor(tmp[:], PS[:, 3:5, :].rearrange("p a (c n) -> p (a c) n", n=H),
                                      gate_of(3, NT), ALU.mult).then_inc(gated_ready, 1)

            def pairs(b, base, more):
                with dve.Fori(1, NPAIR - 1) as p:
                    ch.base, ch.n = base + (p - 1) * CHAIN_PAIR, 0
                    step(p, b, False, False, more)
                    assert ch.n == CHAIN_PAIR, ch.n
                ch.base, ch.n = base + (NPAIR - 2) * CHAIN_PAIR, 0
                step(NPAIR - 1, b, False, True, more)

            dve.wait_ge(const_ready, 3)
            h1_statistics(0)
            h1_normed(0)
            middle(0, 0, False, True)
            step(0, 0, True, False, False)
            assert ch.n == CHAIN_PROLOGUE, ch.n
            with dve.Fori(0, LAST) as b:
                pairs(b, CHAIN_PROLOGUE + b * CHAIN_BATCH, True)
                middle(b, b + 1, True, True)
                step(0, b + 1, True, False, True)
                assert (NPAIR - 2) * CHAIN_PAIR + ch.n == CHAIN_BATCH, (NPAIR - 2) * CHAIN_PAIR + ch.n
            pairs(LAST, CHAIN_PROLOGUE + LAST * CHAIN_BATCH, False)
            middle(LAST, None, True, False)

            dve.wait_ge(tab_landed, 16)
            ch.link(dve.tensor_copy(toku[:], tab[:, :, 0]))
            ch.step(dve.tensor_scalar(bidf[:], tab[:, :, 0], float(T - 1), None, ALU.min))
            ch.step(dve.tensor_copy(bidi[:], bidf[:]))
            dve.tensor_scalar(bid[:], bidi[:], 9, None, ALU.arith_shift_right).then_inc(tok_ready, 1)

            def weigh(e):
                q, r = e % 2, e % RX
                dve.wait_ge(ey_ps, e + 1)
                dve.wait_ge(xg_landed[r], 32 * (e // RX + 1))
                if e >= RX:
                    dve.wait_ge(added, 16 * (e - RX + 1))
                dve.scalar_tensor_tensor(out=ey[:, r, :], in0=PS[:, 6 + q, 0:H], scalar=tab[:, e, 1:2],
                                         in1=gbg[:, r, :], op0=ALU.mult, op1=ALU.mult).then_inc(ey_ready, 1)

            for e in range(NE):
                q = e % 2
                dve.wait_ge(eth_ready, e + 1)
                if e >= 2:
                    dve.wait_ge(emT_ps, e - 1)
                ch.step(dve.scalar_tensor_tensor(out=eth[:], in0=eth[:], scalar=1.0, in1=PS[:, 2 + q, 0:IM],
                                                 op0=ALU.add, op1=ALU.mult))
                dve.tensor_tensor(emid[:, q, :], eth[:], PS[:, 2 + q, IM:2 * IM], ALU.mult).then_inc(emid_ready, 1)
                if e:
                    weigh(e - 1)
            weigh(NE - 1)


def _rope_tables():
    inv = (np.float32(1.0) / np.float32(10000.0) ** (np.arange(0, DR, 2, dtype=np.float32) / np.float32(DR))).astype(np.float32)
    ang = np.arange(S, dtype=np.float32)[:, None] * inv
    c, s = np.cos(ang).astype(np.float32), np.sin(ang).astype(np.float32)
    return np.concatenate([c, c], -1), np.concatenate([-s, s], -1)


def kernel(**inputs):
    import concourse.bacc as bacc
    from concourse.bass_utils import run_bass_kernel_spmd

    a = {k: np.asarray(v) for k, v in inputs.items()}
    wqb = a["L0_attn_w_qb"].reshape(QL, NH, DN + DR)
    wkvb = a["L0_attn_w_kvb"].reshape(KL, NH, DN + DV)
    cos, sin = _rope_tables()
    arrays = {
        "x": a["L0_attn_hidden"],
        "wkva": a["L0_attn_w_kv_a"],
        "wqnT": wqb[:, :, :DN].transpose(1, 2, 0),
        "wqpe": wqb[:, :, DN:],
        "wkT": wkvb[:, :, :DN].transpose(2, 1, 0),
        "wvT": wkvb[:, :, DN:].transpose(2, 1, 0),
        "wo": a["L0_attn_w_o"],
        "qgam": a["L0_attn_q_a_gamma"],
        "kgam": a["L0_attn_kv_a_gamma"],
        "sgate": np.concatenate([a["L0_ffn_sw_gate"], a["L0_ffn_gate_w"].T], axis=1),
        "sup": a["L0_ffn_sw_up"],
        "sdown": a["L0_ffn_sw_down"],
        "egate": a["L0_ffn_w_gate"],
        "eup": a["L0_ffn_w_up"],
        "edown": a["L0_ffn_w_down"],
        "cT": a["L0_c"].T,
        "wmod": a["L0_wmod"],
        "cos": cos,
        "sin": sin,
    }
    nc = bacc.Bacc("TRN2", target_bir_lowering=False, num_devices=1)
    feed, args = {}, []
    for name, v in arrays.items():
        v = np.ascontiguousarray(v)
        feed[f"in_{name}"] = v
        args.append(nc.dram_tensor(f"in_{name}", v.shape, mybir.dt.from_np(v.dtype), kind="ExternalInput").ap())
    out = nc.dram_tensor("out_0", (B, S, H), F32, kind="ExternalOutput").ap()
    adaln_block(nc, *args, out)
    r = run_bass_kernel_spmd(nc, [feed], core_ids=[0])
    return r.results[0]["out_0"]
```

```python
from contextlib import ExitStack

import numpy as np

import concourse.bass as bass
from concourse import mybir

F32 = mybir.dt.float32
F32R = mybir.dt.float32r
BF16 = mybir.dt.bfloat16
I32 = mybir.dt.int32
U32 = mybir.dt.uint32
ALU = mybir.AluOpType
ACT = mybir.ActivationFunctionType
AX = mybir.AxisListType

P = 128
B, S, H = 8, 512, 256
T = B * S
NT = S // P
LAST = B - 1
NH, DN, DR, DV = 16, 128, 64, 128
QL, KL = 192, 64
QR = QL - P
FW = QL + KL + DR
NPAIR = NH // 2
NE, TOPK, IM, IS, CAP = 16, 4, 176, 352, 128
IR = IM - P
MT = [(0, 128), (128, 128), (256, 96)]
LN_EPS, RMS_EPS = 1e-5, 1e-6
SCALE = 1.0 / float(np.sqrt(DN + DR))
NEG = -1e30
FAR = 1e5
UNITS = [(h, i) for h in range(2) for i in range(NT - 1, -1, -1)]
NU = len(UNITS)
UW = [(i + 1) * P for _, i in UNITS]
UO = [sum(UW[:u]) for u in range(NU)]
SBANK = [0, 1, 2, 0, 1, 2, 0, 1]
GROUPS = [((0,), 3), ((1,), 4), ((2, 3), 2), ((4,), 0), ((5,), 1), ((6, 7), 3)]
RBANK = 4
OBANK, QBANKS = 5, [6, 7]
KV_ORDER = [2, 0, 1, 3]
SA, CA, GA, SB, CB, GB = range(6)

CHAIN_PROLOGUE, CHAIN_PAIR, CHAIN_BATCH = 37, 4, 84


COUNT_STEPS = NT + 2


class Chain:

    def __init__(self, eng, sem):
        self.eng, self.sem, self.base, self.n = eng, sem, 0, 0

    def link(self, ins):
        self.n += 1
        ins.then_inc(self.sem, 1)

    def wait(self):
        self.eng.wait_ge(self.sem, self.base + self.n)

    def step(self, ins):
        self.link(ins)
        self.wait()


def adaln_block(nc, x, wkva, wqnT, wqpe, wkT, wvT, wo, qgam, kgam, sgate, sup, sdown,
                egate, eup, edown, cT, wmod, cos, sin, out):
    xr = x.rearrange("b s h -> (b s) h")
    outr = out.rearrange("b s h -> (b s) h")
    mod_dram = nc.dram_tensor("mod_dram", (B, 4 * H), F32, kind="Internal").ap()
    gb_dram = nc.dram_tensor("gb_dram", (B, H), F32, kind="Internal").ap()
    h2_dram = nc.dram_tensor("h2_dram", (T + P, H), F32, kind="Internal").ap()
    tab_dram = nc.dram_tensor("tab_dram", (NE * CAP, 2), F32, kind="Internal").ap()

    def wait_alone(eng, semaphore, value):
        if not isinstance(value, int):
            value = eng.snap(eng.to_reg(value))
            eng.wait_ge(const_ready, 3)
        eng.wait_ge(semaphore, value)

    def rows(ap, b):
        return ap[bass.ts(b, S), :].rearrange("(t p) h -> p t h", p=P)

    with ExitStack() as ctx:
        def sb(name, shape, dt=F32):
            return ctx.enter_context(nc.sbuf_tensor(name, shape, dt))

        def sem(name):
            return ctx.enter_context(nc.semaphore(name))

        wq0h = sb("wq0h", [P, NH * P], F32R)
        wq0l = sb("wq0l", [P, NH * P], F32R)
        wq1hh = sb("wq1hh", [P, NH * P], F32R)
        wq1l = sb("wq1l", [QR, NH * P], F32R)
        wvo = sb("wvo", [P, NPAIR, H])
        wkva_sb = sb("wkva_sb", [P, 2, FW])
        sg_sb = sb("sg_sb", [P, 2, IS + NE])
        su_sb = sb("su_sb", [P, 2, IS])
        sd_sb = sb("sd_sb", [P, 3, H])
        cos_sb = sb("cos_sb", [P, NT, DR])
        sin_sb = sb("sin_sb", [P, NT, DR])
        qg_sb = sb("qg_sb", [P, 2])
        kg_sb = sb("kg_sb", [P, KL])
        ident = sb("ident", [P, P])
        identb = sb("identb", [P, P], BF16)
        caus = sb("caus", [P, P])
        causb = sb("causb", [P, P], BF16)
        tri = sb("tri", [P, P])
        trib = sb("trib", [P, P], BF16)
        onesb = sb("onesb", [P, P], BF16)
        iota_i = sb("iota_i", [P, 3, NE], I32)
        eid = sb("eid", [P, NE])
        tid = sb("tid", [P, NT])
        tab_init = sb("tab_init", [P, NE, 2])
        zrow = sb("zrow", [P, H])
        mhalf = sb("mhalf", [P, 2 * NT])

        x_in = sb("x_in", [P, NT, H])
        x_res = sb("x_res", [P, NT, H])
        x1 = sb("x1", [P, NT, H])
        h1 = sb("h1", [P, NT, H])
        h2 = sb("h2", [P, NT, H])
        tmp = sb("tmp", [P, NT, H])
        hT = sb("hT", [P, 2, S])
        h2T = sb("h2T", [P, 2, S])
        modT = sb("modT", [P, 8, B])
        mod1 = sb("mod1", [P, 4])
        mod2 = sb("mod2", [P, 4])
        modb = sb("modb", [P, 4, H])
        st = sb("st", [P, NT, 6])
        mv = sb("mv", [P, NT, 2])
        rstd = sb("rstd", [P, NT])
        st2 = sb("st2", [P, NT, 6])
        mv2 = sb("mv2", [P, NT, 2])
        rstd2 = sb("rstd2", [P, NT])
        sq = sb("sq", [P, QL])
        ssq = sb("ssq", [P, 2, NT])
        qn = sb("qn", [P, NT, 2 * P])
        kmat = sb("kmat", [P, NT, KL + DR])
        kr1 = sb("kr1", [P, NT, DR])
        kr2 = sb("kr2", [P, NT, DR])
        kTh = sb("kTh", [P, S], F32R)
        kTl = sb("kTl", [P, S], F32R)
        ql0h = sb("ql0h", [P, S], F32R)
        ql0l = sb("ql0l", [P, S], F32R)
        ql1s = sb("ql1s", [P, S], F32R)
        base = sb("base", [P, NT, H])

        qtok = sb("qtok", [P, 2 * NT, P])
        qr1 = sb("qr1", [P, 2 * NT, DR])
        qr2 = sb("qr2", [P, 2 * NT, DR])
        qTh = sb("qTh", [P, 2, S], F32R)
        qTl = sb("qTl", [P, 2, S], F32R)
        ql1t = qTh[:, 1, :]
        probs = sb("probs", [P, sum(UW)])
        pT = sb("pT", [P, 2, NT, S])
        nmax = sb("nmax", [P, NU])
        psums = sb("psums", [P, NU])
        prec = sb("prec", [P, NU])
        oT = sb("oT", [P, NPAIR, S])

        th = sb("th", [P, S])
        mid = sb("mid", [P, S])
        wide = mid
        rb = th
        midT = sb("midT", [P, 3, S])
        lgT = sb("lgT", [NE, S])
        lmax = sb("lmax", [P, NT])
        ls = sb("ls", [P, NT, NE])
        ex = sb("ex", [P, NT, NE])
        esum = sb("esum", [P, NT])
        score = sb("score", [P, NT, NE])
        top = sb("top", [P, NT, 8])
        topi = sb("topi", [P, NT, 8], U32)
        topf = sb("topf", [P, NT, TOPK])
        tsum = sb("tsum", [P, NT])
        oh = sb("oh", [P, NT, TOPK, NE])
        ohs = sb("ohs", [P, NT, TOPK, NE])
        mask = sb("mask", [P, NT, NE])
        maskb = sb("maskb", [P, NT, NE], BF16)
        before = sb("before", [P, NT + 1, NE])
        beforeb = sb("beforeb", [P, NT, NE], BF16)
        slot_e = sb("slot_e", [P, NT, NE])
        over = sb("over", [P, NT, NE])
        slotf = sb("slotf", [P, NT * TOPK])
        slot = sb("slot", [P, NT * TOPK], U32)
        entry = sb("entry", [P, NT * TOPK, 2])

        tab = sb("tab", [P, NE, 2])
        toku = sb("toku", [P, NE], U32)
        bidf = sb("bidf", [P, NE])
        bidi = sb("bidi", [P, NE], I32)
        bid = sb("bid", [P, NE], I32)
        xg = [t[:, i, :] for t in (x_in, h1) for i in range(NT)]
        gbg, ey = [[t[:, i, :] for i in range(NT)] for t in (x1, x_res)]
        RX = len(xg)
        ROWS_AHEAD, GATES_AHEAD = 6, 3
        xgT = sb("xgT", [P, 2, 2, P])
        eth = sb("eth", [P, IM])
        emid = sb("emid", [P, 2, IM])
        emT = sb("emT", [P, 2, 2, P])

        cT_sb = sb("cT_sb", [P, 2, B])
        cth = sb("cth", [P, 2, B])
        csl = sb("csl", [P, 2, B])
        mod_sb = midT[0:B].rearrange("b a s -> b (a s)").rearrange("b (a h) -> b a h", h=H)
        sgn = mid[0:B].rearrange("b (a h) -> b a h", h=H)
        pT_flat = pT[:].rearrange("p a b s -> p (a b s)")
        oT_flat = oT[:].rearrange("p a s -> p (a s)")
        wo_st = pT_flat.rearrange("p (h n) -> p h n", h=NH)
        wqn_st = oT_flat.rearrange("p (h n) -> p h n", h=NH)
        wk_st = h2[:].rearrange("p t n -> p (t n)").rearrange("p (h n) -> p h n", h=NH)
        wv_st = x1[:].rearrange("p t n -> p (t n)").rearrange("p (h n) -> p h n", h=NH)
        wm_st = [t[:].rearrange("p a n -> p (a n)").rearrange("p (c n) -> p c n", c=2) for t in (tmp, base, h2T)]
        pe0_st = probs[:, 0:NH * DR].rearrange("p (h n) -> p h n", h=NH)
        pe1_st = probs[:, NH * DR:2 * NH * DR].rearrange("p (h n) -> p h n", h=NH)

        EW = 4 * IM + 2 * H
        ering = ([pT_flat[:, k * EW:(k + 1) * EW] for k in range(3)] + [probs[:, k * EW:(k + 1) * EW] for k in range(2)]
                 + [oT_flat[:, k * EW:(k + 1) * EW] for k in range(3)])
        RE = len(ering)

        PS = ctx.enter_context(nc.psum_tensor("PS", [P, 8, 512], F32))
        qps = PS[:, 6:8, :].rearrange("p a (c d) -> p (a c) d", d=P)

        wq_in = sem("wq_in")
        wr_in = sem("wr_in")
        wk_in = sem("wk_in")
        wv_in = sem("wv_in")
        mod_in = sem("mod_in")
        const_ready = sem("const_ready")
        c_tanh = sem("c_tanh")
        c_ready = sem("c_ready")
        mod_ps = sem("mod_ps")
        mod_read = sem("mod_read")
        mod_ready = sem("mod_ready")
        mod_out = sem("mod_out")
        init_out = sem("init_out")
        wabs_ps = sem("wabs_ps")
        gain_ready = sem("gain_ready")
        wqh_ready = sem("wqh_ready")
        wql_ready = sem("wql_ready")
        wvo_ps = sem("wvo_ps")
        wvo_ready = sem("wvo_ready")
        x_landed = sem("x_landed")
        modb_landed = sem("modb_landed")
        res_ready = sem("res_ready")
        modT_ps = sem("modT_ps")
        mod1_ready = sem("mod1_ready")
        mod2_ready = sem("mod2_ready")
        h1_ready = sem("h1_ready")
        hT_ps = sem("hT_ps")
        hT_ready = sem("hT_ready")
        kv_ps = sem("kv_ps")
        ssq_ready = sem("ssq_ready")
        k_ready = sem("k_ready")
        kq_ps = sem("kq_ps")
        kqh_ready = sem("kqh_ready")
        kql_ready = sem("kql_ready")
        q_ps = sem("q_ps")
        nope_ready = sem("nope_ready")
        rope_ready = sem("rope_ready")
        qT_ps = sem("qT_ps")
        qTh_ready = sem("qTh_ready")
        qTl_ready = sem("qTl_ready")
        s_ps = sem("s_ps")
        max_ready = sem("max_ready")
        exp_ready = sem("exp_ready")
        wide_ready = sem("wide_ready")
        r_ps = sem("r_ps")
        rb_ready = sem("rb_ready")
        pT_ps = sem("pT_ps")
        pT_act = sem("pT_act")
        pT_dve = sem("pT_dve")
        o_ps = sem("o_ps")
        oT_ready = sem("oT_ready")
        attn_ps = sem("attn_ps")
        x1_ready = sem("x1_ready")
        n2_ready = sem("n2_ready")
        h2_scaled = sem("h2_scaled")
        h2_ready = sem("h2_ready")
        h2_out = sem("h2_out")
        h2T_ps = sem("h2T_ps")
        h2T_ready = sem("h2T_ready")
        gu_ps = sem("gu_ps")
        th_ready = sem("th_ready")
        mid_ready = sem("mid_ready")
        lg_ready = sem("lg_ready")
        lgT_ps = sem("lgT_ps")
        ls_ready = sem("ls_ready")
        ex_ready = sem("ex_ready")
        mask_ready = sem("mask_ready")
        maskb_ready = sem("maskb_ready")
        before_ready = sem("before_ready")
        count_chain = sem("count_chain")
        rank_ps = sem("rank_ps")
        slot_ready = sem("slot_ready")
        scattered = sem("scattered")
        entries_free = sem("entries_free")
        down_ps = sem("down_ps")
        gated_ready = sem("gated_ready")
        base_ready = sem("base_ready")
        base_out = sem("base_out")
        dve_chain = sem("dve_chain")
        pool_chain = sem("pool_chain")
        var1_ready = sem("var1_ready")
        rs1_ready = sem("rs1_ready")
        var2_ready = sem("var2_ready")
        rs2_ready = sem("rs2_ready")
        rsq_ready = sem("rsq_ready")
        eps1 = sem("eps1")
        eps2 = sem("eps2")
        eps3 = sem("eps3")
        tab_landed = sem("tab_landed")
        tok_ready = sem("tok_ready")
        ew_landed = [sem(f"ew_landed{i}") for i in range(RE)]
        xg_landed = [sem(f"xg_landed{i}") for i in range(RX)]
        gb_landed = [sem(f"gb_landed{i}") for i in range(NT)]
        xgT_ps = sem("xgT_ps")
        xgT_ready = sem("xgT_ready")
        egu_ps = sem("egu_ps")
        eth_ready = sem("eth_ready")
        emid_ready = sem("emid_ready")
        emT_ps = sem("emT_ps")
        emT_ready = sem("emT_ready")
        ey_ps = sem("ey_ps")
        ey_ready = sem("ey_ready")
        added = sem("added")

        block = ctx.enter_context(nc.Block())

        def heads(w, lo, hi):
            return w[:].rearrange("p (h c) -> p h c", c=P)[:, :, lo:hi]

        def latent_ps(k):
            return PS[:, 2 + 2 * k:4 + 2 * k, :].rearrange("p a (c d) -> p (a c) d", d=KL)

        ew_g = lambda r, k: ering[r][:, k * 2 * IM:(k + 1) * 2 * IM]
        ew_d = lambda r, k, n: ering[r][0:n, 4 * IM + k * H:4 * IM + (k + 1) * H]

        @block.sync
        def _(sp):
            sp.dma_start(cT_sb[:], cT.rearrange("(c p) b -> p c b", p=P)).then_inc(mod_in, 16)
            for n in range(3):
                sp.dma_start(wm_st[n], wmod[:, n * 512:(n + 1) * 512].rearrange("(c p) n -> p c n", p=P)
                             ).then_inc(mod_in, 16)
            for dst, src in ((wqn_st[:, :, 0:QL], wqnT), (wqn_st[:, :, QL:], wqnT[:, :, P:QL])):
                sp.dma_start(dst, src.rearrange("h p n -> p h n")).then_inc(wq_in, 16)
            sp.dma_start(wk_st, wkT).then_inc(wq_in, 16)
            sp.dma_start(x_in[:], rows(xr, 0)).then_inc(x_landed, 16)
            sp.dma_start(pe0_st, wqpe[0:P]).then_inc(wr_in, 16)
            sp.dma_start(qg_sb[:, 0:1], qgam[0:P].rearrange("(p a) -> p a", a=1)).then_inc(wr_in, 16)
            for lo in (0, QR):
                sp.dma_start(pe1_st[lo:lo + QR], wqpe[P:QL]).then_inc(wr_in, 16)
                sp.dma_start(qg_sb[lo:lo + QR, 1:2], qgam[P:QL].rearrange("(p a) -> p a", a=1)).then_inc(wr_in, 16)
            sp.dma_start(wkva_sb[:], wkva.rearrange("(c p) n -> p c n", p=P)).then_inc(wk_in, 16)
            sp.dma_start(kg_sb[:], kgam.partition_broadcast(P)).then_inc(wk_in, 16)
            sp.dma_start(cos_sb[:], cos.rearrange("(t p) d -> p t d", p=P)).then_inc(wk_in, 16)
            sp.dma_start(sin_sb[:], sin.rearrange("(t p) d -> p t d", p=P)).then_inc(wk_in, 16)
            sp.dma_start(wv_st, wvT).then_inc(wv_in, 16)
            sp.dma_start(wo_st, wo.rearrange("(h p) n -> p h n", p=P)).then_inc(wv_in, 16)
            sp.dma_start(sg_sb[:], sgate.rearrange("(c p) n -> p c n", p=P)).then_inc(init_out, 16)
            sp.dma_start(su_sb[:], sup.rearrange("(c p) n -> p c n", p=P)).then_inc(init_out, 16)
            sp.dma_start(sd_sb[:, 0:2, :], sdown[0:2 * P].rearrange("(c p) n -> p c n", p=P)).then_inc(init_out, 16)
            sp.dma_start(sd_sb[0:MT[2][1], 2, :], sdown[2 * P:IS]).then_inc(init_out, 16)
            sp.wait_ge(mod_ready, 1)
            sp.dma_start(mod_dram, midT[0:B].rearrange("b a s -> b (a s)")[:, 2 * H:]).then_inc(mod_out, 16)
            sp.dma_start(gb_dram, mod_sb[:, GB, :]).then_inc(mod_out, 16)
            sp.wait_ge(const_ready, 3)
            sp.dma_start(h2_dram[T:T + P, :], zrow[:]).then_inc(init_out, 16)
            sp.dma_start(tab_dram.rearrange("(p e) c -> p e c", p=P), tab_init[:]).then_inc(init_out, 16)
            sp.wait_ge(mod_out, 32)

            def load_modb(b):
                sp.dma_start(modb[:].rearrange("p a h -> p (a h)"),
                             mod_dram[bass.ds(b, 1), :].rearrange("a n -> (a n)").partition_broadcast(P)
                             ).then_inc(modb_landed, 16)

            def store_batch(b):
                sp.wait_ge(h2_ready, b + 1)
                sp.dma_start(rows(h2_dram, b), h2[:]).then_inc(h2_out, 16)
                sp.wait_ge(base_ready, b + 2)
                sp.dma_start(rows(outr, b), base[:]).then_inc(base_out, 16)

            load_modb(0)
            with sp.Fori(0, B - 1) as b:
                n = b + 1
                sp.wait_ge(h1_ready, n)
                sp.wait_ge(res_ready, n)
                sp.dma_start(x_in[:], rows(xr, n)).then_inc(x_landed, 16)
                store_batch(b)
                load_modb(n)
            store_batch(B - 1)
            sp.wait_ge(scattered, B * NT * TOPK * 16)
            sp.dma_start(tab[:], tab_dram.rearrange("(p e) c -> p e c", p=P)).then_inc(tab_landed, 16)
            sp.wait_ge(added, NE * 16)
            sp.wait_ge(base_out, B * 16 + 16)
            sp.wait_ge(h2_out, B * 16 + 16)
            sp.wait_ge(init_out, 6 * 16)

        @block.gpsimd
        def _(pool):
            ch = Chain(pool, pool_chain)
            ch.link(pool.memset(ident[:], 0.0))
            ch.link(pool.memset(caus[:], 0.0))
            ch.link(pool.memset(tri[:], 0.0))
            ch.link(pool.memset(zrow[:], 0.0))
            ch.link(pool.memset(mhalf[:], -0.5))
            ch.link(pool.memset(tab_init[:], 0.0))
            ch.wait()
            ch.link(pool.affine_select(out=ident[:], in_=ident[:], compare_op=ALU.not_equal, fill=1.0, base=0,
                                       pattern=[[-1, P]], channel_multiplier=1))
            ch.link(pool.affine_select(out=caus[:], in_=caus[:], compare_op=ALU.is_ge, fill=NEG, base=0,
                                       pattern=[[-1, P]], channel_multiplier=1))
            ch.link(pool.affine_select(out=tri[:], in_=tri[:], compare_op=ALU.is_ge, fill=1.0, base=0,
                                       pattern=[[-1, P]], channel_multiplier=1))
            ch.link(pool.iota(iota_i[:, 0, :], pattern=[[1, NE]], base=0, channel_multiplier=0))
            ch.link(pool.iota(iota_i[:, 1, :], pattern=[[0, NE]], base=T, channel_multiplier=1))
            ch.link(pool.iota(iota_i[:, 2, 0:NT], pattern=[[P, NT]], base=0, channel_multiplier=1))
            ch.wait()
            ch.link(pool.tensor_copy(identb[:], ident[:]))
            ch.link(pool.tensor_copy(causb[:], caus[:]))
            ch.link(pool.tensor_copy(trib[:], tri[:]))
            ch.link(pool.memset(onesb[:], 1.0))
            ch.link(pool.tensor_copy(eid[:], iota_i[:, 0, :]))
            ch.link(pool.tensor_copy(tid[:], iota_i[:, 2, 0:NT]))
            ch.link(pool.tensor_copy(tab_init[:, :, 0], iota_i[:, 1, :]))
            ch.wait()
            pool.memset(before[:, 0, :], 0.0).then_inc(const_ready, 3)

            def root(dst, src, eps, added_eps, ready, k):
                pool.tensor_scalar(dst, src, eps, None, ALU.add).then_inc(added_eps, 1)
                pool.wait_ge(added_eps, k + 1)
                pool.tensor_tensor(dst, dst, mhalf[:, 0:dst.shape[1]], ALU.pow).then_inc(ready, 1)

            def roots_pre(n):
                wait_alone(pool, var1_ready, NT * (n + 1))
                root(rstd[:], mv[:, :, 1], LN_EPS, eps1, rs1_ready, n)
                wait_alone(pool, ssq_ready, 8 * (n + 1))
                ssqf = ssq[:].rearrange("p a t -> p (a t)")
                root(ssqf, ssqf, RMS_EPS, eps3, rsq_ready, n)

            def post(b, n):
                wait_alone(pool, var2_ready, NT * b + 3)
                root(rstd2[:, 0:3], mv2[:, 0:3, 1], LN_EPS, eps2, rs2_ready, 2 * b)
                wait_alone(pool, var2_ready, NT * (b + 1))
                root(rstd2[:, 3:], mv2[:, 3:, 1], LN_EPS, eps2, rs2_ready, 2 * b + 1)
                spread = lambda i: modb[:, i, :].unsqueeze(1).to_broadcast([P, NT, H])
                pool.wait_ge(n2_ready, 2 * (b + 1))
                pool.wait_ge(h2T_ps, 3 * (b + 1))
                pool.tensor_tensor(h2[:], h2[:], spread(2), ALU.mult).then_inc(h2_scaled, 1)
                pool.wait_ge(h2_scaled, b + 1)
                pool.tensor_tensor(h2[:], h2[:], spread(1), ALU.add).then_inc(h2_ready, 1)
                if n is not None:
                    wait_alone(pool, x1_ready, 3 * (b + 1))
                    wait_alone(pool, x_landed, (b + 2) * 16)
                    pool.tensor_copy(x_res[:], x_in[:]).then_inc(res_ready, 1)

            def counts(b):
                def after(ins):
                    ins.then_inc(count_chain, 1)
                    state[0] += 1
                    wait_alone(pool, count_chain, b * COUNT_STEPS + state[0])
                state = [0]
                wait_alone(pool, mask_ready, b + 1)
                pool.tensor_copy(maskb[:], mask[:]).then_inc(maskb_ready, 1)
                for t in range(NT):
                    after(pool.tensor_tensor(before[:, t + 1, :], before[:, t, :], mask[:, t, :], ALU.add))
                after(pool.tensor_copy(beforeb[:], before[:, 0:NT, :]))
                pool.tensor_copy(before[:, 0, :], before[:, NT, :]).then_inc(before_ready, 1)
                ent = entry[:].rearrange("p (t k) c -> p t k c", k=TOPK)
                after(pool.tensor_copy(ent[:, :, :, 0], tid[:].unsqueeze(2).to_broadcast([P, NT, TOPK])))
                pool.tensor_scalar(tid[:], tid[:], float(S), None, ALU.add).then_inc(before_ready, 1)
                assert state[0] == COUNT_STEPS

            def shared(b):
                pool.wait_ge(base_out, 16 * b + 16)
                pool.wait_ge(gated_ready, 2 * b + 2)
                pool.tensor_tensor(base[:], tmp[:], x1[:], ALU.add).then_inc(base_ready, 1)

            roots_pre(0)
            pool.wait_ge(x_landed, 16)
            pool.tensor_copy(x_res[:], x_in[:]).then_inc(res_ready, 1)
            pool.wait_ge(init_out, 6 * 16)

            def scatter(b):
                wait_alone(pool, slot_ready, b + 2)
                for j in range(NT * TOPK):
                    pool.indirect_dma_start(
                        tab_dram[:, :], bass.IndirectOffsetOnAxis(ap=slot[:, j:j + 1], axis=0),
                        entry[:, j, :], None, bounds_check=NE * CAP - 1, oob_is_err=False,
                    ).then_inc(scattered, 16)
                pool.wait_ge(scattered, (b + 1) * NT * TOPK * 16)
                pool.sem_inc(entries_free, 1)

            with pool.Fori(0, B - 1) as b:
                roots_pre(b + 1)
                post(b, b + 1)
                counts(b)
                shared(b)
                scatter(b)
            post(LAST, None)
            counts(LAST)
            scatter(LAST)
            shared(LAST)

            pool.wait_ge(tok_ready, 1)
            pool.wait_ge(h2_out, B * 16 + 16)

            def gather_rows(e):
                if e >= RX:
                    pool.wait_ge(xgT_ps, e - RX + 1)
                pool.indirect_dma_start(xg[e % RX], None, h2_dram[:, :],
                                        bass.IndirectOffsetOnAxis(ap=toku[:, e:e + 1], axis=0),
                                        bounds_check=T + P - 1).then_inc(xg_landed[e % RX], 16)

            def gather_gates(e):
                pool.indirect_dma_start(gbg[e % NT], None, gb_dram[:, :],
                                        bass.IndirectOffsetOnAxis(ap=bid[:, e:e + 1].bitcast(U32), axis=0),
                                        bounds_check=B - 1).then_inc(gb_landed[e % NT], 16)

            for e in range(ROWS_AHEAD):
                gather_rows(e)
                if e % 2 == 0:
                    gather_gates(e // 2)
            pool.wait_ge(base_out, B * 16 + 16)
            for e in range(NE):
                pool.wait_ge(ey_ready, e + 1)
                if e:
                    pool.wait_ge(added, 16 * e)
                pool.indirect_dma_start(outr, bass.IndirectOffsetOnAxis(ap=toku[:, e:e + 1], axis=0),
                                        ey[e % NT], None, bounds_check=T - 1, oob_is_err=False,
                                        compute_op=ALU.add).then_inc(added, 16)
                if e + ROWS_AHEAD < NE:
                    gather_rows(e + ROWS_AHEAD)
                if e + GATES_AHEAD < NE:
                    gather_gates(e + GATES_AHEAD)

        @block.tensor
        def _(pe):
            pe.wait_ge(mod_in, 64)
            pe.wait_ge(c_ready, 1)
            for n in range(3):
                for c in range(2):
                    mm = pe.matmul(PS[0:B, n, :], csl[:, c, :], wm_st[n][:, c, :],
                                   start=c == 0, stop=c == 1)
            mm.then_inc(mod_ps, 1)
            def turn_modulation():
                pe.wait_ge(const_ready, 3)
                pe.wait_ge(mod_ready, 1)
                for k in range(8):
                    mm = pe.transpose(PS[:, 7, k * B:(k + 1) * B],
                                      mod_sb[:, (SA, CA, SB, CB)[k // 2], bass.ts(k % 2, P)], ident[0:B, 0:B])
                mm.then_inc(modT_ps, 1)

            pe.wait_ge(wq_in, 3 * 16)
            pe.wait_ge(mod_read, 1)
            for k in range(2):
                if k:
                    turn_modulation()
                for h in range(NH):
                    bank, col = 2 + 2 * k + h // 8, (h % 8) * KL
                    mm = pe.matmul(PS[:, bank, col:col + KL], wqn_st[:, h, bass.ts(k, P)], wk_st[:, h, :],
                                   start=True, stop=True)
                mm.then_inc(wabs_ps, 1)

            def absorb_output():
                pe.wait_ge(wql_ready, 4)
                pe.wait_ge(hT_ready, 2)
                pe.wait_ge(wv_in, 2 * 16)
                for h in range(NH):
                    p, half = h // 2, (h % 2) * KL
                    mm = pe.matmul(PS[half:half + KL, 4 + p // 2, (p % 2) * H:(p % 2 + 1) * H], wv_st[:, h, :],
                                   wo_st[:, h, :], start=True, stop=True)
                mm.then_inc(wvo_ps, 1)

            def q_project(p, g, tiles):
                cols = bass.ts(p, 2 * P)
                for t in tiles:
                    dst, tok = PS[:, QBANKS[t // 2], (t % 2) * 2 * P:(t % 2 + 1) * 2 * P], bass.ts(t, P)
                    pe.matmul(dst, ql0h[:, tok], wq0h[:, cols], start=True, stop=False)
                    pe.matmul(dst, ql0h[:, tok], wq0l[:, cols], start=False, stop=False)
                    pe.matmul(dst, ql0l[:, tok], wq0h[:, cols], start=False, stop=False)
                    pe.matmul(dst, ql1s[:, tok], wq1hh[:, cols], start=False, stop=False)
                    mm = pe.matmul(dst, ql1s[0:QR, tok], wq1l[:, cols], start=False, stop=True)
                mm.then_inc(q_ps, 1)

            def q_turn(g):
                pe.wait_ge(nope_ready, g + 1)
                pe.wait_ge(rope_ready, g + 1)
                for h in range(2):
                    for t in range(NT):
                        mm = pe.transpose(PS[:, QBANKS[h], bass.ts(t, P)], qtok[:, 2 * t + h, :], ident[:])
                    mm.then_inc(qT_ps, 1)

            def scores(g, first, units):
                for u in units:
                    h, i = UNITS[u]
                    bank, n, rows_q = SBANK[u], UW[u], bass.ts(i, P)
                    if i == NT - 1:
                        pe.wait_ge(qTl_ready, 2 * g + h + 1)
                    if u >= 3:
                        pe.wait_ge(exp_ready, g * NU + u - 2)
                    elif not first:
                        pe.wait_ge(*((pT_dve, 2 * g - 1), (pT_act, 4 * g), (pT_act, 4 * g - 1))[u])
                    pe.matmul(PS[:, bank, 0:n], qTh[:, h, rows_q], kTh[:, 0:n], start=True, stop=False)
                    pe.matmul(PS[:, bank, i * P:n], identb[:], causb[:], start=False, stop=False)
                    pe.matmul(PS[:, bank, 0:n], qTh[:, h, rows_q], kTl[:, 0:n], start=False, stop=False)
                    pe.matmul(PS[:, bank, 0:n], qTl[:, h, rows_q], kTh[:, 0:n], start=False, stop=True).then_inc(s_ps, 1)

            def turn_probs(g, first, groups):
                for k in groups:
                    units, bank = GROUPS[k]
                    pe.wait_ge(exp_ready, g * NU + max(units[-1] + 1, (1, 2, 6, 7, 8, 8)[k]))
                    if k == 0 and not first:
                        pe.wait_ge(pT_dve, 2 * g)
                    if k == 1 and not first:
                        pe.wait_ge(rb_ready, g)
                    if k == 5:
                        pe.wait_ge(pT_act, 4 * g + 1)
                    col = 0
                    for u in units:
                        for j in range(UNITS[u][1] + 1):
                            mm = pe.transpose(PS[:, bank, col:col + P], probs[:, UO[u] + j * P:UO[u] + (j + 1) * P],
                                              ident[:])
                            col += P
                    mm.then_inc(pT_ps, 1)

            def spread_sums(g):
                pe.wait_ge(wide_ready, g + 1)
                pe.wait_ge(pT_act, 4 * g + 2)
                for t in range(NT):
                    mm = pe.transpose(PS[:, RBANK, bass.ts(t, P)], wide[:, bass.ts(NT - 1 - t, P)], ident[:])
                mm.then_inc(r_ps, 1)

            def values(g, b):
                pe.wait_ge(pT_act, (g + 1) * 4)
                pe.wait_ge(pT_dve, (g + 1) * 2)
                pe.wait_ge(oT_ready, g + 1)
                pe.wait_ge(slot_ready, b + 1)
                for j in range(NT):
                    for h in range(2):
                        mm = pe.matmul(PS[h * KL:(h + 1) * KL, OBANK, j * P:S], kmat[:, j, 0:KL],
                                       pT[:, h, j, j * P:S], start=j == 0, stop=j == NT - 1)
                mm.then_inc(o_ps, 1)

            def step(p, b, first, last, more):
                g = b * NPAIR + p
                if last:
                    pe.wait_ge(oT_ready, g)
                    pe.wait_ge(qTl_ready, 2 * g + 2)
                    output(1, 7, range(0, 3))
                else:
                    q_project(p + 1, g + 1, (0, 1))
                if first and more:
                    pe.wait_ge(mid_ready, 3 * b)
                    shared_down(0)
                scores(g, first, (3, 4))
                if last:
                    output(1, 7, range(3, NPAIR - 2))
                else:
                    q_project(p + 1, g + 1, (2, 3))
                scores(g, first, (5, 6, 7))
                if not first:
                    values(g - 1, b)
                if first and more:
                    shared_down(1)
                    pe.wait_ge(gated_ready, 2 * b - 1)
                turn_probs(g, first, (0, 1))
                if not last:
                    q_turn(g + 1)
                elif more:
                    turn_h1(b + 1, 0)
                turn_probs(g, first, (2, 3))
                if last and more:
                    turn_h1(b + 1, 1)
                turn_probs(g, first, (4, 5))
                spread_sums(g)
                if not last:
                    scores(g + 1, False, (0, 1, 2))
                if first and more:
                    pe.wait_ge(gated_ready, 2 * b)
                    ranks(b - 1)

            def ranks(b):
                pe.wait_ge(maskb_ready, b + 1)
                pe.wait_ge(before_ready, 2 * b + 1)
                pe.matmul(PS[:, OBANK, 64:64 + NT * NE], trib[:], maskb[:].rearrange("p t e -> p (t e)"),
                          start=True, stop=False)
                pe.matmul(PS[:, OBANK, 64:64 + NT * NE], onesb[:], beforeb[:].rearrange("p t e -> p (t e)"),
                          start=False, stop=True).then_inc(rank_ps, 1)

            def turn_h1(n, c):
                pe.wait_ge(h1_ready, n + 1)
                if c:
                    pe.wait_ge(hT_ready, 2 * n + 1)
                for t in range(NT):
                    mm = pe.transpose(PS[:, 6, bass.ts(t, P)], h1[:, t, bass.ts(c, P)], ident[:])
                mm.then_inc(hT_ps, 1)

            def turn_h2():
                for c in range(2):
                    for t in range(NT - 1):
                        mm = pe.transpose(PS[:, 1 + c, bass.ts(t, P)], h2[:, t, bass.ts(c, P)], ident[:])
                    mm.then_inc(h2T_ps, 1)

            def turn_h2_last():
                for c in range(2):
                    mm = pe.transpose(PS[:, 0, bass.ts(c, P)], h2[:, NT - 1, bass.ts(c, P)], ident[:])
                mm.then_inc(h2T_ps, 1)

            def ffn(b, m, banks):
                off, w = MT[m]
                wide = w + (NE if m == 2 else 0)
                for c in range(2):
                    if m == 2:
                        pe.wait_ge(h2T_ready, 4 * b + c + 3)
                    pe.matmul(PS[0:wide, banks[0], :], sg_sb[:, c, off:off + wide], h2T[:, c, :],
                              start=c == 0, stop=c == 1)
                    mm = pe.matmul(PS[0:w, banks[1], :], su_sb[:, c, off:off + w], h2T[:, c, :],
                                   start=c == 0, stop=c == 1)
                mm.then_inc(gu_ps, 1)

            def output(t, bank, pairs):
                for p in pairs:
                    mm = pe.matmul(PS[:, bank, 0:H], oT[:, p, bass.ts(t, P)], wvo[:, p, :],
                                   start=p == 0, stop=p == NPAIR - 1)
                return mm

            def shared_down(half):
                for k in range(2):
                    for a, (off, w) in enumerate(MT):
                        mm = pe.matmul(PS[:, 4 + half, k * H:(k + 1) * H], midT[0:w, a, bass.ts(2 * half + k, P)],
                                       sd_sb[0:w, a, :], start=a == 0, stop=a == 2)
                mm.then_inc(down_ps, 1)

            def turn_router(b):
                wait_alone(pe, lg_ready, b + 1)
                for t in range(NT):
                    mm = pe.transpose(PS[:, 1, bass.ts(t, NE)], lgT[:, bass.ts(t, P)], ident[0:NE, 0:NE])
                mm.then_inc(lgT_ps, 1)

            def middle(b, n, post, pre):
                if pre:
                    pe.wait_ge(hT_ready, 2 * (n + 1))
                    if not post:
                        pe.wait_ge(wk_in, 4 * 16)
                        pe.wait_ge(wql_ready, 1)
                    for k, t in enumerate(KV_ORDER):
                        if post:
                            pe.wait_ge(*((pT_act, 4 * n * NPAIR - 1), (pT_dve, 2 * n * NPAIR - 1),
                                         (pT_act, 4 * n * NPAIR), (pT_dve, 2 * n * NPAIR))[k])
                        for c in range(2):
                            mm = pe.matmul(PS[:, t, 0:FW], hT[:, c, bass.ts(t, P)], wkva_sb[:, c, :],
                                           start=c == 0, stop=c == 1)
                        mm.then_inc(kv_ps, 1)
                if post:
                    values(b * NPAIR + NPAIR - 1, b)
                    pe.wait_ge(oT_ready, (b + 1) * NPAIR)
                    output(1, 7, (NPAIR - 2,))
                    output(0, 6, range(0, NPAIR - 1))
                    pe.wait_ge(oT_ready, (b + 1) * NPAIR + 1)
                    output(1, 7, (NPAIR - 1,))
                    output(0, 6, (NPAIR - 1,)).then_inc(attn_ps, 1)
                    output(2, 5, range(0, 2))
                else:
                    absorb_output()
                    pe.wait_ge(wvo_ready, 4)
                if pre:
                    pe.wait_ge(k_ready, n + 1)
                    for bank, src in ((2, kmat[:]), (1, qn[:, :, 0:P]), (0, qn[:, :, P:2 * P])):
                        for t in range(NT):
                            mm = pe.transpose(PS[:, bank, bass.ts(t, P)], src[:, t, :], ident[:])
                        mm.then_inc(kq_ps, 1)
                if not post:
                    pe.wait_ge(wql_ready, 4)
                if post:
                    output(2, 5, range(2, NPAIR)).then_inc(attn_ps, 1)
                    output(3, 3, range(NPAIR)).then_inc(attn_ps, 1)
                if pre:
                    pe.wait_ge(kql_ready, 3 * (n + 1))
                    q_project(0, n * NPAIR, (0, 1))
                if post:
                    pe.wait_ge(n2_ready, 2 * b + 1)
                    turn_h2()
                if pre:
                    q_project(0, n * NPAIR, (2, 3))
                if post:
                    pe.wait_ge(n2_ready, 2 * b + 2)
                    turn_h2_last()
                    ffn(b, 2, (3, 4))
                if pre:
                    q_turn(n * NPAIR)
                if post:
                    if pre:
                        ffn(b, 0, (5, 0))
                    turn_router(b)
                    if not pre:
                        ffn(b, 0, (5, 0))
                    pe.wait_ge(mid_ready, 3 * b + 1)
                    ffn(b, 1, (3, 4))
                    pe.wait_ge(mid_ready, 3 * b + 2)
                    pe.wait_ge(ls_ready, b + 1)
                if not pre:
                    ranks(b)
                if pre:
                    scores(n * NPAIR, True, (0, 1, 2))
                else:
                    pe.wait_ge(mid_ready, 3 * b + 3)
                    shared_down(0)
                    pe.wait_ge(slot_ready, b + 2)
                    shared_down(1)

            def pairs(b, more):
                with pe.Fori(1, NPAIR - 1) as p:
                    step(p, b, False, False, more)
                step(NPAIR - 1, b, False, True, more)

            turn_h1(0, 0)
            turn_h1(0, 1)
            middle(0, 0, False, True)
            step(0, 0, True, False, False)
            with pe.Fori(0, LAST) as b:
                pairs(b, True)
                middle(b, b + 1, True, True)
                step(0, b + 1, True, False, True)
            pairs(LAST, False)
            middle(LAST, None, True, False)
            pe.wait_ge(gated_ready, 2 * B)

            def turn_rows(e):
                q = e % 2
                pe.wait_ge(xg_landed[e % RX], 16 * (e // RX + 1))
                for c in range(2):
                    mm = pe.transpose(PS[:, q, bass.ts(c, P)], xg[e % RX][:, bass.ts(c, P)], ident[:])
                mm.then_inc(xgT_ps, 1)

            def gate_up(e):
                r, q = e % RE, e % 2
                pe.wait_ge(xgT_ready, e + 1)
                pe.wait_ge(ew_landed[r], 64 * (e // RE + 1))
                for c in range(2):
                    mm = pe.matmul(PS[:, 2 + q, 0:2 * IM], xgT[:, q, c, :], ew_g(r, c), start=c == 0, stop=c == 1)
                mm.then_inc(egu_ps, 1)

            def turn_inner(e):
                q = e % 2
                pe.wait_ge(emid_ready, e + 1)
                pe.transpose(PS[:, 4 + q, 0:P], emid[:, q, 0:P], ident[:])
                pe.transpose(PS[0:IR, 4 + q, P:2 * P], emid[:, q, P:IM], ident[:]).then_inc(emT_ps, 1)

            def down(e):
                r, q = e % RE, e % 2
                pe.wait_ge(emT_ready, e + 1)
                if e >= 2:
                    pe.wait_ge(ey_ready, e - 1)
                pe.matmul(PS[:, 6 + q, 0:H], emT[:, q, 0, :], ew_d(r, 0, P), start=True, stop=False)
                pe.matmul(PS[:, 6 + q, 0:H], emT[0:IR, q, 1, :], ew_d(r, 1, IR), start=False,
                          stop=True).then_inc(ey_ps, 1)

            turn_rows(0)
            for e in range(NE):
                gate_up(e)
                if e:
                    turn_inner(e - 1)
                if e + 1 < NE:
                    turn_rows(e + 1)
                if e >= 2:
                    down(e - 2)
            turn_inner(NE - 1)
            down(NE - 2)
            down(NE - 1)

        @block.scalar
        def _(act):
            act.sem_inc(oT_ready, 1)
            act.sem_inc(h2_out, 16)
            act.sem_inc(base_out, 16)
            act.sem_inc(base_ready, 1)
            act.sem_inc(slot_ready, 1)
            act.sem_inc(entries_free, 1)
            act.wait_ge(mod_in, 64)
            act.activation(cth[:], cT_sb[:], ACT.Tanh, scale=0.5).then_inc(c_tanh, 1)

            def nope_copy(g):
                act.wait_ge(q_ps, 2 * g + 2)
                act.activation(qtok[:, :, 0:KL], qps[:, :, 0:KL], ACT.Copy).then_inc(nope_ready, 1)

            def q_high(g, h):
                act.wait_ge(qT_ps, 2 * g + h + 1)
                act.activation(qTh[:, h, :], PS[:, QBANKS[h], :], ACT.Copy).then_inc(qTh_ready, 1)

            def exps(g, units):
                for u in units:
                    act.wait_ge(max_ready, g * NU + u + 1)
                    act.activation(probs[:, UO[u]:UO[u] + UW[u]], PS[:, SBANK[u], 0:UW[u]], ACT.Exp,
                                   bias=nmax[:, u:u + 1], accum_out=psums[:, u:u + 1]).then_inc(exp_ready, 1)

            def group_out(g, k):
                units, bank = GROUPS[k]
                act.wait_ge(pT_ps, g * len(GROUPS) + k + 1)
                col = 0
                for u in units:
                    h, i = UNITS[u]
                    cp = act.activation(pT[:, h, 0:i + 1, bass.ts(i, P)],
                                        PS[:, bank, col:col + UW[u]].rearrange("p (j q) -> p j q", q=P), ACT.Copy)
                    col += UW[u]
                cp.then_inc(pT_act, 1)

            def sums_out(g):
                act.wait_ge(r_ps, g + 1)
                act.wait_ge(oT_ready, g + 1)
                act.activation(rb[:], PS[:, RBANK, :], ACT.Copy).then_inc(rb_ready, 1)

            def step(p, b, last, more):
                g = b * NPAIR + p
                exps(g, (3, 4))
                if not last:
                    nope_copy(g + 1)
                exps(g, (5, 6, 7))
                group_out(g, 0)
                group_out(g, 1)
                if not last:
                    q_high(g + 1, 0)
                    q_high(g + 1, 1)
                elif more:
                    turned_h1(b + 1)
                group_out(g, 2)
                group_out(g, 4)
                sums_out(g)
                if not last:
                    exps(g + 1, (0, 1, 2))

            def pairs(b, more):
                with act.Fori(1, NPAIR - 1) as p:
                    step(p, b, False, more)
                step(NPAIR - 1, b, True, more)

            def tanh_gate(b, k, m, bank):
                w = MT[m][1]
                act.wait_ge(gu_ps, 3 * b + k + 1)
                if k:
                    act.wait_ge(mid_ready, 3 * b + k)
                act.activation(th[0:w, :], PS[0:w, bank, :], ACT.Tanh, scale=0.5).then_inc(th_ready, 1)

            def turned_h1(n):
                act.wait_ge(mod1_ready, n + 1)
                for c in range(2):
                    act.wait_ge(hT_ps, 2 * n + c + 1)
                    act.activation(hT[:, c, :], PS[:, 6, :], ACT.Identity, scale=mod1[:, 2 + c:3 + c],
                                   bias=mod1[:, c:c + 1]).then_inc(hT_ready, 1)

            def turned_h2(b):
                act.wait_ge(mod2_ready, b + 1)
                for c in range(2):
                    act.wait_ge(h2T_ps, 3 * b + c + 1)
                    act.activation(h2T[:, c, 0:S - P], PS[:, 1 + c, 0:S - P], ACT.Identity, scale=mod2[:, 2 + c:3 + c],
                                   bias=mod2[:, c:c + 1]).then_inc(h2T_ready, 1)

            def turned_h2_last(b):
                act.wait_ge(h2T_ps, 3 * b + 3)
                for c in range(2):
                    act.activation(h2T[:, c, S - P:S], PS[:, 0, bass.ts(c, P)], ACT.Identity,
                                   scale=mod2[:, 2 + c:3 + c], bias=mod2[:, c:c + 1]).then_inc(h2T_ready, 1)

            def middle(b, n, post, pre):
                if pre:
                    for k, t in enumerate(KV_ORDER):
                        act.wait_ge(kv_ps, NT * n + k + 1)
                        act.activation(sq[:], PS[:, t, 0:QL], ACT.Square, scale=QL ** -0.5,
                                       accum_out=ssq[:, 0, t:t + 1]).then_inc(ssq_ready, 1)
                        act.wait_ge(ssq_ready, 2 * (NT * n + k) + 1)
                        act.activation(sq[:, 0:KL], PS[:, t, QL:QL + KL], ACT.Square, scale=KL ** -0.5,
                                       accum_out=ssq[:, 1, t:t + 1]).then_inc(ssq_ready, 1)
                        act.wait_ge(ssq_ready, 2 * (NT * n + k) + 2)
                    if not post:
                        act.wait_ge(wvo_ps, 1)
                        for a in range(4):
                            act.activation(wvo[:, 2 * a:2 * a + 2, :].rearrange("p a n -> p (a n)"), PS[:, 4 + a, :],
                                           ACT.Copy).then_inc(wvo_ready, 1)
                    for k, (dst, bank) in enumerate([(kTh, 2), (ql0h, 1)]):
                        act.wait_ge(kq_ps, 3 * n + k + 1)
                        act.activation(dst[:], PS[:, bank, :], ACT.Copy).then_inc(kqh_ready, 1)
                    act.wait_ge(kq_ps, 3 * n + 3)
                    act.activation(ql1s[0:QR, :], PS[0:QR, 0, :], ACT.Copy).then_inc(kqh_ready, 1)
                    act.activation(ql1t[QR:P, :], PS[QR:P, 0, :], ACT.Copy).then_inc(kqh_ready, 1)
                if post:
                    turned_h2(b)
                    turned_h2_last(b)
                if pre:
                    nope_copy(n * NPAIR)
                if post:
                    tanh_gate(b, 0, 2, 3)
                    w = MT[2][1]
                    act.activation(lgT[:], PS[w:w + NE, 3, :], ACT.Copy).then_inc(lg_ready, 1)
                if pre:
                    q_high(n * NPAIR, 0)
                    q_high(n * NPAIR, 1)
                if post:
                    if pre:
                        tanh_gate(b, 1, 0, 5)
                    act.wait_ge(ls_ready, b + 1)
                    act.activation(ex[:], ls[:], ACT.Exp).then_inc(ex_ready, 1)
                    if not pre:
                        tanh_gate(b, 1, 0, 5)
                    tanh_gate(b, 2, 1, 3)
                if pre:
                    exps(n * NPAIR, (0, 1, 2))

            act.wait_ge(gain_ready, 1)
            for k, (high, pe_st) in enumerate([(wq0h, pe0_st), (wq1hh, pe1_st)]):
                act.wait_ge(wabs_ps, k + 1)
                for src, lo, hi in ((latent_ps(k), 0, KL), (pe_st, KL, P)):
                    act.activation(heads(high, lo, hi), src, ACT.Copy, scale=qg_sb[:, k:k + 1]).then_inc(wqh_ready, 1)
            turned_h1(0)
            middle(0, 0, False, True)
            step(0, 0, False, False)
            with act.Fori(0, LAST) as b:
                pairs(b, True)
                middle(b, b + 1, True, True)
                step(0, b + 1, False, True)
            pairs(LAST, False)
            middle(LAST, None, True, False)

            def load(e):
                r = e % RE
                if e >= RE:
                    act.wait_ge(ey_ps, e - RE + 1)
                elif e == 0:
                    act.wait_ge(o_ps, B * NPAIR)
                elif e == 5:
                    act.wait_ge(attn_ps, 3 * B)
                act.dma_start(ering[r][:, 0:4 * IM].rearrange("p (c n) -> p c n", c=2)[:, :, 0:IM],
                              egate[e].rearrange("(c p) n -> p c n", p=P)).then_inc(ew_landed[r], 16)
                act.dma_start(ering[r][:, 0:4 * IM].rearrange("p (c n) -> p c n", c=2)[:, :, IM:2 * IM],
                              eup[e].rearrange("(c p) n -> p c n", p=P)).then_inc(ew_landed[r], 16)
                act.dma_start(ew_d(r, 0, P), edown[e, 0:P, :]).then_inc(ew_landed[r], 16)
                act.dma_start(ew_d(r, 1, IR), edown[e, P:IM, :]).then_inc(ew_landed[r], 16)

            for e in range(RE):
                load(e)

            def rows_out(e):
                act.wait_ge(xgT_ps, e + 1)
                act.activation(xgT[:, e % 2, :, :].rearrange("p c s -> p (c s)"), PS[:, e % 2, 0:2 * P],
                               ACT.Copy).then_inc(xgT_ready, 1)

            def inner_out(e):
                act.wait_ge(emT_ps, e + 1)
                act.activation(emT[:, e % 2, 0, :], PS[:, 4 + e % 2, 0:P], ACT.Copy)
                act.activation(emT[0:IR, e % 2, 1, :], PS[0:IR, 4 + e % 2, P:2 * P], ACT.Copy).then_inc(emT_ready, 1)

            rows_out(0)
            for e in range(NE):
                act.wait_ge(egu_ps, e + 1)
                if e:
                    act.wait_ge(emid_ready, e)
                act.activation(eth[:], PS[:, 2 + e % 2, 0:IM], ACT.Tanh, scale=0.5).then_inc(eth_ready, 1)
                if e:
                    inner_out(e - 1)
                if e + 1 < NE:
                    rows_out(e + 1)
                if e >= 2 and e - 2 + RE < NE:
                    load(e - 2 + RE)
            inner_out(NE - 1)

        @block.vector
        def _(dve):
            ch = Chain(dve, dve_chain)
            dve.wait_ge(c_tanh, 1)
            ch.step(dve.tensor_scalar(cth[:], cth[:], 1.0, 0.5, ALU.add, ALU.mult))
            dve.tensor_tensor(csl[:], cth[:], cT_sb[:], ALU.mult).then_inc(c_ready, 1)
            dve.wait_ge(mod_ps, 1)
            dve.tensor_copy(midT[0:B].rearrange("b a s -> b (a s)"),
                            PS[0:B, 0:3, :].rearrange("b a n -> b (a n)")).then_inc(mod_read, 1)
            dve.wait_ge(mod_read, 1)
            for k, i in enumerate((GA, GB)):
                ch.step(dve.tensor_scalar(sgn[:, 0, :], mod_sb[:, i, :], 0.0, 2.0, ALU.is_ge, ALU.mult))
                ch.step(dve.tensor_scalar(sgn[:, 0, :], sgn[:, 0, :], -1.0, 0.5 if i == GB else 1.0, ALU.add, ALU.mult))
                ch.step(dve.scalar_tensor_tensor(out=sgn[:, 1, :], in0=mod_sb[:, i, :], scalar=-1.0,
                                                 in1=mod_sb[:, i, :], op0=ALU.mult, op1=ALU.max))
                ch.step(dve.scalar_tensor_tensor(out=mod_sb[:, i, :], in0=sgn[:, 1, :], scalar=0.25,
                                                 in1=sgn[:, 0, :], op0=ALU.max, op1=ALU.mult))
            ch.step(dve.tensor_scalar(mod_sb[:, CA, :], mod_sb[:, CA, :], 1.0, None, ALU.add))
            dve.tensor_scalar(mod_sb[:, CB, :], mod_sb[:, CB, :], 1.0, None, ALU.add).then_inc(mod_ready, 1)
            dve.wait_ge(modT_ps, 1)
            ch.step(dve.tensor_copy(modT[:].rearrange("p k b -> p (k b)"), PS[:, 7, 0:8 * B]))
            dve.wait_ge(wr_in, 6 * 16)
            dve.tensor_scalar(qg_sb[:], qg_sb[:], SCALE, None, ALU.mult).then_inc(gain_ready, 1)

            def statistics(src, stats, mean_var, var_ready, tiles):
                for t in tiles:
                    ch.link(dve.bn_stats(stats[:, t, :], src[:, t, :]))
                wait_alone(dve, ch.sem, ch.base + ch.n)
                for t in tiles:
                    dve.bn_aggr(mean_var[:, t, :], stats[:, t, :]).then_inc(var_ready, 1)

            def normed(src, dst, mean_var, rs, tiles, ready):
                for t in tiles:
                    last = dve.tensor_scalar(dst[:, t, :], src[:, t, :], mean_var[:, t, 0:1], rs[:, t:t + 1],
                                             ALU.subtract, ALU.mult)
                last.then_inc(ready, 1)

            def h1_statistics(n):
                dve.wait_ge(x_landed, 16 * (n + 1))
                dve.tensor_copy(mod1[:], modT[:, 0:4, bass.ds(n, 1)].rearrange("p k b -> p (k b)")).then_inc(mod1_ready, 1)
                statistics(x_in, st, mv, var1_ready, range(NT))

            def h1_normed(n):
                dve.wait_ge(var1_ready, NT * (n + 1))
                dve.wait_ge(rs1_ready, n + 1)
                normed(x_in, h1, mv, rstd, range(NT), h1_ready)

            HALF = DR // 2

            def rope_parts(raw, t1, t2, heads):
                def tab(a, lo, hi):
                    return a[:, :, lo:hi].unsqueeze(2).to_broadcast([P, NT, heads, hi - lo])

                def v(a, lo, hi):
                    return a[:, :, lo:hi].rearrange("p (t h) d -> p t h d", h=heads)
                return [lambda: dve.tensor_tensor(v(t1, 0, DR), v(raw, 0, DR), tab(cos_sb, 0, DR), ALU.mult),
                        lambda: dve.tensor_tensor(v(t2, 0, HALF), v(raw, HALF, DR), tab(sin_sb, 0, HALF), ALU.mult),
                        lambda: dve.tensor_tensor(v(t2, HALF, DR), v(raw, 0, HALF), tab(sin_sb, HALF, DR), ALU.mult)]

            def q_rope(g):
                parts = rope_parts(qps[:, :, KL:P], qr1, qr2, 2)

                def first():
                    dve.wait_ge(nope_ready, g + 1)
                    ch.link(parts[0]())

                def last():
                    ch.wait()
                    dve.tensor_tensor(qtok[:, :, KL:P], qr1[:], qr2[:], ALU.add).then_inc(rope_ready, 1)
                return [first, lambda: ch.link(parts[1]()), lambda: ch.link(parts[2]()), last]

            def maxima(g, units):
                for u in units:
                    dve.wait_ge(s_ps, g * NU + u + 1)
                    dve.tensor_reduce(nmax[:, u:u + 1], PS[:, SBANK[u], 0:UW[u]], AX.X, ALU.max,
                                      negate=True).then_inc(max_ready, 1)

            def invert_sums(g):
                dve.wait_ge(exp_ready, g * NU + NU)
                ch.step(dve.reciprocal(prec[:], psums[:]))
                dve.tensor_copy(wide[:].rearrange("p (t h d) -> p h t d", t=NT, h=2),
                                prec[:].rearrange("p (h t) -> p h t", h=2).unsqueeze(3).to_broadcast(
                                    [P, 2, NT, KL])).then_inc(wide_ready, 1)

            def group_out(g, k):
                units, bank = GROUPS[k]
                dve.wait_ge(pT_ps, g * len(GROUPS) + k + 1)
                col = 0
                for u in units:
                    h, i = UNITS[u]
                    cp = dve.tensor_copy(pT[:, h, 0:i + 1, bass.ts(i, P)],
                                         PS[:, bank, col:col + UW[u]].rearrange("p (j q) -> p j q", q=P))
                    col += UW[u]
                cp.then_inc(pT_dve, 1)

            def values_out(p, g):
                dve.wait_ge(o_ps, g + 1)
                dve.wait_ge(rb_ready, g + 1)
                dve.tensor_tensor(oT[:, p, :], PS[:, OBANK, :], rb[:], ALU.mult).then_inc(oT_ready, 1)

            def q_low(g, h):
                dve.wait_ge(qTh_ready, 2 * g + h + 1)
                dve.tensor_tensor(qTl[:, h, :], PS[:, QBANKS[h], :], qTh[:, h, :].bitcast(F32),
                                  ALU.subtract).then_inc(qTl_ready, 1)

            def step(p, b, first, last, more):
                g = b * NPAIR + p
                maxima(g, (3, 4))
                if first and more:
                    gated(b - 1, 0)
                if last and more:
                    h1_statistics(b + 1)
                maxima(g, (5, 6, 7))
                if not last:
                    for part in q_rope(g + 1):
                        part()
                elif more:
                    h1_normed(b + 1)
                invert_sums(g)
                if not first:
                    values_out(p - 1, g - 1)
                elif more:
                    gated(b - 1, 1)
                if not last:
                    q_low(g + 1, 0)
                group_out(g, 3)
                group_out(g, 5)
                if not last:
                    q_low(g + 1, 1)
                    maxima(g + 1, (0, 1, 2))
                if first and more:
                    slots(b - 1)

            def silu_mid(b, k, m, banks):
                w = MT[m][1]
                dve.wait_ge(th_ready, 3 * b + k + 1)
                ch.step(dve.scalar_tensor_tensor(out=mid[0:w, :], in0=th[0:w, :], scalar=1.0,
                                                 in1=PS[0:w, banks[0], :], op0=ALU.add, op1=ALU.mult))
                dve.tensor_tensor(midT[0:w, m, :], mid[0:w, :], PS[0:w, banks[1], :], ALU.mult).then_inc(mid_ready, 1)

            def over_e(a):
                return a.unsqueeze(2).to_broadcast([P, NT, NE])

            def router_scores(b):
                dve.wait_ge(lgT_ps, b + 1)
                lg = PS[:, 1, 0:NT * NE].rearrange("p (t e) -> p t e", e=NE)
                ch.step(dve.tensor_reduce(lmax[:], lg, AX.X, ALU.max))
                dve.tensor_tensor(ls[:], lg, over_e(lmax[:]), ALU.subtract).then_inc(ls_ready, 1)

            def route(b):
                dve.wait_ge(ex_ready, b + 1)
                ch.step(dve.tensor_reduce(esum[:], ex[:], AX.X, ALU.add))
                ch.step(dve.reciprocal(esum[:], esum[:]))
                ch.link(dve.tensor_tensor(score[:], ex[:], over_e(esum[:]), ALU.mult))
                wait_alone(dve, ch.sem, ch.base + ch.n)
                for t in range(NT):
                    ch.link(dve.max(top[:, t, :], score[:, t, :]))
                wait_alone(dve, ch.sem, ch.base + ch.n)
                for t in range(NT):
                    ch.link(dve.max_index(topi[:, t, :], top[:, t, :], score[:, t, :]))
                ch.step(dve.tensor_reduce(tsum[:], top[:, :, 0:TOPK], AX.X, ALU.add))
                ch.step(dve.tensor_scalar(tsum[:], tsum[:], 1e-20, None, ALU.add))
                ch.step(dve.reciprocal(tsum[:], tsum[:]))
                ch.step(dve.tensor_copy(topf[:], topi[:, :, 0:TOPK]))
                ent = entry[:].rearrange("p (t k) c -> p t k c", k=TOPK)

                def over_k(a):
                    return a.unsqueeze(2).to_broadcast([P, NT, TOPK])
                dve.wait_ge(entries_free, b + 1)
                ch.link(dve.tensor_tensor(ent[:, :, :, 1], top[:, :, 0:TOPK], over_k(tsum[:]), ALU.mult))
                ch.step(dve.tensor_tensor(oh[:].rearrange("p t k e -> p (t k) e"),
                                          eid[:].unsqueeze(1).to_broadcast([P, NT * TOPK, NE]),
                                          topf[:].rearrange("p t k -> p (t k)").unsqueeze(2).to_broadcast(
                                              [P, NT * TOPK, NE]), ALU.is_equal))
                dve.tensor_reduce(mask[:], oh[:].rearrange("p t k e -> p t e k"), AX.X, ALU.add).then_inc(mask_ready, 1)

            def slots(b):
                dve.wait_ge(rank_ps, b + 1)
                rank = PS[:, OBANK, 64:64 + NT * NE].rearrange("p (t e) -> p t e", e=NE)
                ch.link(dve.tensor_scalar(over[:], rank, float(CAP), FAR, ALU.is_ge, ALU.mult))
                ch.step(dve.scalar_tensor_tensor(out=slot_e[:], in0=rank, scalar=float(NE),
                                                 in1=eid[:].unsqueeze(1).to_broadcast([P, NT, NE]),
                                                 op0=ALU.mult, op1=ALU.add))
                ch.step(dve.tensor_tensor(slot_e[:], slot_e[:], over[:], ALU.add))
                ch.step(dve.tensor_tensor(ohs[:], oh[:], slot_e[:].unsqueeze(2).to_broadcast([P, NT, TOPK, NE]),
                                          ALU.mult))
                ch.step(dve.tensor_reduce(slotf[:], ohs[:].rearrange("p t k e -> p (t k) e"), AX.X, ALU.add))
                dve.tensor_copy(slot[:], slotf[:]).then_inc(slot_ready, 1)

            def gate_of(i, tiles):
                return modb[:, i, :].unsqueeze(1).to_broadcast([P, tiles, H])

            def gated(b, half):
                dve.wait_ge(down_ps, 2 * b + half + 1)
                dve.tensor_tensor(tmp[:, 2 * half:2 * half + 2, :], PS[:, 4 + half, :].rearrange("p (c n) -> p c n", n=H),
                                  gate_of(3, 2), ALU.mult).then_inc(gated_ready, 1)

            def residual(b, k, lo, hi, src):
                dve.wait_ge(attn_ps, 3 * b + k + 1)
                ch.step(dve.tensor_tensor(tmp[:, lo:hi, :], src, gate_of(0, hi - lo), ALU.mult))
                dve.tensor_tensor(x1[:, lo:hi, :], tmp[:, lo:hi, :], x_res[:, lo:hi, :], ALU.add).then_inc(x1_ready, 1)
                dve.wait_ge(x1_ready, 3 * b + k + 1)
                for t in range(lo, hi):
                    ch.link(dve.bn_stats(st2[:, t, :], x1[:, t, :]))

            def variances(tiles):
                wait_alone(dve, ch.sem, ch.base + ch.n)
                for t in tiles:
                    dve.bn_aggr(mv2[:, t, :], st2[:, t, :]).then_inc(var2_ready, 1)

            def middle(b, n, post, pre):
                if post:
                    values_out(NPAIR - 1, b * NPAIR + NPAIR - 1)
                if pre:
                    dve.wait_ge(rsq_ready, n + 1)
                    for t in range(NT):
                        ch.link(dve.tensor_scalar(qn[:, t, 0:QL], PS[:, t, 0:QL], ssq[:, 0, t:t + 1], None, ALU.mult))
                        ch.link(dve.tensor_scalar(qn[:, t, QL:], PS[:, t, P:QL], ssq[:, 0, t:t + 1], None, ALU.mult))
                    for t in range(NT):
                        ch.link(dve.scalar_tensor_tensor(out=kmat[:, t, 0:KL], in0=PS[:, t, QL:QL + KL],
                                                         scalar=ssq[:, 1, t:t + 1], in1=kg_sb[:],
                                                         op0=ALU.mult, op1=ALU.mult))
                    for part in rope_parts(PS[:, 0:4, QL + KL:FW], kr1, kr2, 1):
                        ch.link(part())
                    ch.wait()
                    dve.tensor_tensor(kmat[:, :, KL:], kr1[:], kr2[:], ALU.add).then_inc(k_ready, 1)
                if post:
                    dve.tensor_copy(mod2[:], modT[:, 4:8, bass.ds(b, 1)].rearrange("p k b -> p (k b)")
                                    ).then_inc(mod2_ready, 1)
                    dve.wait_ge(modb_landed, 16 * (b + 1))
                    dve.wait_ge(res_ready, b + 1)
                    dve.wait_ge(base_ready, b + 1)
                    residual(b, 0, 0, 2, PS[:, 6:8, 0:H])
                if pre:
                    for k, (low, high, bank, lo) in enumerate([(kTl, kTh, 2, 0), (ql0l, ql0h, 1, 0),
                                                               (ql1s, ql1t, 0, QR)]):
                        dve.wait_ge(kqh_ready, 4 * n + (k + 1 if k < 2 else 4))
                        dve.tensor_tensor(low[lo:P, :], PS[lo:P, bank, :], high[lo:P, :].bitcast(F32),
                                          ALU.subtract).then_inc(kql_ready, 1)
                if post:
                    residual(b, 1, 2, 3, PS[:, 5:6, 0:H])
                    variances(range(3))
                    dve.wait_ge(h2_out, 16 * b + 16)
                    dve.wait_ge(rs2_ready, 2 * b + 1)
                    normed(x1, h2, mv2, rstd2, range(3), n2_ready)
                    residual(b, 2, 3, 4, PS[:, 3:4, 0:H])
                    variances(range(3, 4))
                    dve.wait_ge(rs2_ready, 2 * b + 2)
                    normed(x1, h2, mv2, rstd2, range(3, 4), n2_ready)
                if pre:
                    for part in q_rope(n * NPAIR):
                        part()
                if post and pre:
                    silu_mid(b, 0, 2, (3, 4))
                if pre:
                    q_low(n * NPAIR, 0)
                    q_low(n * NPAIR, 1)
                if post:
                    router_scores(b)
                    if not pre:
                        silu_mid(b, 0, 2, (3, 4))
                        route(b)
                    silu_mid(b, 1, 0, (5, 0))
                    if not pre:
                        slots(b)
                    silu_mid(b, 2, 1, (3, 4))
                if pre:
                    maxima(n * NPAIR, (0, 1, 2))
                    if post:
                        route(b)
                if post:
                    if not pre:
                        gated(b, 0)
                        gated(b, 1)

            def pairs(b, base, more):
                with dve.Fori(1, NPAIR - 1) as p:
                    ch.base, ch.n = base + (p - 1) * CHAIN_PAIR, 0
                    step(p, b, False, False, more)
                    assert ch.n == CHAIN_PAIR, ch.n
                ch.base, ch.n = base + (NPAIR - 2) * CHAIN_PAIR, 0
                step(NPAIR - 1, b, False, True, more)

            dve.wait_ge(const_ready, 3)
            h1_statistics(0)
            h1_normed(0)
            for k, (high, low, n, pe_st) in enumerate([(wq0h, wq0l, P, pe0_st), (wq1hh, wq1l, QR, pe1_st)]):
                for j, (src, lo, hi) in enumerate(((latent_ps(k), 0, KL), (pe_st, KL, P))):
                    dve.wait_ge(wqh_ready, 2 * k + j + 1)
                    dve.scalar_tensor_tensor(out=heads(low, lo, hi), in0=src[0:n], scalar=qg_sb[0:n, k:k + 1],
                                             in1=heads(high, lo, hi)[0:n].bitcast(F32),
                                             op0=ALU.mult, op1=ALU.subtract).then_inc(wql_ready, 1)
            dve.wait_ge(wk_in, 4 * 16)
            middle(0, 0, False, True)
            step(0, 0, True, False, False)
            assert ch.n == CHAIN_PROLOGUE, ch.n
            with dve.Fori(0, LAST) as b:
                pairs(b, CHAIN_PROLOGUE + b * CHAIN_BATCH, True)
                middle(b, b + 1, True, True)
                step(0, b + 1, True, False, True)
                assert (NPAIR - 2) * CHAIN_PAIR + ch.n == CHAIN_BATCH, (NPAIR - 2) * CHAIN_PAIR + ch.n
            pairs(LAST, CHAIN_PROLOGUE + LAST * CHAIN_BATCH, False)
            middle(LAST, None, True, False)

            dve.wait_ge(tab_landed, 16)
            ch.link(dve.tensor_copy(toku[:], tab[:, :, 0]))
            ch.step(dve.tensor_scalar(bidf[:], tab[:, :, 0], float(T - 1), None, ALU.min))
            ch.step(dve.tensor_copy(bidi[:], bidf[:]))
            dve.tensor_scalar(bid[:], bidi[:], 9, None, ALU.arith_shift_right).then_inc(tok_ready, 1)

            def weigh(e):
                q, r = e % 2, e % NT
                dve.wait_ge(ey_ps, e + 1)
                dve.wait_ge(gb_landed[r], 16 * (e // NT + 1))
                if e >= NT:
                    dve.wait_ge(added, 16 * (e - NT + 1))
                dve.scalar_tensor_tensor(out=ey[r], in0=PS[:, 6 + q, 0:H], scalar=tab[:, e, 1:2],
                                         in1=gbg[r], op0=ALU.mult, op1=ALU.mult).then_inc(ey_ready, 1)

            for e in range(NE):
                q = e % 2
                dve.wait_ge(eth_ready, e + 1)
                if e >= 2:
                    dve.wait_ge(emT_ps, e - 1)
                ch.step(dve.scalar_tensor_tensor(out=eth[:], in0=eth[:], scalar=1.0, in1=PS[:, 2 + q, 0:IM],
                                                 op0=ALU.add, op1=ALU.mult))
                dve.tensor_tensor(emid[:, q, :], eth[:], PS[:, 2 + q, IM:2 * IM], ALU.mult).then_inc(emid_ready, 1)
                if e >= 2:
                    weigh(e - 2)
            weigh(NE - 2)
            weigh(NE - 1)


def _rope_tables():
    inv = (np.float32(1.0) / np.float32(10000.0) ** (np.arange(0, DR, 2, dtype=np.float32) / np.float32(DR))).astype(np.float32)
    ang = np.arange(S, dtype=np.float32)[:, None] * inv
    c, s = np.cos(ang).astype(np.float32), np.sin(ang).astype(np.float32)
    return np.concatenate([c, c], -1), np.concatenate([-s, s], -1)


def kernel(**inputs):
    import concourse.bacc as bacc
    from concourse.bass_utils import run_bass_kernel_spmd

    a = {k: np.asarray(v) for k, v in inputs.items()}
    wqb = a["L0_attn_w_qb"].reshape(QL, NH, DN + DR)
    wkvb = a["L0_attn_w_kvb"].reshape(KL, NH, DN + DV)
    cos, sin = _rope_tables()
    arrays = {
        "x": a["L0_attn_hidden"],
        "wkva": a["L0_attn_w_kv_a"],
        "wqnT": wqb[:, :, :DN].transpose(1, 2, 0),
        "wqpe": wqb[:, :, DN:],
        "wkT": wkvb[:, :, :DN].transpose(2, 1, 0),
        "wvT": wkvb[:, :, DN:].transpose(2, 1, 0),
        "wo": a["L0_attn_w_o"],
        "qgam": a["L0_attn_q_a_gamma"],
        "kgam": a["L0_attn_kv_a_gamma"],
        "sgate": np.concatenate([a["L0_ffn_sw_gate"], a["L0_ffn_gate_w"].T], axis=1),
        "sup": a["L0_ffn_sw_up"],
        "sdown": a["L0_ffn_sw_down"],
        "egate": a["L0_ffn_w_gate"],
        "eup": a["L0_ffn_w_up"],
        "edown": a["L0_ffn_w_down"],
        "cT": a["L0_c"].T,
        "wmod": a["L0_wmod"],
        "cos": cos,
        "sin": sin,
    }
    nc = bacc.Bacc("TRN2", target_bir_lowering=False, num_devices=1)
    feed, args = {}, []
    for name, v in arrays.items():
        v = np.ascontiguousarray(v)
        feed[f"in_{name}"] = v
        args.append(nc.dram_tensor(f"in_{name}", v.shape, mybir.dt.from_np(v.dtype), kind="ExternalInput").ap())
    out = nc.dram_tensor("out_0", (B, S, H), F32, kind="ExternalOutput").ap()
    adaln_block(nc, *args, out)
    r = run_bass_kernel_spmd(nc, [feed], core_ids=[0])
    return r.results[0]["out_0"]
```
